# Optimizing a Trainium2 kernel written in Bass

```python
import numpy as np
import jax
import jax.numpy as jnp

def _softmax(x, axis=-1):
    return jax.nn.softmax(x, axis=axis)

def _gelu(x):
    return jax.nn.gelu(x, approximate=True)

def _silu(x):
    return jax.nn.silu(x)

def _sigmoid(x):
    return jax.nn.sigmoid(x)

def _layernorm(x, axis=-1, eps=1e-05):
    m = jnp.mean(x, axis=axis, keepdims=True)
    v = jnp.var(x, axis=axis, keepdims=True)
    return (x - m) / jnp.sqrt(v + eps)

def _scatter_add(tgt, idx, src, axis=0):
    return tgt.at[idx].add(src)

def _segment_sum(src, seg, n):
    return jax.ops.segment_sum(src, seg, n)
kernel_name = 'mk_perceiver_d1_seqx_r8_bb6c4f'

def setup_inputs(seed: int=0):
    np.random.seed(seed)
    _w = jnp.asarray

    def _rec_inputs():
        import jax
        import jax.numpy as jnp
        _rk = jax.random.key(seed)
        x = 7.22e-05 + 1 * jax.random.normal(jax.random.fold_in(_rk, 1), (64, 32, 128), jnp.float32)
        _lenS = 32 - jax.random.randint(jax.random.fold_in(_rk, 7), (64,), 0, max(1, 32 // 4) + 1, jnp.int32)
        _lenS2 = 257 - jax.random.randint(jax.random.fold_in(_rk, 8), (64,), 0, max(1, 257 // 4) + 1, jnp.int32)
        _ctx_1024P = jax.random.normal(jax.random.fold_in(_rk, 11), (64, 16, 128), jnp.float32)
        _ctx_1024c = jax.random.dirichlet(jax.random.fold_in(_rk, 511), 0.3 * jnp.ones((16,), jnp.float32), (64, 257))
        _ctx_1024t = jnp.einsum('bsk,bkd->bsd', _ctx_1024c, _ctx_1024P)
        _ctx_1024t = _ctx_1024t * jax.lax.rsqrt(jnp.mean(jnp.square(_ctx_1024t)) + 1e-12) * 0.953939
        ctx_1024 = 4.13588e-05 + 0.999923 * (_ctx_1024t + 0.3 * jax.random.normal(jax.random.fold_in(_rk, 611), (64, 257, 128), jnp.float32))
        return (x, ctx_1024)
    x, ctx_1024 = _rec_inputs()

    def _L0_xattn_setup():
        import jax, jax.numpy as jnp
        import numpy as np
        B, S, D, DFF = (4, 256, 128, 512)
        EPS = 1e-05

        def layernorm(x, gamma, beta):
            mu = jnp.mean(x, axis=-1, keepdims=True)
            var = jnp.var(x, axis=-1, keepdims=True)
            return (x - mu) * jax.lax.rsqrt(var + EPS) * gamma + beta

        def attention(Q, K, V, causal):
            d_k = Q.shape[-1]
            scores = jnp.einsum('bqd,bkd->bqk', Q, K) / jnp.sqrt(jnp.asarray(d_k, Q.dtype))
            if causal:
                q_len, k_len = (scores.shape[-2], scores.shape[-1])
                mask = jnp.tril(jnp.ones((q_len, k_len), dtype=bool))
                scores = jnp.where(mask[None], scores, jnp.asarray(-jnp.inf, scores.dtype))
            w = jax.nn.softmax(scores, axis=-1)
            return jnp.einsum('bqk,bkd->bqd', w, V)
        key = jax.random.key(seed)
        ks = jax.random.split(key, 12)
        sd = 0.02
        return {'y': jax.random.normal(ks[0], (B, S, D), jnp.float32), 'Z': jax.random.normal(ks[1], (B, S, D), jnp.float32), 'w1': jax.random.normal(ks[2], (D, DFF), jnp.float32) * sd, 'b1': jnp.zeros((DFF,), jnp.float32), 'w2': jax.random.normal(ks[3], (DFF, D), jnp.float32) * sd, 'b2': jnp.zeros((D,), jnp.float32), 'g1': jnp.ones((D,), jnp.float32), 'beta1': jnp.zeros((D,), jnp.float32), 'g2': jnp.ones((D,), jnp.float32), 'beta2': jnp.zeros((D,), jnp.float32), 'g3': jnp.ones((D,), jnp.float32), 'beta3': jnp.zeros((D,), jnp.float32)}
    _L0_xattn_all = _L0_xattn_setup()
    _L0_xattn_in = {k: v for k, v in _L0_xattn_all.items() if k in ('w1', 'b1', 'w2', 'b2', 'g1', 'beta1', 'g2', 'beta2', 'g3', 'beta3')}
    del _L0_xattn_all

    def _L0_attn_setup():
        import jax, jax.numpy as jnp
        import numpy as np
        L = 2
        D = 128
        H = 8
        DK = D // H
        DV = D // H
        T = 256
        B = 4
        INTER = 352
        EPS = 1e-06

        def rmsnorm(x, w):
            return x * jax.lax.rsqrt(jnp.mean(x * x, axis=-1, keepdims=True) + EPS) * w

        def l2norm(x):
            return x * jax.lax.rsqrt(jnp.sum(x * x, axis=-1, keepdims=True) + EPS)

        def delta_attn(x, Wq, Wk, Wv, Wb, Wo, onorm_w):
            b, t, _ = x.shape
            q = jax.nn.silu((x @ Wq).reshape(b, t, H, DK))
            k = jax.nn.silu((x @ Wk).reshape(b, t, H, DK))
            q = l2norm(q)
            k = l2norm(k)
            v = jax.nn.silu((x @ Wv).reshape(b, t, H, DV))
            beta = jax.nn.sigmoid(x @ Wb) * 2.0
            qt = q.transpose(1, 0, 2, 3)
            kt = k.transpose(1, 0, 2, 3)
            vt = v.transpose(1, 0, 2, 3)
            bt = beta.transpose(1, 0, 2)

            def step(S, inps):
                qi, ki, vi, bi = inps
                pred = jnp.einsum('bhkv,bhk->bhv', S, ki)
                S = S + bi[..., None, None] * ki[..., :, None] * (vi - pred)[..., None, :]
                o = jnp.einsum('bhkv,bhk->bhv', S, qi)
                return (S, o)
            S0 = jnp.zeros((b, H, DK, DV), x.dtype)
            _, o = jax.lax.scan(step, S0, (qt, kt, vt, bt))
            o = rmsnorm(o, onorm_w)
            o = o.transpose(1, 0, 2, 3).reshape(b, t, H * DV)
            return o @ Wo
        key = jax.random.key(seed)
        ks = jax.random.split(key, 13)
        s = 0.02
        f32 = jnp.float32
        return {'input_embeds': jax.random.normal(ks[0], (T, B, D), f32), 'Wq': jax.random.normal(ks[1], (L, D, D), f32) * s, 'Wk': jax.random.normal(ks[2], (L, D, D), f32) * s, 'Wv': jax.random.normal(ks[3], (L, D, D), f32) * s, 'Wb': jax.random.normal(ks[4], (L, D, H), f32) * s, 'Wo': jax.random.normal(ks[5], (L, D, D), f32) * s, 'onorm_w': jnp.ones((L, DV), f32) + jax.random.normal(ks[6], (L, DV), f32) * 0.02, 'norm1_w': jnp.ones((L, D), f32) + jax.random.normal(ks[7], (L, D), f32) * 0.02, 'norm2_w': jnp.ones((L, D), f32) + jax.random.normal(ks[8], (L, D), f32) * 0.02, 'Wg': jax.random.normal(ks[9], (L, D, 2 * INTER), f32) * s, 'Wd': jax.random.normal(ks[10], (L, INTER, D), f32) * s, 'final_norm_w': jnp.ones((D,), f32) + jax.random.normal(ks[11], (D,), f32) * 0.02}
    _L0_attn_all = _L0_attn_setup()
    _L0_attn_in = {k: v for k, v in _L0_attn_all.items() if k in ('Wq', 'Wk', 'Wv', 'Wb', 'Wo', 'onorm_w', 'norm1_w', 'norm2_w', 'Wg', 'Wd', 'final_norm_w')}
    del _L0_attn_all

    def _L0_ffn_setup():
        import jax, jax.numpy as jnp
        import numpy as np
        E = 32
        H = 128
        I = 64
        G = 8
        TKG = 4
        TOPK = 8
        NSH = 2
        SCALE = 2.5
        key = jax.random.key(seed)
        ks = jax.random.split(key, 10)
        s = 0.02
        return {'hidden_states': jax.random.normal(ks[0], (2, 128, H), jnp.float32), 'gate_w': jax.random.normal(ks[1], (E, H), jnp.float32) * s, 'gate_bias': jax.random.normal(ks[2], (E,), jnp.float32) * s, 'w_gate': jax.random.normal(ks[3], (E, I, H), jnp.float32) * s, 'w_up': jax.random.normal(ks[4], (E, I, H), jnp.float32) * s, 'w_down': jax.random.normal(ks[5], (E, H, I), jnp.float32) * s, 'sh_gate': jax.random.normal(ks[6], (I * NSH, H), jnp.float32) * s, 'sh_up': jax.random.normal(ks[7], (I * NSH, H), jnp.float32) * s, 'sh_down': jax.random.normal(ks[8], (H, I * NSH), jnp.float32) * s}
    _L0_ffn_all = _L0_ffn_setup()
    _L0_ffn_in = {k: v for k, v in _L0_ffn_all.items() if k in ('gate_w', 'gate_bias', 'w_gate', 'w_up', 'w_down', 'sh_gate', 'sh_up', 'sh_down')}
    del _L0_ffn_all
    return {'x': x, 'ctx_1024': ctx_1024, 'L0_xattn_w1': _L0_xattn_in['w1'], 'L0_xattn_b1': _L0_xattn_in['b1'], 'L0_xattn_w2': _L0_xattn_in['w2'], 'L0_xattn_b2': _L0_xattn_in['b2'], 'L0_xattn_g1': _L0_xattn_in['g1'], 'L0_xattn_beta1': _L0_xattn_in['beta1'], 'L0_xattn_g2': _L0_xattn_in['g2'], 'L0_xattn_beta2': _L0_xattn_in['beta2'], 'L0_xattn_g3': _L0_xattn_in['g3'], 'L0_xattn_beta3': _L0_xattn_in['beta3'], 'L0_attn_Wq': _L0_attn_in['Wq'], 'L0_attn_Wk': _L0_attn_in['Wk'], 'L0_attn_Wv': _L0_attn_in['Wv'], 'L0_attn_Wb': _L0_attn_in['Wb'], 'L0_attn_Wo': _L0_attn_in['Wo'], 'L0_attn_onorm_w': _L0_attn_in['onorm_w'], 'L0_attn_norm1_w': _L0_attn_in['norm1_w'], 'L0_attn_norm2_w': _L0_attn_in['norm2_w'], 'L0_attn_Wg': _L0_attn_in['Wg'], 'L0_attn_Wd': _L0_attn_in['Wd'], 'L0_attn_final_norm_w': _L0_attn_in['final_norm_w'], 'L0_ffn_gate_w': _L0_ffn_in['gate_w'], 'L0_ffn_gate_bias': _L0_ffn_in['gate_bias'], 'L0_ffn_w_gate': _L0_ffn_in['w_gate'], 'L0_ffn_w_up': _L0_ffn_in['w_up'], 'L0_ffn_w_down': _L0_ffn_in['w_down'], 'L0_ffn_sh_gate': _L0_ffn_in['sh_gate'], 'L0_ffn_sh_up': _L0_ffn_in['sh_up'], 'L0_ffn_sh_down': _L0_ffn_in['sh_down']}

def reference(x, ctx_1024, L0_xattn_w1, L0_xattn_b1, L0_xattn_w2, L0_xattn_b2, L0_xattn_g1, L0_xattn_beta1, L0_xattn_g2, L0_xattn_beta2, L0_xattn_g3, L0_xattn_beta3, L0_attn_Wq, L0_attn_Wk, L0_attn_Wv, L0_attn_Wb, L0_attn_Wo, L0_attn_onorm_w, L0_attn_norm1_w, L0_attn_norm2_w, L0_attn_Wg, L0_attn_Wd, L0_attn_final_norm_w, L0_ffn_gate_w, L0_ffn_gate_bias, L0_ffn_w_gate, L0_ffn_w_up, L0_ffn_w_down, L0_ffn_sh_gate, L0_ffn_sh_up, L0_ffn_sh_down):
    import jax
    import jax.numpy as jnp

    def _L0_xattn_ref(y, Z, w1, b1, w2, b2, g1, beta1, g2, beta2, g3, beta3):
        import jax, jax.numpy as jnp
        import numpy as np
        B, S, D, DFF = (4, 256, 128, 512)
        EPS = 1e-05

        def layernorm(x, gamma, beta):
            mu = jnp.mean(x, axis=-1, keepdims=True)
            var = jnp.var(x, axis=-1, keepdims=True)
            return (x - mu) * jax.lax.rsqrt(var + EPS) * gamma + beta

        def attention(Q, K, V, causal):
            d_k = Q.shape[-1]
            scores = jnp.einsum('bqd,bkd->bqk', Q, K) / jnp.sqrt(jnp.asarray(d_k, Q.dtype))
            if causal:
                q_len, k_len = (scores.shape[-2], scores.shape[-1])
                mask = jnp.tril(jnp.ones((q_len, k_len), dtype=bool))
                scores = jnp.where(mask[None], scores, jnp.asarray(-jnp.inf, scores.dtype))
            w = jax.nn.softmax(scores, axis=-1)
            return jnp.einsum('bqk,bkd->bqd', w, V)
        sa = attention(y, y, y, causal=True)
        y = layernorm(y + sa, g1, beta1)
        ca = attention(y, Z, Z, causal=False)
        y = layernorm(y + ca, g2, beta2)
        h = jax.nn.relu(jnp.einsum('bsd,df->bsf', y, w1) + b1)
        ff = jnp.einsum('bsf,fd->bsd', h, w2) + b2
        y = layernorm(y + ff, g3, beta3)
        return y

    def _L0_attn_ref(input_embeds, Wq, Wk, Wv, Wb, Wo, onorm_w, norm1_w, norm2_w, Wg, Wd, final_norm_w):
        import jax, jax.numpy as jnp
        import numpy as np
        L = 2
        D = 128
        H = 8
        DK = D // H
        DV = D // H
        T = 256
        B = 4
        INTER = 352
        EPS = 1e-06

        def rmsnorm(x, w):
            return x * jax.lax.rsqrt(jnp.mean(x * x, axis=-1, keepdims=True) + EPS) * w

        def l2norm(x):
            return x * jax.lax.rsqrt(jnp.sum(x * x, axis=-1, keepdims=True) + EPS)

        def delta_attn(x, Wq, Wk, Wv, Wb, Wo, onorm_w):
            b, t, _ = x.shape
            q = jax.nn.silu((x @ Wq).reshape(b, t, H, DK))
            k = jax.nn.silu((x @ Wk).reshape(b, t, H, DK))
            q = l2norm(q)
            k = l2norm(k)
            v = jax.nn.silu((x @ Wv).reshape(b, t, H, DV))
            beta = jax.nn.sigmoid(x @ Wb) * 2.0
            qt = q.transpose(1, 0, 2, 3)
            kt = k.transpose(1, 0, 2, 3)
            vt = v.transpose(1, 0, 2, 3)
            bt = beta.transpose(1, 0, 2)

            def step(S, inps):
                qi, ki, vi, bi = inps
                pred = jnp.einsum('bhkv,bhk->bhv', S, ki)
                S = S + bi[..., None, None] * ki[..., :, None] * (vi - pred)[..., None, :]
                o = jnp.einsum('bhkv,bhk->bhv', S, qi)
                return (S, o)
            S0 = jnp.zeros((b, H, DK, DV), x.dtype)
            _, o = jax.lax.scan(step, S0, (qt, kt, vt, bt))
            o = rmsnorm(o, onorm_w)
            o = o.transpose(1, 0, 2, 3).reshape(b, t, H * DV)
            return o @ Wo
        x = input_embeds.transpose(1, 0, 2)
        for l in range(L):
            h = rmsnorm(x, norm1_w[l])
            x = x + delta_attn(h, Wq[l], Wk[l], Wv[l], Wb[l], Wo[l], onorm_w[l])
            h = rmsnorm(x, norm2_w[l])
            gy = h @ Wg[l]
            g, y = jnp.split(gy, 2, axis=-1)
            x = x + jax.nn.silu(g) * y @ Wd[l]
        x = rmsnorm(x, final_norm_w)
        return x.transpose(1, 0, 2)

    def _L0_ffn_ref(hidden_states, gate_w, gate_bias, w_gate, w_up, w_down, sh_gate, sh_up, sh_down):
        import jax, jax.numpy as jnp
        import numpy as np
        E = 32
        H = 128
        I = 64
        G = 8
        TKG = 4
        TOPK = 8
        NSH = 2
        SCALE = 2.5
        B, S, Hd = hidden_states.shape
        h = hidden_states.reshape(-1, Hd)
        logits = h.astype(jnp.float32) @ gate_w.T
        scores = jax.nn.sigmoid(logits)
        sc = scores + gate_bias
        grp = sc.reshape(-1, G, E // G)
        group_scores = jax.lax.top_k(grp, 2)[0].sum(-1)
        gidx = jax.lax.top_k(group_scores, TKG)[1]
        gmask = jnp.sum(jax.nn.one_hot(gidx, G, dtype=sc.dtype), axis=1)
        smask = jnp.repeat(gmask, E // G, axis=1)
        masked = jnp.where(smask > 0, sc, jnp.zeros_like(sc))
        tki = jax.lax.top_k(masked, TOPK)[1]
        tkw = jnp.take_along_axis(scores, tki, axis=1)
        tkw = tkw / (tkw.sum(-1, keepdims=True) + 1e-20)
        tkw = tkw * SCALE
        combine = (jax.nn.one_hot(tki, E, dtype=tkw.dtype) * tkw[..., None]).sum(1)
        g = jax.nn.silu(jnp.einsum('th,eih->tei', h, w_gate))
        u = jnp.einsum('th,eih->tei', h, w_up)
        routed = jnp.einsum('tei,ehi->th', g * u * combine[:, :, None], w_down)
        sg = jax.nn.silu(h @ sh_gate.T)
        shared = sg * (h @ sh_up.T) @ sh_down.T
        return (routed + shared).reshape(B, S, Hd)
    x = x + _L0_xattn_ref(_layernorm(x, axis=-1), ctx_1024, L0_xattn_w1, L0_xattn_b1, L0_xattn_w2, L0_xattn_b2, L0_xattn_g1, L0_xattn_beta1, L0_xattn_g2, L0_xattn_beta2, L0_xattn_g3, L0_xattn_beta3)
    x = x + _L0_attn_ref(_layernorm(x, axis=-1), L0_attn_Wq, L0_attn_Wk, L0_attn_Wv, L0_attn_Wb, L0_attn_Wo, L0_attn_onorm_w, L0_attn_norm1_w, L0_attn_norm2_w, L0_attn_Wg, L0_attn_Wd, L0_attn_final_norm_w)
    x = x + _L0_ffn_ref(_layernorm(x, axis=-1), L0_ffn_gate_w, L0_ffn_gate_bias, L0_ffn_w_gate, L0_ffn_w_up, L0_ffn_w_down, L0_ffn_sh_gate, L0_ffn_sh_up, L0_ffn_sh_down)
    return x

_drawn_inputs = setup_inputs


def setup_inputs(seed=0):
    import zlib

    import numpy as np

    out = dict(_drawn_inputs(seed))
    spreads = {'L0_xattn_b1': (0.0, 0.551),
     'L0_xattn_b2': (0.0, 0.1),
     'L0_xattn_g1': (1.0, 0.2),
     'L0_xattn_beta1': (0.0, 0.1),
     'L0_xattn_g2': (1.0, 0.2),
     'L0_xattn_beta2': (0.0, 0.1),
     'L0_xattn_g3': (1.0, 0.2),
     'L0_xattn_beta3': (0.0, 0.1)}
    factors = {'L0_attn_Wb': 4.085,
     'L0_attn_onorm_w': 8.0,
     'L0_attn_norm1_w': 8.0,
     'L0_attn_norm2_w': 8.0,
     'L0_attn_Wg': 8.0,
     'L0_attn_Wd': 8.0,
     'L0_attn_final_norm_w': 7.932,
     'L0_ffn_gate_w': 8.0,
     'L0_ffn_gate_bias': 8.0,
     'L0_ffn_w_gate': 8.0,
     'L0_ffn_w_up': 8.0,
     'L0_ffn_w_down': 8.0,
     'L0_ffn_sh_gate': 8.0,
     'L0_ffn_sh_up': 8.0,
     'L0_ffn_sh_down': 8.0}
    for name, (base, spread) in spreads.items():
        noise = np.random.default_rng([zlib.crc32(name.encode()), seed]).standard_normal(out[name].shape)
        drawn = base * np.exp(spread * noise) if base else spread * noise
        out[name] = jnp.asarray(drawn.astype(out[name].dtype))
    for name, factor in factors.items():
        out[name] = (out[name] * factor).astype(out[name].dtype)
    return out
```

```python
from contextlib import ExitStack

import concourse.bass as bass
from concourse import mybir

F32 = mybir.dt.float32
BF16 = mybir.dt.bfloat16
ALU = mybir.AluOpType
ACT = mybir.ActivationFunctionType
AX = mybir.AxisListType

P = 128
D = 128
NJ = 16
GT = 4
GW = GT * D
NU = 2
IT = NJ // (GT * NU)
NA, S = 4, 32
KEYS = 257
FFC = 4
L = 2
H, DK = 8, 16
HH, H2 = 4, 2
T = 64
QKVB = 3 * D + H
INTER = 352
IC = [(0, 128), (128, 128), (256, 96)]
E = 32
EI = 64
NPAIR = E // 2
NGRP = 8
TOPG = 4
SCALE_ATT = float(D) ** -0.5
EPS_LN, EPS_RMS = 1e-5, 1e-6
NEG = -1e30
REPLACED = -3e38
ROUTE_SCALE = 2.5

G1, BE1, G2, BE2, G3, BE3, B2, FINALW = range(8)
C_N1, C_N2, C_ON, C_B1 = 0, L, 2 * L, 3 * L


class Steps:

    def __init__(self, eng, sem):
        self.eng, self.sem, self.n = eng, sem, 0

    def after(self, ins):
        ins.then_inc(self.sem, 1)
        self.n += 1
        self.eng.wait_ge(self.sem, self.n)

    def end(self):
        self.eng.sem_clear(self.sem)


def need(eng, sem, it, k, per=NU):
    eng.wait_ge(sem, it * per + (k + 1))


def perceiver(nc, x, ctx_t, ctx_z, ctx_last, rows, cols, w1, w2, wqkvb, wo, wgu, wd, gate_t, gate_bias,
              we_gate, we_up, we_down, sh_gate, sh_up, sh_down, ident_in, causal_in, spread_in, before_in, out):
    with ExitStack() as stack:
        def sb(name, shape, dt=F32):
            return stack.enter_context(nc.sbuf_tensor(name, shape, dt))

        def sem(name):
            return stack.enter_context(nc.semaphore(name))

        banks = [stack.enter_context(nc.psum_tensor(f"bank{i}", [P, 512], F32)) for i in range(8)]

        ident = sb("ident", [P, P])
        causal = sb("causal", [P, S])
        spread = sb("spread", [96, NPAIR * P], BF16)
        before = sb("before", [P, NGRP * NGRP])
        rowv = sb("rowv", [P, 8, D])
        colv = sb("colv", [P, 3 * L + FFC])
        gbias = sb("gbias", [P, E])
        w1_sb = sb("w1_sb", [P, FFC * P])
        w2_sb = sb("w2_sb", [P, FFC, D])
        wqkvb_sb = sb("wqkvb_sb", [P, L, QKVB])
        wo_sb = sb("wo_sb", [P, L, D])
        wgu_sb = sb("wgu_sb", [P, L, 2 * INTER])
        wd_sb = sb("wd_sb", [P, L, 3, D])
        gate_sb = sb("gate_sb", [P, E])
        weg_sb = sb("weg_sb", [P, NPAIR + 1, P])
        weu_sb = sb("weu_sb", [P, NPAIR + 1, P])
        wed_sb = sb("wed_sb", [P, NPAIR + 1, D])
        neg_half, eps_ln, eps_rms = sb("neg_half", [P, 64]), sb("eps_ln", [P, 64]), sb("eps_rms", [P, 64])

        X = sb("X", [P, NJ * D])
        R = sb("R", [P, NJ * D])
        zlast = sb("zlast", [P, NJ * D])
        NRING = 8
        arena = sb("arena", [P, NRING * (NA * KEYS + 2 * NA * D)])
        zt_ring = arena[:, 0:NRING * NA * KEYS].rearrange("p (n c) -> p n c", n=NRING)
        z_ring = arena[:, NRING * NA * KEYS:].rearrange("p (n c) -> p n c", n=NRING)
        PKW = H * 4 * DK
        PK = arena[:, 0:NJ * PKW].rearrange("p (n c) -> p n c", n=NJ)
        PS = arena[:, NJ * PKW:NJ * PKW + T * D].rearrange("p (t c) -> p t c", t=T)
        Os = sb("Os", [P, T * 32])
        O = zlast

        yr = [sb(f"yr{u}", [P, 2 * GT, D]) for u in range(NU)]
        y = [yr[u][:, 0:GT, :] for u in range(NU)]
        yn = [sb(f"yn{u}", [P, GT, D]) for u in range(NU)]
        r = [yr[u][:, GT:2 * GT, :] for u in range(NU)]
        yT = [sb(f"yT{u}", [P, GW]) for u in range(NU)]
        hT = [sb(f"hT{u}", [P, FFC, GW]) for u in range(NU)]
        stat = [sb(f"stat{u}", [P, GT, 6]) for u in range(NU)]
        mv = [sb(f"mv{u}", [P, GT, 2]) for u in range(NU)]
        ve = [sb(f"ve{u}", [P, 64]) for u in range(NU)]
        rstd = [sb(f"rstd{u}", [P, 64]) for u in range(NU)]
        ss = [sb(f"ss{u}", [P, GT]) for u in range(NU)]
        ssh = [sb(f"ssh{u}", [P, 64]) for u in range(NU)]
        rstdh = [sb(f"rstdh{u}", [P, 64]) for u in range(NU)]
        s1 = [sb(f"s1{u}", [P, GT, S]) for u in range(NU)]
        p1 = [sb(f"p1{u}", [P, GT, S]) for u in range(NU)]
        p1T = [sb(f"p1T{u}", [P, GT, S]) for u in range(NU)]
        mx = [sb(f"mx{u}", [P, GT]) for u in range(NU)]
        rs1 = [sb(f"rs1{u}", [P, GT]) for u in range(NU)]
        ri1 = [sb(f"ri1{u}", [P, GT]) for u in range(NU)]
        NT = NU * GT
        nmax = sb("nmax", [P, NT])
        rsum = sb("rsum", [P, NT])
        rinv = sb("rinv", [P, NT])
        pc = sb("pc", [P, NT, KEYS])
        pcT = sb("pcT", [P, NT, 2 * P])
        qkv = [pc[:, 0:6, :].rearrange("p n c -> p (n c)")[:, 0:GT * 3 * D].rearrange("p (j c) -> p j c", j=GT),
               pcT[:, 0:6, :].rearrange("p n c -> p (n c)").rearrange("p (j c) -> p j c", j=GT)]
        sq = [yr[u][:, :, :].rearrange("p (j i) c -> p j (i c)", j=GT) for u in range(NU)]
        th = [sb(f"th{u}", [P, GT, H]) for u in range(NU)]
        beta = [sb(f"beta{u}", [P, GT, H]) for u in range(NU)]
        NS = 4
        def carve(flat):
            at = [0]

            def take(shape, parts=P, dt=F32):
                n = 1
                for d in shape:
                    n *= d
                words = n if dt is F32 else n // 2
                piece = flat[0:parts, at[0]:at[0] + words]
                at[0] += words
                if dt is not F32:
                    piece = piece.bitcast(dt)
                if len(shape) == 1:
                    return piece
                names = "abc"[:len(shape)]
                return piece.rearrange(f"p ({' '.join(names)}) -> p {' '.join(names)}",
                                       **{k: v for k, v in zip(names, shape)})
            return take

        take = carve(hT[0][:, :, :].rearrange("p c n -> p (c n)"))
        St = [take((H2, DK, DK)) for i in range(NS)]
        take = carve(hT[1][:, :, :].rearrange("p c n -> p (c n)"))
        prod, outer, oprod = take((H2, DK, DK)), take((H2, DK, DK)), take((H2, DK, DK))
        osum8, osum4, osum2 = take((H2, DK, 8)), take((H2, DK, 4)), take((H2, DK, 2))
        pred, upd = take((H2, DK)), take((H2, DK))
        take = carve(pc[:, :, :].rearrange("p n c -> p (n c)"))
        sg = [take((GT, E)) for u in range(NU)]
        sc = [take((GT, E)) for u in range(NU)]
        msk = [take((GT, E)) for u in range(NU)]
        rep = [take((GT, E)) for u in range(NU)]
        comb = [take((GT, E)) for u in range(NU)]
        gs = [take((4, GT * NGRP)) for u in range(NU)]
        gmask = [take((GT * NGRP,)) for u in range(NU)]
        pmx = [take((GT * NGRP, 2)) for u in range(NU)]
        pmn = [take((GT * NGRP, 2)) for u in range(NU)]
        top8 = [take((GT, 8)) for u in range(NU)]
        den = [take((GT,)) for u in range(NU)]
        take = carve(pcT[:, :, :].rearrange("p n c -> p (n c)"))
        cmp1 = [take((GT * NGRP, NGRP)) for u in range(NU)]
        cmp2 = [take((GT * NGRP, NGRP)) for u in range(NU)]
        take = carve(arena[:, :])
        cf = [take((GW,), E) for u in range(NU)]
        c3 = [take((GW,), 3 * E, BF16) for u in range(NU)]
        cmid = [take((GW,), E, BF16) for u in range(NU)]
        act_g = [sb(f"act_g{u}", [P, GW]) for u in range(NU)]
        scrap = [sb(f"scrap{u}", [P, 1]) for u in range(NU)]
        scrap2 = [sb(f"scrap2{u}", [P, 1]) for u in range(NU)]
        act_gu = [hT[u][:, 0, :] for u in range(NU)]
        act_a = [hT[u][:, 1, :] for u in range(NU)]

        x_in, const_in, zlast_in, w_in = sem("x_in"), sem("const_in"), sem("zlast_in"), sem("w_in")
        ring_in = [sem(f"ring_in{i}") for i in range(NRING)]
        consts_made = sem("consts_made")
        dve_steps = [sem(f"dve_steps{i}") for i in range(2 * L + 3)]
        pool_steps = [sem(f"pool_steps{i}") for i in range(2 * L + 3)]
        a_var, a_rstd, a_norm, a_scaled = sem("a_var"), sem("a_rstd"), sem("a_norm"), sem("a_scaled")
        a_y, a_tr, a_yT = sem("a_y"), sem("a_tr"), sem("a_yT")
        sa_scores, sa_shift, sa_exp, sa_pT, sa_out = (sem("sa_scores"), sem("sa_shift"), sem("sa_exp"),
                                                      sem("sa_pT"), sem("sa_out"))
        ca_scores, ca_max, ca_exp, ca_tr, ca_pT, ca_out = (sem("ca_scores"), sem("ca_max"), sem("ca_exp"),
                                                           sem("ca_tr"), sem("ca_pT"), sem("ca_out"))
        ff_up, ff_h, ff_out, ff_res = sem("ff_up"), sem("ff_h"), sem("ff_out"), sem("ff_res")
        def lsem(name):
            return [sem(f"{name}_{l}") for l in range(L)]
        d_var, d_rstd = sem("d_var"), sem("d_rstd")
        q_r, q_ss, q_rr, q_h, q_tr, q_hT, q_proj, q_silu, q_n2, q_rn, q_k, q_qk, q_pk = map(lsem, (
            "q_r", "q_ss", "q_rr", "q_h", "q_tr", "q_hT", "q_proj", "q_silu", "q_n2", "q_rn", "q_k", "q_qk",
            "q_pk"))
        scan_in, st_ready, st_free, o_ready, o_home = map(lsem, ("scan_in", "st_ready", "st_free", "o_ready",
                                                                 "o_home"))
        o_n2, o_rn, o_n, o_tr, o_oT, o_wo, r1_ready, m_ss, m_rr, m_h, m_tr, m_hT, m_gu, m_silu, m_a, m_out = map(
            lsem, ("o_n2", "o_rn", "o_n", "o_tr", "o_oT", "o_wo", "r1_ready", "m_ss", "m_rr", "m_h", "m_tr",
                   "m_hT", "m_gu", "m_silu", "m_a", "m_out"))
        r2_ready, f_ss, f_rr, f_n, f_w = sem("r2_ready"), sem("f_ss"), sem("f_rr"), sem("f_n"), sem("f_w")
        e_var, e_rstd, e_h, e_tr, e_hT, e_log, e_sig, e_comb, e_ctr, e_c3, e_mid, e_cf = (
            sem("e_var"), sem("e_rstd"), sem("e_h"), sem("e_tr"), sem("e_hT"), sem("e_log"), sem("e_sig"),
            sem("e_comb"), sem("e_ctr"), sem("e_c3"), sem("e_mid"), sem("e_cf"))
        x_gate, x_silu, x_gu, x_a, x_down = sem("x_gate"), sem("x_silu"), sem("x_gu"), sem("x_a"), sem("x_down")
        e_acc, e_otr, e_xo = sem("e_acc"), sem("e_otr"), sem("e_xo")
        x_dve_steps, x_pool_steps = sem("x_dve_steps"), sem("x_pool_steps")
        out_done = [sem(f"out_done{u}") for u in range(NU)]

        consts = [(ident, ident_in), (causal, causal_in), (spread[:, :].bitcast(mybir.dt.uint16), spread_in), (before, before_in),
                  (colv, cols)]
        N_CONST = 16 * (len(consts) + 8 + 1)
        weights = [(w1_sb, w1), (w2_sb, w2), (wqkvb_sb, wqkvb), (wo_sb, wo), (wgu_sb, wgu), (wd_sb, wd),
                   (gate_sb, gate_t), (weg_sb, we_gate), (weu_sb, we_up), (wed_sb, we_down)]
        shared = [(weg_sb, sh_gate), (weu_sb, sh_up), (wed_sb, sh_down)]
        N_WEIGHT = 16 * (len(weights) + len(shared))

        def whole(t):
            if isinstance(t, bass.AP):
                return t
            return t[:, :] if len(t.shape) == 2 else t[:, :, :] if len(t.shape) == 3 else t[:, :, :, :]

        def tile_of(t, it, u, jj):
            return t[:, bass.ds(it * (NU * GW) + (u * GW + jj * D), D)]

        def group_of(t, it, u):
            return t[:, bass.ds(it * (NU * GW) + u * GW, GW)]

        def bc(ap, shape):
            return ap.to_broadcast(shape)

        block = stack.enter_context(nc.Block())

        @block.sync
        def _(sp):
            sp.dma_start(X[:, :], x).then_inc(x_in, 16)
            for dst, src in consts:
                sp.dma_start(whole(dst), src).then_inc(const_in, 16)
            for i in range(8):
                sp.dma_start(rowv[:, i, :], rows[i:i + 1, :].partition_broadcast(P)).then_inc(const_in, 16)
            sp.dma_start(gbias[:, :], gate_bias.partition_broadcast(P)).then_inc(const_in, 16)

            def load_ctx(half):
                for n in range(NRING):
                    if half > 0:
                        sp.wait_ge(ca_out, (half - 1) * NT + n + 1)
                    sp.dma_start(zt_ring[:, n, :], ctx_t[half * NRING + n]).then_inc(ring_in[n], 16)
                    sp.dma_start(z_ring[:, n, :], ctx_z[half * NRING + n]).then_inc(ring_in[n], 16)

            load_ctx(0)
            for a in range(NA):
                sp.dma_start(zlast[S * a:S * a + S, :],
                             ctx_last[a:a + 1, :].partition_broadcast(S)).then_inc(zlast_in, 16)
            for dst, src in weights:
                d = dst[:, 0:NPAIR, :] if dst is weg_sb or dst is weu_sb or dst is wed_sb else whole(dst)
                sp.dma_start(d, src).then_inc(w_in, 16)
            for dst, src in shared:
                sp.dma_start(dst[:, NPAIR, :], src).then_inc(w_in, 16)
            load_ctx(1)

            for l in range(L):
                sp.wait_ge(q_pk[l], IT * NU)
                sp.wait_ge(q_qk[l], IT * NU)
                for a in range(NA):
                    for hh in range(HH):
                        sp.dma_start(PS[S * hh:S * hh + S, NJ * a:NJ * a + NJ, :],
                                     PK[S * a:S * a + S, :, D * hh:D * hh + D]).then_inc(scan_in[l], 16)
                for a in range(NA):
                    sp.wait_ge(o_ready[l], NJ * (a + 1))
                    for hh in range(HH):
                        sp.dma_start(O[S * a:S * a + S, :].rearrange("p (j c) -> p j c", j=NJ)[:, :, 32 * hh:32 * hh + 32],
                                     Os[S * hh:S * hh + S, 32 * NJ * a:32 * NJ * (a + 1)]
                                     .rearrange("p (j c) -> p j c", j=NJ)).then_inc(o_home[l], 16)

            with sp.Fori(0, IT) as it:
                for u in range(NU):
                    need(sp, e_xo, it, u)
                    sp.dma_start(out[:, bass.ds(it * (NU * GW) + u * GW, GW)],
                                 r[u][:, :, :].rearrange("p j c -> p (j c)")).then_inc(out_done[u], 16)
            for u in range(NU):
                sp.wait_ge(out_done[u], 16 * (IT + 1))

        @block.tensor
        def _(pe):
            def transposes(bank, src, u, ready):
                for jj in range(GT):
                    last = pe.transpose(bank[:, jj * D:(jj + 1) * D], src[u][:, jj, :], ident[:, :])
                last.then_inc(ready, 1)

            pe.wait_ge(const_in, N_CONST)

            with pe.Fori(0, IT) as it:
                for u in range(NU):
                    need(pe, a_y, it, u)
                    transposes(banks[6 + u], y, u, a_tr)
                for u in range(NU):
                    need(pe, a_yT, it, u, per=3 * NU)
                    for jj in range(GT):
                        for a in range(NA):
                            q = yT[u][:, jj * D + a * S:jj * D + a * S + S]
                            last = pe.matmul(banks[6 + u][a * S:a * S + S, jj * S:jj * S + S], q, q,
                                             start=True, stop=True)
                    last.then_inc(sa_scores, 1)
                for u in range(NU):
                    pe.wait_ge(sa_pT, u + 1)
                    for jj in range(GT):
                        for a in range(NA):
                            rows_ = slice(a * S, a * S + S)
                            last = pe.matmul(banks[6 + u][rows_, jj * D:(jj + 1) * D], p1T[u][rows_, jj, :],
                                             y[u][rows_, jj, :], start=True, stop=True)
                    last.then_inc(sa_out, 1)
                pe.sem_clear(sa_pT)
                for u in range(NU):
                    need(pe, a_scaled, it, u, per=3 * NU)
                    transposes(banks[6 + u], y, u, a_tr)

                def scores(n):
                    u, jj = divmod(n, GT)
                    need(pe, a_yT, it, NU + u, per=3 * NU)
                    pe.wait_ge(ring_in[n], 32 * it + 32)
                    for a in range(NA):
                        last = pe.matmul(banks[n % 2][a * S:a * S + S, 0:KEYS],
                                         yT[u][:, jj * D + a * S:jj * D + a * S + S],
                                         zt_ring[:, n, a * KEYS:(a + 1) * KEYS], start=True, stop=True)
                    last.then_inc(ca_scores, 1)

                def turn(n):
                    need(pe, ca_exp, it, n, per=NT)
                    for c in range(2):
                        last = pe.transpose(banks[2 + n % 2][:, c * P:(c + 1) * P], pc[:, n, c * P:(c + 1) * P],
                                            ident[:, :])
                    last.then_inc(ca_tr, 1)

                def attend(n):
                    u, jj = divmod(n, GT)
                    need(pe, ca_pT, it, n, per=NT)
                    for a in range(NA):
                        for c in range(2):
                            last = pe.matmul(banks[4 + u][a * S:a * S + S, jj * D:(jj + 1) * D],
                                             pcT[:, n, c * P + a * S:c * P + a * S + S],
                                             z_ring[:, n, (c * NA + a) * D:(c * NA + a + 1) * D],
                                             start=(c == 0), stop=(c == 1))
                    last.then_inc(ca_out, 1)

                for n in range(NT + 2):
                    if n < NT:
                        scores(n)
                    if 1 <= n <= NT:
                        turn(n - 1)
                    if n >= 2:
                        attend(n - 2)
                for u in range(NU):
                    need(pe, a_scaled, it, NU + u, per=3 * NU)
                    transposes(banks[6 + u], y, u, a_tr)
                pe.wait_ge(w_in, N_WEIGHT)
                for u in range(NU):
                    need(pe, a_yT, it, 2 * NU + u, per=3 * NU)
                    for c in range(FFC):
                        if c >= 2:
                            need(pe, ff_h, it, u * FFC + c - 2, per=NU * FFC)
                        pe.matmul(banks[2 * u + c % 2][:, :], w1_sb[:, c * P:(c + 1) * P], yT[u][:, :],
                                  start=True, stop=True).then_inc(ff_up, 1)
                for u in range(NU):
                    need(pe, ff_h, it, u * FFC + FFC - 1, per=NU * FFC)
                    for jj in range(GT):
                        for c in range(FFC):
                            last = pe.matmul(banks[4 + u][:, jj * D:(jj + 1) * D], hT[u][:, c, jj * D:(jj + 1) * D],
                                             w2_sb[:, c, :], start=(c == 0), stop=(c == FFC - 1))
                    last.then_inc(ff_out, 1)

            for l in range(L):
                with pe.Fori(0, IT) as it:
                    for u in range(NU):
                        need(pe, q_h[l], it, u)
                        transposes(banks[4 * u], yn, u, q_tr[l])
                    for u in range(NU):
                        need(pe, q_hT[l], it, u)
                        for jj in range(GT):
                            pe.matmul(banks[4 * u + jj][:, 0:QKVB], yT[u][:, jj * D:(jj + 1) * D],
                                      wqkvb_sb[:, l, :], start=True, stop=True).then_inc(q_proj[l], 1)

                with pe.Fori(0, IT) as it:
                    for u in range(NU):
                        need(pe, o_n[l], it, u)
                        transposes(banks[4 * u], yn, u, o_tr[l])
                    for u in range(NU):
                        need(pe, o_oT[l], it, u)
                        for jj in range(GT):
                            last = pe.matmul(banks[4 * u + 1][:, jj * D:(jj + 1) * D], yT[u][:, jj * D:(jj + 1) * D],
                                             wo_sb[:, l, :], start=True, stop=True)
                        last.then_inc(o_wo[l], 1)
                    for u in range(NU):
                        need(pe, m_h[l], it, u)
                        transposes(banks[4 * u], yn, u, m_tr[l])
                    for c, (f0, fn) in enumerate(IC):
                        for u in range(NU):
                            need(pe, m_hT[l], it, u)
                            if c == 2:
                                need(pe, m_a[l], it, u, per=3 * NU)
                            bg, by = ((1, 2), (3, 0), (1, 2))[c]
                            pe.matmul(banks[4 * u + bg][0:fn, :], wgu_sb[:, l, f0:f0 + fn], yT[u][:, :],
                                      start=True, stop=True)
                            pe.matmul(banks[4 * u + by][0:fn, :], wgu_sb[:, l, INTER + f0:INTER + f0 + fn],
                                      yT[u][:, :], start=True, stop=True).then_inc(m_gu[l], 1)
                    for u in range(NU):
                        need(pe, m_a[l], it, 2 * NU + u, per=3 * NU)
                        for jj in range(GT):
                            for c, (f0, fn) in enumerate(IC):
                                last = pe.matmul(banks[4 * u + 3][:, jj * D:(jj + 1) * D],
                                                 hT[u][0:fn, c, jj * D:(jj + 1) * D], wd_sb[0:fn, l, c, :],
                                                 start=(c == 0), stop=(c == 2))
                        last.then_inc(m_out[l], 1)

            with pe.Fori(0, IT) as it:
                for u in range(NU):
                    need(pe, e_h, it, u)
                    transposes(banks[4 * u], yn, u, e_tr)
                for u in range(NU):
                    need(pe, e_hT, it, u)
                    for jj in range(GT):
                        last = pe.matmul(banks[4 * u + 1][:, jj * E:(jj + 1) * E], yT[u][:, jj * D:(jj + 1) * D],
                                         gate_sb[:, :], start=True, stop=True)
                    last.then_inc(e_log, 1)

                def gate_up(p, u):
                    n = (p + 1) * NU + u
                    if n >= NU:
                        need(pe, x_a, it, n - NU, per=(NPAIR + 1) * NU)
                    w = p % (NPAIR + 1)
                    pe.matmul(banks[4 * u][:, :], weg_sb[:, w, :], yT[u][:, :], start=True, stop=True)
                    last = pe.matmul(banks[4 * u + 1][:, :], weu_sb[:, w, :], yT[u][:, :], start=True, stop=True)
                    if p >= 0:
                        last = pe.matmul(banks[4 * u + 2][:, :], spread[:, p * P:(p + 1) * P], c3[u][:, :],
                                         start=True, stop=True)
                    last.then_inc(x_gate, 1)

                def down(p, u):
                    n = (p + 1) * NU + u
                    need(pe, x_a, it, n, per=(NPAIR + 1) * NU)
                    pe.matmul(banks[4 * u + 3][:, :], wed_sb[:, p % (NPAIR + 1), :], act_a[u][:, :],
                              start=(p == -1), stop=(p == NPAIR - 1), skip_group_check=True).then_inc(x_down, 1)

                for u in range(NU):
                    need(pe, e_comb, it, u)
                    for jj in range(GT):
                        last = pe.transpose(banks[4 * u + 2][0:E, jj * D:(jj + 1) * D], comb[u][:, jj, :], ident[:, :])
                    last.then_inc(e_ctr, 1)
                order = [(p, u) for p in range(-1, NPAIR) for u in range(NU)]
                for n in range(len(order) + NU):
                    if n < len(order):
                        if n == NU or n == NU + 1:
                            need(pe, e_c3, it, n - NU)
                            need(pe, e_mid, it, n - NU)
                        gate_up(*order[n])
                    if n >= NU:
                        down(*order[n - NU])
                for u in range(NU):
                    need(pe, e_acc, it, u)
                    for jj in range(GT):
                        last = pe.transpose(banks[4 * u][:, jj * D:(jj + 1) * D], r[u][:, jj, :], ident[:, :])
                    last.then_inc(e_otr, 1)

        @block.scalar
        def _(act):
            def copy(out_, in_, scale=1.0):
                return act.activation(out_, in_, ACT.Copy, scale=scale)

            act.wait_ge(const_in, N_CONST)
            with act.Fori(0, IT) as it:
                for u in range(NU):
                    need(act, a_tr, it, u, per=3 * NU)
                    copy(yT[u][:, :], banks[6 + u][:, :]).then_inc(a_yT, 1)
                for u in range(NU):
                    need(act, sa_shift, it, u)
                    act.activation(p1[u][:, :, :], s1[u][:, :, :], ACT.Exp, scale=SCALE_ATT).then_inc(sa_exp, 1)
                for u in range(NU):
                    need(act, a_tr, it, NU + u, per=3 * NU)
                    copy(yT[u][:, :], banks[6 + u][:, :], SCALE_ATT).then_inc(a_yT, 1)
                for n in range(NT):
                    need(act, ca_max, it, n, per=NT)
                    act.activation(pc[:, n, :], banks[n % 2][:, 0:KEYS], ACT.Exp, bias=nmax[:, n:n + 1],
                                   accum_out=rsum[:, n:n + 1]).then_inc(ca_exp, 1)
                for u in range(NU):
                    need(act, a_tr, it, 2 * NU + u, per=3 * NU)
                    copy(yT[u][:, :], banks[6 + u][:, :]).then_inc(a_yT, 1)
                for u in range(NU):
                    for c in range(FFC):
                        need(act, ff_up, it, u * FFC + c, per=NU * FFC)
                        act.activation(hT[u][:, c, :], banks[2 * u + c % 2][:, :], ACT.Relu,
                                       bias=colv[:, C_B1 + c:C_B1 + c + 1]).then_inc(ff_h, 1)

            def squares(src, it, u, done, sem_in=None, k=0, per=NU):
                if sem_in is not None:
                    need(act, sem_in, it, k, per=per)
                    copy(scrap[u][:, 0:1], colv[:, 0:1])
                for jj in range(GT):
                    last = act.activation(act_g[u][:, jj * D:(jj + 1) * D], tile_of(src, it, u, jj), ACT.Square,
                                          scale=float(D) ** -0.5, accum_out=ss[u][:, jj:jj + 1])
                last.then_inc(done, 1)

            for l in range(L):
                if l > 0:
                    act.wait_ge(r2_ready, l * IT * NU)
                with act.Fori(0, IT) as it:
                    for u in range(NU):
                        if l == 0:
                            squares(R, it, u, q_ss[l], q_r[l], u, NU)
                        else:
                            squares(R, it, u, q_ss[l])
                    for u in range(NU):
                        need(act, q_tr[l], it, u)
                        act.activation(yT[u][:, :], banks[4 * u][:, :], ACT.Copy,
                                       scale=colv[:, C_N1 + l:C_N1 + l + 1]).then_inc(q_hT[l], 1)
                    for u in range(NU):
                        for jj in range(GT):
                            need(act, q_proj[l], it, u * GT + jj, per=NU * GT)
                            act.activation(qkv[u][:, jj, :], banks[4 * u + jj][:, 0:3 * D], ACT.Silu)
                            last = act.activation(th[u][:, jj, :], banks[4 * u + jj][:, 3 * D:QKVB], ACT.Tanh,
                                                  scale=0.5)
                        last.then_inc(q_silu[l], 1)

                with act.Fori(0, IT) as it:
                    for u in range(NU):
                        need(act, o_tr[l], it, u)
                        act.activation(yT[u][:, :], banks[4 * u][:, :], ACT.Copy,
                                       scale=colv[:, C_ON + l:C_ON + l + 1]).then_inc(o_oT[l], 1)
                    for u in range(NU):
                        squares(R, it, u, m_ss[l], r1_ready[l], u, NU)
                    for u in range(NU):
                        need(act, m_tr[l], it, u)
                        act.activation(yT[u][:, :], banks[4 * u][:, :], ACT.Copy,
                                       scale=colv[:, C_N2 + l:C_N2 + l + 1]).then_inc(m_hT[l], 1)
                    for c, (f0, fn) in enumerate(IC):
                        for u in range(NU):
                            need(act, m_gu[l], it, c * NU + u, per=3 * NU)
                            if c > 0:
                                need(act, m_a[l], it, (c - 1) * NU + u, per=3 * NU)
                            bg = (1, 3, 1)[c]
                            act.activation(act_g[u][0:fn, :], banks[4 * u + bg][0:fn, :],
                                           ACT.Silu).then_inc(m_silu[l], 1)
                    if l == L - 1:
                        for u in range(NU):
                            squares(R, it, u, f_ss, r2_ready, u + IT * NU * (L - 1), NU)

            for u in range(NU):
                copy(scrap2[u][:, 0:1], colv[:, 0:1]).then_inc(out_done[u], 16)
            with act.Fori(0, IT) as it:
                for u in range(NU):
                    need(act, e_tr, it, u)
                    copy(yT[u][:, :], banks[4 * u][:, :]).then_inc(e_hT, 1)
                for u in range(NU):
                    need(act, e_log, it, u)
                    act.activation(sg[u][:, :, :].rearrange("p j e -> p (j e)"), banks[4 * u + 1][:, 0:GT * E],
                                   ACT.Sigmoid).then_inc(e_sig, 1)
                for u in range(NU):
                    need(act, e_ctr, it, u)
                    copy(cf[u][:, :], banks[4 * u + 2][0:E, :]).then_inc(e_cf, 1)
                for u in range(NU):
                    need(act, e_c3, it, u)
                    copy(c3[u][E:2 * E, :], cmid[u][:, :]).then_inc(e_mid, 1)
                for p in range(-1, NPAIR):
                    for u in range(NU):
                        n = (p + 1) * NU + u
                        need(act, x_gate, it, n, per=(NPAIR + 1) * NU)
                        if p == 0:
                            need(act, x_a, it, n - NU, per=(NPAIR + 1) * NU)
                        if p > 0:
                            need(act, x_gu, it, n - 2 * NU, per=NPAIR * NU)
                        act.activation(act_g[u][:, :], banks[4 * u][:, :], ACT.Silu).then_inc(x_silu, 1)
                for u in range(NU):
                    need(act, x_down, it, NPAIR * NU + u, per=(NPAIR + 1) * NU)
                    need(act, out_done[u], it * 16, 15, per=1)
                    copy(r[u][:, :, :].rearrange("p j c -> p (j c)"), banks[4 * u + 3][:, :]).then_inc(e_acc, 1)

        @block.gpsimd
        def _(pool):
            pool.memset(neg_half[:, :], -0.5)
            pool.memset(eps_ln[:, :], EPS_LN)
            pool.memset(eps_rms[:, :], EPS_RMS).then_inc(consts_made, 1)
            pool.wait_ge(consts_made, 1)
            pool.wait_ge(const_in, N_CONST)

            def rsqrt(st, u, src, n, eps, done, dst=rstd):
                v = ve[u][:, 0:n]
                st.after(pool.tensor_tensor(v, src, eps[:, 0:n], ALU.add))
                pool.tensor_tensor(dst[u][:, 0:n], v, neg_half[:, 0:n], ALU.pow).then_inc(done, 1)

            def affine(u, g, b, st, done):
                g_ = bc(rowv[:, g:g + 1, :], [P, GT, D])
                b_ = bc(rowv[:, b:b + 1, :], [P, GT, D])
                st.after(pool.tensor_tensor(r[u][:, :, :], yn[u][:, :, :], g_, ALU.mult))
                pool.tensor_tensor(y[u][:, :, :], r[u][:, :, :], b_, ALU.add).then_inc(done, 1)

            with pool.Fori(0, IT) as it:
                st = Steps(pool, pool_steps[0])
                for k in range(4):
                    for u in range(NU):
                        need(pool, a_var, it, k * NU + u, per=4 * NU)
                        rsqrt(st, u, mv[u][:, :, 1], GT, eps_ln, a_rstd)
                    if k == 0:
                        continue
                    for u in range(NU):
                        need(pool, a_norm, it, (k - 1) * NU + u, per=3 * NU)
                        g, b = ((G1, BE1), (G2, BE2), (G3, BE3))[k - 1]
                        affine(u, g, b, st, a_scaled)
                        if k == 2:
                            need(pool, a_scaled, it, NU * (k - 1) + u, per=3 * NU)
                            pool.tensor_tensor(r[u][:, :, :], y[u][:, :, :],
                                               bc(rowv[:, B2:B2 + 1, :], [P, GT, D]), ALU.add).then_inc(ff_res, 1)
                st.end()

            for l in range(L):
                with pool.Fori(0, IT) as it:
                    st = Steps(pool, pool_steps[1 + 2 * l])
                    if l == 0:
                        for u in range(NU):
                            need(pool, d_var, it, u)
                            rsqrt(st, u, mv[u][:, :, 1], GT, eps_ln, d_rstd)
                    for u in range(NU):
                        need(pool, q_ss[l], it, u)
                        rsqrt(st, u, ss[u][:, 0:GT], GT, eps_rms, q_rr[l])
                    for u in range(NU):
                        need(pool, q_n2[l], it, u)
                        rsqrt(st, u, ssh[u][:, 0:GT * 2 * H], GT * 2 * H, eps_rms, q_rn[l], rstdh)
                        need(pool, q_qk[l], it, u)
                        pk = PK[:, bass.ds(it * (NU * GT) + u * GT, GT), :].rearrange(
                            "p j (h t e) -> p (j h) t e", h=H, t=4)
                        b_ = bc(beta[u][:, :, :].rearrange("p j h -> p (j h)").unsqueeze(2), [P, GT * H, DK])
                        st.after(pool.tensor_tensor(pk[:, :, 2, :], pk[:, :, 1, :], b_, ALU.mult))
                        v4 = qkv[u][:, :, 2 * D:3 * D].rearrange("p j (h e) -> p j h e", h=H)
                        b4 = bc(beta[u][:, :, :].unsqueeze(3), [P, GT, H, DK])
                        pk4 = PK[:, bass.ds(it * (NU * GT) + u * GT, GT), :].rearrange(
                            "p j (h t e) -> p j h t e", h=H, t=4)
                        pool.tensor_tensor(pk4[:, :, :, 3, :], v4, b4, ALU.mult).then_inc(q_pk[l], 1)
                    st.end()

                pool.wait_ge(scan_in[l], 16 * NA * HH)
                pool.memset(oprod[:, :, :, :], 0.0).then_inc(st_free[l], NS)
                with pool.Fori(0, T // NS) as it:
                    st = Steps(pool, pool_steps[2 + 2 * l])
                    for i in range(NS):
                        need(pool, st_ready[l], it, i + 1, per=NS)
                        q_t = PS[:, bass.ds(it * NS + i, 1), :].rearrange("p o (g t e) -> p (o g) t e", g=H2, t=4)[
                            :, :, 0:1, :]
                        pool.tensor_tensor(oprod[:, :, :, :], St[(i + 1) % NS][:, :, :, :],
                                           bc(q_t, [P, H2, DK, DK]), ALU.mult).then_inc(st_free[l], 1)
                        pool.wait_ge(st_free[l], it * NS + (NS + i + 1))
                        st.after(pool.tensor_tensor(osum8[:, :, :, :], oprod[:, :, :, 0:8], oprod[:, :, :, 8:16],
                                                    ALU.add))
                        st.after(pool.tensor_tensor(osum4[:, :, :, :], osum8[:, :, :, 0:4], osum8[:, :, :, 4:8],
                                                    ALU.add))
                        st.after(pool.tensor_tensor(osum2[:, :, :, :], osum4[:, :, :, 0:2], osum4[:, :, :, 2:4],
                                                    ALU.add))
                        o_t = Os[:, bass.ds(it * (NS * 32) + i * 32, 32)].rearrange("p (g v) -> p g v", g=H2)
                        pool.tensor_tensor(o_t, osum2[:, :, :, 0], osum2[:, :, :, 1], ALU.add).then_inc(o_ready[l], 1)
                    st.end()

                with pool.Fori(0, IT) as it:
                    st = Steps(pool, pool_steps[2 * L + 1 + l])
                    for u in range(NU):
                        need(pool, o_n2[l], it, u)
                        rsqrt(st, u, ssh[u][:, 0:GT * H], GT * H, eps_rms, o_rn[l], rstdh)
                    for u in range(NU):
                        need(pool, m_ss[l], it, u)
                        rsqrt(st, u, ss[u][:, 0:GT], GT, eps_rms, m_rr[l])
                    if l == L - 1:
                        for u in range(NU):
                            need(pool, f_ss, it, u)
                            rsqrt(st, u, ss[u][:, 0:GT], GT, eps_rms, f_rr)
                        for u in range(NU):
                            need(pool, f_n, it, u)
                            pool.tensor_tensor(y[u][:, :, :], yn[u][:, :, :],
                                               bc(rowv[:, FINALW:FINALW + 1, :], [P, GT, D]),
                                               ALU.mult).then_inc(f_w, 1)
                    st.end()

            with pool.Fori(0, IT) as it:
                st = Steps(pool, x_pool_steps)
                for u in range(NU):
                    need(pool, e_var, it, u)
                    rsqrt(st, u, mv[u][:, :, 1], GT, eps_ln, e_rstd)
                st.end()

        @block.vector
        def _(dve):
            def stats(st, src, u, done):
                for jj in range(GT):
                    last = dve.bn_stats(stat[u][:, jj, :], src(jj))
                st.after(last)
                for jj in range(GT):
                    last = dve.bn_aggr(mv[u][:, jj, :], stat[u][:, jj, :])
                last.then_inc(done, 1)

            def normed(src, dst, u):
                for jj in range(GT):
                    last = dve.tensor_scalar(dst(jj), src(jj), mv[u][:, jj, 0:1], rstd[u][:, jj:jj + 1],
                                             ALU.subtract, ALU.mult)
                return last

            def scaled(src, dst, u):
                for jj in range(GT):
                    last = dve.tensor_scalar(dst(jj), src(jj), rstd[u][:, jj:jj + 1], None, ALU.mult)
                return last

            dve.wait_ge(x_in, 16)
            dve.wait_ge(const_in, N_CONST)
            with dve.Fori(0, IT) as it:
                st = Steps(dve, dve_steps[0])
                X_ = [lambda jj, u=u: tile_of(X, it, u, jj) for u in range(NU)]
                y_ = [lambda jj, u=u: y[u][:, jj, :] for u in range(NU)]
                yn_ = [lambda jj, u=u: yn[u][:, jj, :] for u in range(NU)]
                r_ = [lambda jj, u=u: r[u][:, jj, :] for u in range(NU)]
                for u in range(NU):
                    stats(st, X_[u], u, a_var)
                for u in range(NU):
                    need(dve, a_rstd, it, u, per=4 * NU)
                    normed(X_[u], y_[u], u).then_inc(a_y, 1)
                for u in range(NU):
                    need(dve, sa_scores, it, u)
                    s_ps = banks[6 + u][:, 0:GT * S].rearrange("p (j k) -> p j k", j=GT)
                    st.after(dve.tensor_tensor(s1[u][:, :, :], s_ps, bc(causal[:, :].unsqueeze(1), [P, GT, S]), ALU.add))
                    st.after(dve.tensor_reduce(mx[u][:, :], s1[u][:, :, :], AX.X, ALU.max))
                    dve.tensor_tensor(s1[u][:, :, :], s1[u][:, :, :], bc(mx[u][:, :].unsqueeze(2), [P, GT, S]),
                                      ALU.subtract).then_inc(sa_shift, 1)
                for u in range(NU):
                    need(dve, sa_exp, it, u)
                    dve.transpose(p1T[u][:, :, :].rearrange("p j k -> p (j k)"),
                                  p1[u][:, :, :].rearrange("p j k -> p (j k)")).then_inc(sa_pT, 1)
                    st.after(dve.tensor_reduce(rs1[u][:, :], p1[u][:, :, :], AX.X, ALU.add))
                    st.after(dve.reciprocal(ri1[u][:, :], rs1[u][:, :]))
                for u in range(NU):
                    need(dve, sa_out, it, u)
                    for jj in range(GT):
                        last = dve.scalar_tensor_tensor(out=r[u][:, jj, :], in0=banks[6 + u][:, jj * D:(jj + 1) * D],
                                                        scalar=ri1[u][:, jj:jj + 1], in1=y[u][:, jj, :],
                                                        op0=ALU.mult, op1=ALU.add)
                    st.after(last)
                    stats(st, r_[u], u, a_var)
                for u in range(NU):
                    need(dve, a_rstd, it, NU + u, per=4 * NU)
                    normed(r_[u], yn_[u], u).then_inc(a_norm, 1)

                def row_max(n):
                    need(dve, ca_scores, it, n, per=NT)
                    dve.tensor_reduce(nmax[:, n:n + 1], banks[n % 2][:, 0:KEYS], AX.X, ALU.max,
                                      negate=True).then_inc(ca_max, 1)

                def keep_turned(n):
                    need(dve, ca_tr, it, n, per=NT)
                    dve.tensor_copy(pcT[:, n, :], banks[2 + n % 2][:, 0:2 * P]).then_inc(ca_pT, 1)

                def cross_residual(u):
                    st.after(dve.reciprocal(rinv[:, u * GT:(u + 1) * GT], rsum[:, u * GT:(u + 1) * GT]))
                    need(dve, ca_out, it, u * GT + GT - 1, per=NT)
                    need(dve, a_scaled, it, u, per=3 * NU)
                    for jj in range(GT):
                        n = u * GT + jj
                        last = dve.scalar_tensor_tensor(out=yn[u][:, jj, :], in0=tile_of(zlast, it, u, jj),
                                                        scalar=pc[:, n, KEYS - 1:KEYS],
                                                        in1=banks[4 + u][:, jj * D:(jj + 1) * D],
                                                        op0=ALU.mult, op1=ALU.add)
                    st.after(last)
                    for jj in range(GT):
                        n = u * GT + jj
                        last = dve.scalar_tensor_tensor(out=r[u][:, jj, :], in0=yn[u][:, jj, :],
                                                        scalar=rinv[:, n:n + 1], in1=y[u][:, jj, :],
                                                        op0=ALU.mult, op1=ALU.add)
                    st.after(last)
                    stats(st, r_[u], u, a_var)

                dve.wait_ge(zlast_in, 16 * NA)
                for n in range(NT + 1):
                    if n < NT:
                        row_max(n)
                    if n >= 1:
                        keep_turned(n - 1)
                    if n == GT + 1:
                        cross_residual(0)
                cross_residual(1)
                for u in range(NU):
                    need(dve, a_rstd, it, 2 * NU + u, per=4 * NU)
                    normed(r_[u], yn_[u], u).then_inc(a_norm, 1)
                for u in range(NU):
                    need(dve, ff_out, it, u)
                    need(dve, ff_res, it, u)
                    st.after(dve.tensor_tensor(yn[u][:, :, :], banks[4 + u][:, :].rearrange("p (j c) -> p j c", j=GT),
                                               r[u][:, :, :], ALU.add))
                    stats(st, yn_[u], u, a_var)
                for u in range(NU):
                    need(dve, a_rstd, it, 3 * NU + u, per=4 * NU)
                    normed(yn_[u], yn_[u], u).then_inc(a_norm, 1)
                for u in range(NU):
                    need(dve, a_scaled, it, 2 * NU + u, per=3 * NU)
                    st.after(dve.tensor_tensor(group_of(X, it, u), group_of(X, it, u),
                                               y[u][:, :, :].rearrange("p j c -> p (j c)"), ALU.add))
                st.end()

            for l in range(L):
                with dve.Fori(0, IT) as it:
                    R_ = [lambda jj, u=u: tile_of(R, it, u, jj) for u in range(NU)]
                    X_ = [lambda jj, u=u: tile_of(X, it, u, jj) for u in range(NU)]
                    yn_ = [lambda jj, u=u: yn[u][:, jj, :] for u in range(NU)]
                    st = Steps(dve, dve_steps[1 + 2 * l])
                    if l == 0:
                        for u in range(NU):
                            stats(st, X_[u], u, d_var)
                        for u in range(NU):
                            need(dve, d_rstd, it, u)
                            normed(X_[u], R_[u], u).then_inc(q_r[l], 1)
                    for u in range(NU):
                        if l == 0:
                            need(dve, q_r[l], it, u)
                        need(dve, q_rr[l], it, u)
                        scaled(R_[u], yn_[u], u).then_inc(q_h[l], 1)
                    for u in range(NU):
                        need(dve, q_silu[l], it, u)
                        st.after(dve.tensor_scalar(beta[u][:, :, :], th[u][:, :, :], 1.0, None, ALU.add))
                        st.after(dve.tensor_tensor(sq[u][:, :, :], qkv[u][:, :, 0:2 * D], qkv[u][:, :, 0:2 * D], ALU.mult))
                        dve.tensor_reduce(ssh[u][:, 0:GT * 2 * H],
                                          sq[u][:, :, :].rearrange("p j (h e) -> p (j h) e", e=DK),
                                          AX.X, ALU.add).then_inc(q_n2[l], 1)
                    for u in range(NU):
                        need(dve, q_rn[l], it, u)
                        pk4 = PK[:, bass.ds(it * (NU * GT) + u * GT, GT), :].rearrange(
                            "p j (h t e) -> p j h t e", h=H, t=4)
                        rn = rstdh[u][:, 0:GT * 2 * H].rearrange("p (j h) -> p j h", j=GT)
                        for i in range(2):
                            q4 = qkv[u][:, :, i * D:(i + 1) * D].rearrange("p j (h e) -> p j h e", h=H)
                            last = dve.tensor_tensor(pk4[:, :, :, i, :], q4,
                                                     bc(rn[:, :, i * H:(i + 1) * H].unsqueeze(3), [P, GT, H, DK]), ALU.mult)
                            if i == 0:
                                st.after(last)
                        last.then_inc(q_qk[l], 1)
                    st.end()

                dve.wait_ge(scan_in[l], 16 * NA * HH)
                dve.wait_ge(st_free[l], NS)
                dve.memset(St[0], 0.0).then_inc(st_ready[l], 1)
                with dve.Fori(0, T // NS) as it:
                    st = Steps(dve, dve_steps[2 + 2 * l])
                    for i in range(NS):
                        need(dve, st_ready[l], it, i, per=NS)
                        ps = PS[:, bass.ds(it * NS + i, 1), :].rearrange("p o (g t e) -> p (o g) t e", g=H2, t=4)
                        st.after(dve.tensor_tensor(prod[:, :, :, :], St[i][:, :, :, :],
                                                   bc(ps[:, :, 2:3, :], [P, H2, DK, DK]), ALU.mult))
                        st.after(dve.tensor_reduce(pred[:, :, :], prod[:, :, :, :], AX.X, ALU.add))
                        st.after(dve.tensor_tensor(upd[:, :, :], ps[:, :, 3, :], pred[:, :, :], ALU.subtract))
                        st.after(dve.tensor_tensor(outer[:, :, :, :], bc(ps[:, :, 1:2, :], [P, H2, DK, DK]),
                                                   bc(upd[:, :, :].unsqueeze(3), [P, H2, DK, DK]), ALU.mult))
                        dve.wait_ge(st_free[l], it * NS + (i + 1))
                        dve.tensor_tensor(St[(i + 1) % NS][:, :, :, :], St[i][:, :, :, :], outer[:, :, :, :],
                                          ALU.add).then_inc(st_ready[l], 1)
                    st.end()

                dve.wait_ge(o_home[l], 16 * NA * HH)
                with dve.Fori(0, IT) as it:
                    R_ = [lambda jj, u=u: tile_of(R, it, u, jj) for u in range(NU)]
                    yn_ = [lambda jj, u=u: yn[u][:, jj, :] for u in range(NU)]
                    st = Steps(dve, dve_steps[2 * L + 1 + l])
                    for u in range(NU):
                        o_g = group_of(O, it, u)
                        st.after(dve.scalar_tensor_tensor(out=sq[u][:, 0:2, :].rearrange("p j c -> p (j c)"), in0=o_g,
                                                          scalar=1.0 / DK, in1=o_g, op0=ALU.mult, op1=ALU.mult))
                        dve.tensor_reduce(ssh[u][:, 0:GT * H],
                                          sq[u][:, 0:2, :].rearrange("p j c -> p (j c)").rearrange(
                                              "p (h e) -> p h e", e=DK), AX.X, ALU.add).then_inc(o_n2[l], 1)
                    for u in range(NU):
                        need(dve, o_rn[l], it, u)
                        dve.tensor_tensor(yn[u][:, :, :].rearrange("p j (h e) -> p (j h) e", e=DK),
                                          group_of(O, it, u).rearrange("p (h e) -> p h e", e=DK),
                                          bc(rstdh[u][:, 0:GT * H].unsqueeze(2), [P, GT * H, DK]),
                                          ALU.mult).then_inc(o_n[l], 1)
                    for u in range(NU):
                        need(dve, o_wo[l], it, u)
                        dve.tensor_tensor(group_of(R, it, u), banks[4 * u + 1][:, :], group_of(R, it, u),
                                          ALU.add).then_inc(r1_ready[l], 1)
                    for u in range(NU):
                        need(dve, r1_ready[l], it, u)
                        need(dve, m_rr[l], it, u)
                        scaled(R_[u], yn_[u], u).then_inc(m_h[l], 1)
                    for c, (f0, fn) in enumerate(IC):
                        for u in range(NU):
                            need(dve, m_silu[l], it, c * NU + u, per=3 * NU)
                            by = (2, 0, 2)[c]
                            dve.tensor_tensor(hT[u][0:fn, c, :], banks[4 * u + by][0:fn, :], act_g[u][0:fn, :],
                                              ALU.mult).then_inc(m_a[l], 1)
                    for u in range(NU):
                        need(dve, m_out[l], it, u)
                        dve.tensor_tensor(group_of(R, it, u), banks[4 * u + 3][:, :], group_of(R, it, u),
                                          ALU.add).then_inc(r2_ready, 1)
                    if l == L - 1:
                        for u in range(NU):
                            dve.wait_ge(r2_ready, it * NU + (IT * NU * (L - 1) + u + 1))
                            need(dve, f_rr, it, u)
                            scaled(R_[u], yn_[u], u).then_inc(f_n, 1)
                        for u in range(NU):
                            need(dve, f_w, it, u)
                            st.after(dve.tensor_tensor(group_of(X, it, u), group_of(X, it, u),
                                                       y[u][:, :, :].rearrange("p j c -> p (j c)"), ALU.add))
                    st.end()

            with dve.Fori(0, IT) as it:
                X_ = [lambda jj, u=u: tile_of(X, it, u, jj) for u in range(NU)]
                yn_ = [lambda jj, u=u: yn[u][:, jj, :] for u in range(NU)]
                st = Steps(dve, x_dve_steps)
                for u in range(NU):
                    stats(st, X_[u], u, e_var)
                for u in range(NU):
                    need(dve, e_rstd, it, u)
                    normed(X_[u], yn_[u], u).then_inc(e_h, 1)
                for u in range(NU):
                    need(dve, e_sig, it, u)
                    tt = dve.tensor_tensor
                    st.after(tt(sc[u][:, :, :], sg[u][:, :, :], bc(gbias[:, :].unsqueeze(1), [P, GT, E]), ALU.add))
                    pair = sc[u][:, :, :].rearrange("p j (g c k) -> p (j g) c k", g=NGRP, c=2)
                    tt(pmx[u][:, :, :], pair[:, :, :, 0], pair[:, :, :, 1], ALU.max)
                    st.after(tt(pmn[u][:, :, :], pair[:, :, :, 0], pair[:, :, :, 1], ALU.min))
                    tt(gs[u][:, 0, :], pmx[u][:, :, 0], pmx[u][:, :, 1], ALU.max)
                    tt(gs[u][:, 1, :], pmx[u][:, :, 0], pmx[u][:, :, 1], ALU.min)
                    st.after(tt(gs[u][:, 2, :], pmn[u][:, :, 0], pmn[u][:, :, 1], ALU.max))
                    st.after(tt(gs[u][:, 3, :], gs[u][:, 1, :], gs[u][:, 2, :], ALU.max))
                    st.after(tt(gs[u][:, 1, :], gs[u][:, 0, :], gs[u][:, 3, :], ALU.add))
                    for jj in range(GT):
                        mine = bc(gs[u][:, 1, jj * NGRP:(jj + 1) * NGRP].unsqueeze(2), [P, NGRP, NGRP])
                        other = bc(gs[u][:, 1, jj * NGRP:(jj + 1) * NGRP].unsqueeze(1), [P, NGRP, NGRP])
                        tt(cmp1[u][:, jj * NGRP:(jj + 1) * NGRP, :], other, mine, ALU.is_gt)
                        last = tt(cmp2[u][:, jj * NGRP:(jj + 1) * NGRP, :], other, mine, ALU.is_equal)
                    st.after(last)
                    c1 = cmp1[u][:, :, :].rearrange("p (j g) o -> p j (g o)", j=GT)
                    c2 = cmp2[u][:, :, :].rearrange("p (j g) o -> p j (g o)", j=GT)
                    st.after(tt(c2, c2, bc(before[:, :].unsqueeze(1), [P, GT, NGRP * NGRP]), ALU.mult))
                    st.after(tt(c1, c1, c2, ALU.add))
                    st.after(dve.tensor_reduce(gs[u][:, 2, :], cmp1[u][:, :, :],
                                               AX.X, ALU.add))
                    st.after(dve.tensor_scalar(gmask[u][:, :], gs[u][:, 2, :], TOPG - 0.5, None, ALU.is_lt))
                    four = msk[u][:, :, :].rearrange("p j (g k) -> p (j g) k", g=NGRP)
                    st.after(tt(four, sc[u][:, :, :].rearrange("p j (g k) -> p (j g) k", g=NGRP),
                                bc(gmask[u][:, :].unsqueeze(2), [P, GT * NGRP, E // NGRP]), ALU.mult))
                    st.after(dve.tensor_scalar(msk[u][:, :, :], msk[u][:, :, :], 0.0, None, ALU.add))
                    for jj in range(GT):
                        last = dve.max(top8[u][:, jj, :], msk[u][:, jj, :])
                    st.after(last)
                    for jj in range(GT):
                        last = dve.match_replace(rep[u][:, jj, :], top8[u][:, jj, :], msk[u][:, jj, :], REPLACED)
                    st.after(last)
                    st.after(tt(rep[u][:, :, :], rep[u][:, :, :], msk[u][:, :, :], ALU.not_equal))
                    st.after(tt(rep[u][:, :, :], rep[u][:, :, :], sg[u][:, :, :], ALU.mult))
                    st.after(dve.tensor_reduce(den[u][:, :], rep[u][:, :, :], AX.X, ALU.add))
                    st.after(dve.tensor_scalar(den[u][:, :], den[u][:, :], 1e-20, None, ALU.add))
                    st.after(dve.reciprocal(mx[u][:, :], den[u][:, :]))
                    st.after(dve.tensor_scalar(mx[u][:, :], mx[u][:, :], ROUTE_SCALE, None, ALU.mult))
                    tt(comb[u][:, :, :], rep[u][:, :, :], bc(mx[u][:, :].unsqueeze(2), [P, GT, E]),
                       ALU.mult).then_inc(e_comb, 1)
                for u in range(NU):
                    need(dve, e_cf, it, u)
                    st.after(dve.tensor_copy(c3[u][0:E, :], cf[u][:, :]))
                    st.after(dve.tensor_tensor(cf[u][:, :], cf[u][:, :], c3[u][0:E, :], ALU.subtract))
                    st.after(dve.tensor_copy(cmid[u][:, :], cf[u][:, :]))
                    dve.tensor_tensor(c3[u][2 * E:3 * E, :], cf[u][:, :], cmid[u][:, :], ALU.subtract).then_inc(e_c3, 1)
                for p in range(-1, NPAIR):
                    for u in range(NU):
                        n = (p + 1) * NU + u
                        need(dve, x_silu, it, n, per=(NPAIR + 1) * NU)
                        if n >= NU:
                            need(dve, x_down, it, n - NU, per=(NPAIR + 1) * NU)
                        dst = act_a[u] if p < 0 else act_gu[u]
                        dve.tensor_tensor(dst[:, :], banks[4 * u + 1][:, :], act_g[u][:, :],
                                          ALU.mult).then_inc(x_a if p < 0 else x_gu, 1)
                        if p >= 0:
                            need(dve, x_gu, it, n - NU, per=NPAIR * NU)
                            dve.tensor_tensor(act_a[u][:, :], banks[4 * u + 2][:, :], act_gu[u][:, :],
                                              ALU.mult).then_inc(x_a, 1)
                for u in range(NU):
                    need(dve, e_otr, it, u)
                    dve.tensor_tensor(r[u][:, :, :].rearrange("p j c -> p (j c)"), banks[4 * u][:, :],
                                      group_of(X, it, u), ALU.add).then_inc(e_xo, 1)
                st.end()


def _layout(inputs):
    import numpy as np

    a = {k: np.asarray(v) for k, v in inputs.items()}

    def tr(w):
        return np.ascontiguousarray(w.T)

    def chunks(w, n):
        return w.reshape(n, P, -1).transpose(1, 0, 2)

    ctx = a["ctx_1024"].reshape(NA, NJ, KEYS, D)
    o = {}
    o["x"] = a["x"].reshape(NA, NJ, S, D).transpose(0, 2, 1, 3).reshape(P, NJ * D)
    o["ctx_t"] = ctx.transpose(1, 3, 0, 2).reshape(NJ, D, NA * KEYS)
    o["ctx_z"] = ctx[:, :, :KEYS - 1].reshape(NA, NJ, 2, P, D).transpose(1, 3, 2, 0, 4).reshape(NJ, P, 2 * NA * D)
    o["ctx_last"] = ctx[:, :, KEYS - 1].reshape(NA, NJ * D)
    o["rows"] = np.stack([a["L0_xattn_g1"], a["L0_xattn_beta1"], a["L0_xattn_g2"], a["L0_xattn_beta2"],
                          a["L0_xattn_g3"], a["L0_xattn_beta3"], a["L0_xattn_b2"], a["L0_attn_final_norm_w"]])
    o["cols"] = np.concatenate([a["L0_attn_norm1_w"].T, a["L0_attn_norm2_w"].T,
                                np.concatenate([a["L0_attn_onorm_w"].T] * H, axis=0),
                                a["L0_xattn_b1"].reshape(FFC, P).T], axis=1)
    o["w1"] = a["L0_xattn_w1"]
    o["w2"] = chunks(a["L0_xattn_w2"], FFC)
    o["wqkvb"] = np.concatenate([a["L0_attn_Wq"], a["L0_attn_Wk"], a["L0_attn_Wv"], a["L0_attn_Wb"]],
                                axis=2).transpose(1, 0, 2)
    o["wo"] = a["L0_attn_Wo"].transpose(1, 0, 2)
    o["wgu"] = a["L0_attn_Wg"].transpose(1, 0, 2)
    wd = np.zeros((L, 3 * P, D), a["L0_attn_Wd"].dtype)
    wd[:, :INTER] = a["L0_attn_Wd"]
    o["wd"] = wd.reshape(L, 3, P, D).transpose(2, 0, 1, 3)
    o["gate_t"] = tr(a["L0_ffn_gate_w"])
    o["gate_bias"] = a["L0_ffn_gate_bias"].reshape(1, E)
    o["we_gate"] = tr(a["L0_ffn_w_gate"].reshape(E * EI, D)).reshape(D, NPAIR, P)
    o["we_up"] = tr(a["L0_ffn_w_up"].reshape(E * EI, D)).reshape(D, NPAIR, P)
    o["we_down"] = chunks(a["L0_ffn_w_down"].transpose(0, 2, 1).reshape(E * EI, D), NPAIR)
    o["sh_gate"] = tr(a["L0_ffn_sh_gate"])
    o["sh_up"] = tr(a["L0_ffn_sh_up"])
    o["sh_down"] = tr(a["L0_ffn_sh_down"])
    o["ident"] = np.eye(P, dtype=np.float32)
    q, k = np.arange(P)[:, None] % S, np.arange(S)[None, :]
    o["causal"] = np.where(k <= q, 0.0, NEG).astype(np.float32)
    spread = np.zeros((3, E, NPAIR, 2, EI), np.uint16)
    for e in range(E):
        spread[:, e, e // 2, e % 2, :] = 0x3F80
    o["spread"] = spread.reshape(3 * E, NPAIR * P)
    g = np.arange(NGRP)
    before = (g[None, :] < g[:, None]).astype(np.float32).reshape(1, NGRP * NGRP)
    o["before"] = np.repeat(before, P, axis=0)
    return {k_: np.ascontiguousarray(v) for k_, v in o.items()}


_ORDER = ["x", "ctx_t", "ctx_z", "ctx_last", "rows", "cols", "w1", "w2", "wqkvb", "wo", "wgu", "wd", "gate_t",
          "gate_bias", "we_gate", "we_up", "we_down", "sh_gate", "sh_up", "sh_down", "ident", "causal", "spread",
          "before"]


def kernel(**inputs):
    import numpy as _np
    import concourse.bacc as _bacc
    from concourse import mybir as _mybir
    from concourse.bass_utils import run_bass_kernel_spmd as _run

    nc = _bacc.Bacc("TRN2", target_bir_lowering=False, num_devices=1)
    laid = _layout(inputs)
    arrays, args = {}, []
    for name in _ORDER:
        arr = laid[name]
        arrays[f"in_{name}"] = arr
        args.append(nc.dram_tensor(f"in_{name}", arr.shape, _mybir.dt.from_np(arr.dtype), kind="ExternalInput").ap())
    args.append(nc.dram_tensor("out_0", (P, NJ * D), _mybir.dt.float32, kind="ExternalOutput").ap())
    perceiver(nc, *args)
    res = _run(nc, [arrays], core_ids=[0])
    got = _np.asarray(res.results[0]["out_0"])
    return _np.ascontiguousarray(got.reshape(NA, S, NJ, D).transpose(0, 2, 1, 3).reshape(NA * NJ, S, D))
```

```python
from contextlib import ExitStack

import concourse.bass as bass
from concourse import mybir

F32 = mybir.dt.float32
I32 = mybir.dt.int32
BF16 = mybir.dt.bfloat16
ALU = mybir.AluOpType
ACT = mybir.ActivationFunctionType
AX = mybir.AxisListType

P = 128
D = 128
NJ = 16
GT = 4
GW = GT * D
NU = 2
IT = NJ // (GT * NU)
NA, S = 4, 32
KEYS = 257
FFC = 4
L = 2
H, DK = 8, 16
HH, H2 = 4, 2
T = 64
QKVB = 3 * D + H
INTER = 352
IC = [(0, 128), (128, 128), (256, 96)]
E = 32
EI = 64
NPAIR = E // 2
NGRP = 8
TOPG = 4
SCALE_ATT = float(D) ** -0.5
EPS_LN, EPS_RMS = 1e-5, 1e-6
NEG = -1e30
RSQRT_MAGIC = float(0x5F3759DF)
REPLACED = -3e38
ROUTE_SCALE = 2.5

G1, BE1, G2, BE2, G3, BE3, B2, FINALW = range(8)
C_N1, C_N2, C_ON, C_B1 = 0, L, 2 * L, 3 * L
C_G1, C_G2 = 3 * L + FFC, 3 * L + FFC + 2


class Steps:

    def __init__(self, eng, sem):
        self.eng, self.sem, self.n = eng, sem, 0

    def after(self, ins):
        ins.then_inc(self.sem, 1)
        self.n += 1
        self.eng.wait_ge(self.sem, self.n)

    def end(self):
        self.eng.sem_clear(self.sem)


def need(eng, sem, it, k, per=NU):
    eng.wait_ge(sem, it * per + (k + 1))


def perceiver(nc, x, ctx_t, ctx_z, ctx_last, rows, cols, w1, w2, wqkvb, wo, wgu, wd, gate_t, gate_bias,
              we_gate, we_up, we_down, sh_gate, sh_up, sh_down, ident_in, causal_in, spread_in, before_in, out):
    with ExitStack() as stack:
        def sb(name, shape, dt=F32):
            return stack.enter_context(nc.sbuf_tensor(name, shape, dt))

        def sem(name):
            return stack.enter_context(nc.semaphore(name))

        banks = [stack.enter_context(nc.psum_tensor(f"bank{i}", [P, 512], F32)) for i in range(8)]

        ident = sb("ident", [P, P])
        causal = sb("causal", [P, S])
        spread = sb("spread", [96, NPAIR * P], BF16)
        before = sb("before", [P, NGRP * NGRP])
        rowv = sb("rowv", [P, 8, D])
        colv = sb("colv", [P, 3 * L + FFC + 4])
        gb1s = sb("gb1s", [P, 2])
        gbias = sb("gbias", [P, E])
        w1_sb = sb("w1_sb", [P, FFC * P])
        w2_sb = sb("w2_sb", [P, FFC, D])
        wqkvb_sb = sb("wqkvb_sb", [P, L, QKVB])
        wo_sb = sb("wo_sb", [P, L, D])
        wgu_sb = sb("wgu_sb", [P, L, 2 * INTER])
        wd_sb = sb("wd_sb", [P, L, 3, D])
        gate_sb = sb("gate_sb", [P, E])
        weg_sb = sb("weg_sb", [P, NPAIR + 1, P])
        weu_sb = sb("weu_sb", [P, NPAIR + 1, P])
        wed_sb = sb("wed_sb", [P, NPAIR + 1, D])
        neg_half, eps_ln, eps_rms = sb("neg_half", [P, 64]), sb("eps_ln", [P, 64]), sb("eps_rms", [P, 64])

        X = sb("X", [P, NJ * D])
        R = sb("R", [P, NJ * D])
        zlast = sb("zlast", [P, NJ * D])
        NRING = 8
        arena = sb("arena", [P, NRING * (NA * KEYS + 2 * NA * D)])
        zt_ring = arena[:, 0:NRING * NA * KEYS].rearrange("p (n c) -> p n c", n=NRING)
        z_ring = arena[:, NRING * NA * KEYS:].rearrange("p (n c) -> p n c", n=NRING)
        PKW = H * 4 * DK
        PK = arena[:, 0:NJ * PKW].rearrange("p (n c) -> p n c", n=NJ)
        PS = arena[:, NJ * PKW:NJ * PKW + T * D].rearrange("p (t c) -> p t c", t=T)
        Os = sb("Os", [P, T * 32])
        O = zlast

        yr = [sb(f"yr{u}", [P, 2 * GT, D]) for u in range(NU)]
        y = [yr[u][:, 0:GT, :] for u in range(NU)]
        yn = [sb(f"yn{u}", [P, GT, D]) for u in range(NU)]
        r = [yr[u][:, GT:2 * GT, :] for u in range(NU)]
        yT = [sb(f"yT{u}", [P, GW]) for u in range(NU)]
        NST, HS = 8, 4
        SW = H2 * DK * (DK + 1)
        mid = sb("mid", [P, NST * SW])
        hT = [mid[:, u * FFC * GW:(u + 1) * FFC * GW].rearrange("p (c n) -> p c n", c=FFC) for u in range(NU)]
        stat = [sb(f"stat{u}", [P, GT, 6]) for u in range(NU)]
        mv = [sb(f"mv{u}", [P, GT, 2]) for u in range(NU)]
        ve = [sb(f"ve{u}", [P, 64]) for u in range(NU)]
        rstd = [sb(f"rstd{u}", [P, 64]) for u in range(NU)]
        ss = [sb(f"ss{u}", [P, GT]) for u in range(NU)]
        ssh = [sb(f"ssh{u}", [P, 64]) for u in range(NU)]
        rstdh = [sb(f"rstdh{u}", [P, 64]) for u in range(NU)]
        s1 = [sb(f"s1{u}", [P, GT, S]) for u in range(NU)]
        p1 = [sb(f"p1{u}", [P, GT, S]) for u in range(NU)]
        p1T = [sb(f"p1T{u}", [P, GT, S]) for u in range(NU)]
        mx = [sb(f"mx{u}", [P, GT]) for u in range(NU)]
        rs1 = [sb(f"rs1{u}", [P, GT]) for u in range(NU)]
        ri1 = [sb(f"ri1{u}", [P, GT]) for u in range(NU)]
        NT = NU * GT
        nmax = sb("nmax", [P, NT])
        rsum = sb("rsum", [P, NT])
        rinv = sb("rinv", [P, NT])
        pc = sb("pc", [P, NT, KEYS])
        pcT = sb("pcT", [P, NT, 2 * P])
        qkv = [pc[:, 0:6, :].rearrange("p n c -> p (n c)")[:, 0:GT * 3 * D].rearrange("p (j c) -> p j c", j=GT),
               pcT[:, 0:6, :].rearrange("p n c -> p (n c)").rearrange("p (j c) -> p j c", j=GT)]
        sq = [yr[u][:, :, :].rearrange("p (j i) c -> p j (i c)", j=GT) for u in range(NU)]
        th = [sb(f"th{u}", [P, GT, H]) for u in range(NU)]
        beta = [sb(f"beta{u}", [P, GT, H]) for u in range(NU)]
        act_o = sb("act_o", [P, 2 * GW])
        def carve(flat):
            at = [0]

            def take(shape, parts=P, dt=F32):
                n = 1
                for d in shape:
                    n *= d
                words = n if dt is F32 else n // 2
                piece = flat[0:parts, at[0]:at[0] + words]
                at[0] += words
                if dt is not F32:
                    piece = piece.bitcast(dt)
                if len(shape) == 1:
                    return piece
                names = "abc"[:len(shape)]
                return piece.rearrange(f"p ({' '.join(names)}) -> p {' '.join(names)}",
                                       **{k: v for k, v in zip(names, shape)})
            return take

        ring = mid[:, :].rearrange("p (i g v k) -> p i g v k", i=NST, g=H2, v=DK)
        St = [ring[:, i] for i in range(NST)]
        take = carve(pc[:, :, :].rearrange("p n c -> p (n c)"))
        oprod = take((HS * H2, DK, DK))
        take = carve(pcT[:, :, :].rearrange("p n c -> p (n c)"))
        prod, outer = take((H2 * DK, DK + 1)), take((H2 * DK, DK))
        prod = prod.rearrange("p (g v) k -> p g v k", g=H2)
        outer = outer.rearrange("p (g v) k -> p g v k", g=H2)
        negu = take((H2, DK))
        kb_now = [take((HS * H2, DK + 1)) for k in range(2)]
        k_now = [take((HS * H2, DK)) for k in range(2)]
        osum2 = take((HS * H2, DK, 2))
        osum4 = carve(yT[0][:, :])((HS * H2, DK, 4))
        osum8 = carve(act_o[:, :])((HS * H2, DK, 8))
        take = carve(pc[:, :, :].rearrange("p n c -> p (n c)"))
        sg = [take((GT, E)) for u in range(NU)]
        sc = [take((GT, E)) for u in range(NU)]
        msk = [take((GT, E)) for u in range(NU)]
        rep = [take((GT, E)) for u in range(NU)]
        comb = [take((GT, E)) for u in range(NU)]
        gs = [take((4, GT * NGRP)) for u in range(NU)]
        gmask = [take((GT * NGRP,)) for u in range(NU)]
        pmx = [take((GT * NGRP, 2)) for u in range(NU)]
        pmn = [take((GT * NGRP, 2)) for u in range(NU)]
        top8 = [take((GT, 8)) for u in range(NU)]
        den = [take((GT,)) for u in range(NU)]
        take = carve(pcT[:, :, :].rearrange("p n c -> p (n c)"))
        cmp1 = [take((GT * NGRP, NGRP)) for u in range(NU)]
        cmp2 = [take((GT * NGRP, NGRP)) for u in range(NU)]
        take = carve(arena[:, :])
        cf = [take((GW,), E) for u in range(NU)]
        c3 = [take((GW,), 3 * E, BF16) for u in range(NU)]
        cmid = [take((GW,), E, BF16) for u in range(NU)]
        act_g = [act_o[:, u * GW:(u + 1) * GW] for u in range(NU)]
        scrap = [sb(f"scrap{u}", [P, 1]) for u in range(NU)]
        scrap2 = [sb(f"scrap2{u}", [P, 1]) for u in range(NU)]
        act_gu = [hT[u][:, 0, :] for u in range(NU)]
        act_a = [hT[u][:, 1, :] for u in range(NU)]

        x_in, const_in, zlast_in, w_in = sem("x_in"), sem("const_in"), sem("zlast_in"), sem("w_in")
        ring_in = [sem(f"ring_in{i}") for i in range(NRING)]
        consts_made, gb1s_made = sem("consts_made"), sem("gb1s_made")
        dve_steps, pool_steps = sem("dve_steps"), sem("pool_steps")
        a_var, a_rstd, a_norm, a_scaled = sem("a_var"), sem("a_rstd"), sem("a_norm"), sem("a_scaled")
        a_y, a_tr, a_yT = sem("a_y"), sem("a_tr"), sem("a_yT")
        sa_scores, sa_shift, sa_exp, sa_pT, sa_out = (sem("sa_scores"), sem("sa_shift"), sem("sa_exp"),
                                                      sem("sa_pT"), sem("sa_out"))
        ca_scores, ca_max, ca_exp, ca_tr, ca_pT, ca_out = (sem("ca_scores"), sem("ca_max"), sem("ca_exp"),
                                                           sem("ca_tr"), sem("ca_pT"), sem("ca_out"))
        ff_up, ff_h, ff_out, ff_res = sem("ff_up"), sem("ff_h"), sem("ff_out"), sem("ff_res")
        def lsem(name):
            return [sem(f"{name}_{l}") for l in range(L)]
        d_var, d_rstd = sem("d_var"), sem("d_rstd")
        q_r, q_ss, q_rr, q_h, q_tr, q_hT, q_proj, q_silu, q_qk, q_pk = map(lsem, (
            "q_r", "q_ss", "q_rr", "q_h", "q_tr", "q_hT", "q_proj", "q_silu", "q_qk",
            "q_pk"))
        scan_in = [[sem(f"scan_in_{l}_{a}") for a in range(NA)] for l in range(L)]
        st_init, st_fed = map(lsem, ("st_init", "st_fed"))
        st_ready, st_free, o_ready, o_home = map(lsem, ("st_ready", "st_free", "o_ready", "o_home"))
        o_n, o_tr, o_oT, o_wo, r1_ready, m_ss, m_rr, m_h, m_tr, m_hT, m_gu, m_silu, m_a, m_out = map(
            lsem, ("o_n", "o_tr", "o_oT", "o_wo", "r1_ready", "m_ss", "m_rr", "m_h", "m_tr",
                   "m_hT", "m_gu", "m_silu", "m_a", "m_out"))
        r2_ready, f_ss, f_rr, f_n, f_w = sem("r2_ready"), sem("f_ss"), sem("f_rr"), sem("f_n"), sem("f_w")
        e_var, e_rstd, e_h, e_tr, e_hT, e_log, e_sig, e_comb, e_ctr, e_c3, e_mid, e_cf = (
            sem("e_var"), sem("e_rstd"), sem("e_h"), sem("e_tr"), sem("e_hT"), sem("e_log"), sem("e_sig"),
            sem("e_comb"), sem("e_ctr"), sem("e_c3"), sem("e_mid"), sem("e_cf"))
        x_gate, x_silu, x_gu, x_a, x_down = sem("x_gate"), sem("x_silu"), sem("x_gu"), sem("x_a"), sem("x_down")
        e_acc, e_otr, e_xo = sem("e_acc"), sem("e_otr"), sem("e_xo")
        out_done = [sem(f"out_done{u}") for u in range(NU)]

        consts = [(ident, ident_in), (causal, causal_in), (spread[:, :].bitcast(mybir.dt.uint16), spread_in), (before, before_in),
                  (colv, cols)]
        N_CONST = 16 * (len(consts) + 8 + 1)
        weights = [(w1_sb, w1), (w2_sb, w2), (wqkvb_sb, wqkvb), (wo_sb, wo), (wgu_sb, wgu), (wd_sb, wd),
                   (gate_sb, gate_t), (weg_sb, we_gate), (weu_sb, we_up), (wed_sb, we_down)]
        shared = [(weg_sb, sh_gate), (weu_sb, sh_up), (wed_sb, sh_down)]
        N_WEIGHT = 16 * (len(weights) + len(shared))

        def whole(t):
            if isinstance(t, bass.AP):
                return t
            return t[:, :] if len(t.shape) == 2 else t[:, :, :] if len(t.shape) == 3 else t[:, :, :, :]

        def tile_of(t, it, u, jj):
            return t[:, bass.ds(it * (NU * GW) + (u * GW + jj * D), D)]

        def group_of(t, it, u):
            return t[:, bass.ds(it * (NU * GW) + u * GW, GW)]

        def bc(ap, shape):
            return ap.to_broadcast(shape)

        block = stack.enter_context(nc.Block())

        @block.sync
        def _(sp):
            sp.dma_start(X[:, :], x).then_inc(x_in, 16)
            for dst, src in consts:
                sp.dma_start(whole(dst), src).then_inc(const_in, 16)
            for i in range(8):
                sp.dma_start(rowv[:, i, :], rows[i:i + 1, :].partition_broadcast(P)).then_inc(const_in, 16)
            sp.dma_start(gbias[:, :], gate_bias.partition_broadcast(P)).then_inc(const_in, 16)

            def load_ctx(half):
                for n in range(NRING):
                    if half > 0:
                        sp.wait_ge(ca_out, (half - 1) * NT + n + 1)
                    sp.dma_start(zt_ring[:, n, :], ctx_t[half * NRING + n]).then_inc(ring_in[n], 16)
                    sp.dma_start(z_ring[:, n, :], ctx_z[half * NRING + n]).then_inc(ring_in[n], 16)

            load_ctx(0)
            for a in range(NA):
                sp.dma_start(zlast[S * a:S * a + S, :],
                             ctx_last[a:a + 1, :].partition_broadcast(S)).then_inc(zlast_in, 16)
            for dst, src in weights:
                d = dst[:, 0:NPAIR, :] if dst is weg_sb or dst is weu_sb or dst is wed_sb else whole(dst)
                sp.dma_start(d, src).then_inc(w_in, 16)
            for dst, src in shared:
                sp.dma_start(dst[:, NPAIR, :], src).then_inc(w_in, 16)
            load_ctx(1)

            for l in range(L):
                sp.wait_ge(q_pk[l], IT * NU)
                sp.wait_ge(q_qk[l], IT * NU)
                for a in range(NA):
                    for hh in range(HH):
                        sp.dma_start(PS[S * hh:S * hh + S, NJ * a:NJ * a + NJ, :],
                                     PK[S * a:S * a + S, :, D * hh:D * hh + D]).then_inc(scan_in[l][a], 16)
                for a in range(NA):
                    sp.wait_ge(o_ready[l], NJ // HS * (a + 1))
                    for hh in range(HH):
                        sp.dma_start(O[S * a:S * a + S, :].rearrange("p (j c) -> p j c", j=NJ)[:, :, 32 * hh:32 * hh + 32],
                                     Os[S * hh:S * hh + S, 32 * NJ * a:32 * NJ * (a + 1)]
                                     .rearrange("p (j c) -> p j c", j=NJ)).then_inc(o_home[l], 16)

            with sp.Fori(0, IT) as it:
                for u in range(NU):
                    need(sp, e_xo, it, u)
                    sp.dma_start(out[:, bass.ds(it * (NU * GW) + u * GW, GW)],
                                 r[u][:, :, :].rearrange("p j c -> p (j c)")).then_inc(out_done[u], 16)
            for u in range(NU):
                sp.wait_ge(out_done[u], 16 * (IT + 1))

        @block.tensor
        def _(pe):
            def transposes(bank, src, u, ready):
                for jj in range(GT):
                    last = pe.transpose(bank[:, jj * D:(jj + 1) * D], src[u][:, jj, :], ident[:, :])
                last.then_inc(ready, 1)

            pe.wait_ge(const_in, N_CONST)

            with pe.Fori(0, IT) as it:
                for u in range(NU):
                    need(pe, a_y, it, u)
                    transposes(banks[6 + u], y, u, a_tr)
                for u in range(NU):
                    need(pe, a_yT, it, u, per=3 * NU)
                    for jj in range(GT):
                        for a in range(NA):
                            q = yT[u][:, jj * D + a * S:jj * D + a * S + S]
                            last = pe.matmul(banks[6 + u][a * S:a * S + S, jj * S:jj * S + S], q, q,
                                             start=True, stop=True)
                    last.then_inc(sa_scores, 1)
                for u in range(NU):
                    pe.wait_ge(sa_pT, u + 1)
                    for jj in range(GT):
                        for a in range(NA):
                            rows_ = slice(a * S, a * S + S)
                            last = pe.matmul(banks[6 + u][rows_, jj * D:(jj + 1) * D], p1T[u][rows_, jj, :],
                                             y[u][rows_, jj, :], start=True, stop=True)
                    last.then_inc(sa_out, 1)
                pe.sem_clear(sa_pT)
                for u in range(NU):
                    need(pe, a_norm, it, u, per=3 * NU)
                    transposes(banks[6 + u], yn, u, a_tr)

                def scores(n):
                    u, jj = divmod(n, GT)
                    need(pe, a_yT, it, NU + u, per=3 * NU)
                    pe.wait_ge(ring_in[n], 32 * it + 32)
                    for a in range(NA):
                        last = pe.matmul(banks[n % 2][a * S:a * S + S, 0:KEYS],
                                         yT[u][:, jj * D + a * S:jj * D + a * S + S],
                                         zt_ring[:, n, a * KEYS:(a + 1) * KEYS], start=True, stop=True)
                    last.then_inc(ca_scores, 1)

                def turn(n):
                    need(pe, ca_exp, it, n, per=NT)
                    for c in range(2):
                        last = pe.transpose(banks[2 + n % 2][:, c * P:(c + 1) * P], pc[:, n, c * P:(c + 1) * P],
                                            ident[:, :])
                    last.then_inc(ca_tr, 1)

                def attend(n):
                    u, jj = divmod(n, GT)
                    need(pe, ca_pT, it, n, per=NT)
                    for a in range(NA):
                        for c in range(2):
                            last = pe.matmul(banks[4 + u][a * S:a * S + S, jj * D:(jj + 1) * D],
                                             pcT[:, n, c * P + a * S:c * P + a * S + S],
                                             z_ring[:, n, (c * NA + a) * D:(c * NA + a + 1) * D],
                                             start=(c == 0), stop=(c == 1))
                    last.then_inc(ca_out, 1)

                for n in range(NT + 2):
                    if n < NT:
                        scores(n)
                    if 1 <= n <= NT:
                        turn(n - 1)
                    if n >= 2:
                        attend(n - 2)
                for u in range(NU):
                    need(pe, a_norm, it, NU + u, per=3 * NU)
                    transposes(banks[6 + u], yn, u, a_tr)
                pe.wait_ge(w_in, N_WEIGHT)
                for u in range(NU):
                    need(pe, a_yT, it, 2 * NU + u, per=3 * NU)
                    for c in range(FFC):
                        if c >= 2:
                            need(pe, ff_h, it, u * FFC + c - 2, per=NU * FFC)
                        pe.matmul(banks[2 * u + c % 2][:, :], w1_sb[:, c * P:(c + 1) * P], yT[u][:, :],
                                  start=True, stop=True).then_inc(ff_up, 1)
                for u in range(NU):
                    need(pe, ff_h, it, u * FFC + FFC - 1, per=NU * FFC)
                    for jj in range(GT):
                        for c in range(FFC):
                            last = pe.matmul(banks[4 + u][:, jj * D:(jj + 1) * D], hT[u][:, c, jj * D:(jj + 1) * D],
                                             w2_sb[:, c, :], start=(c == 0), stop=(c == FFC - 1))
                    last.then_inc(ff_out, 1)

            for l in range(L):
                with pe.Fori(0, IT) as it:
                    for u in range(NU):
                        need(pe, q_h[l], it, u)
                        transposes(banks[4 * u], yn, u, q_tr[l])
                    for u in range(NU):
                        need(pe, q_hT[l], it, u)
                        for jj in range(GT):
                            pe.matmul(banks[4 * u + jj][:, 0:QKVB], yT[u][:, jj * D:(jj + 1) * D],
                                      wqkvb_sb[:, l, :], start=True, stop=True).then_inc(q_proj[l], 1)

                with pe.Fori(0, IT) as it:
                    for u in range(NU):
                        need(pe, o_n[l], it, u)
                        transposes(banks[4 * u], yn, u, o_tr[l])
                    for u in range(NU):
                        need(pe, o_oT[l], it, u)
                        for jj in range(GT):
                            last = pe.matmul(banks[4 * u + 1][:, jj * D:(jj + 1) * D], yT[u][:, jj * D:(jj + 1) * D],
                                             wo_sb[:, l, :], start=True, stop=True)
                        last.then_inc(o_wo[l], 1)
                    for u in range(NU):
                        need(pe, m_h[l], it, u)
                        transposes(banks[4 * u], yn, u, m_tr[l])
                    for c, (f0, fn) in enumerate(IC):
                        for u in range(NU):
                            need(pe, m_hT[l], it, u)
                            if c == 2:
                                need(pe, m_a[l], it, u, per=3 * NU)
                            bg, by = ((1, 2), (3, 0), (1, 2))[c]
                            pe.matmul(banks[4 * u + bg][0:fn, :], wgu_sb[:, l, f0:f0 + fn], yT[u][:, :],
                                      start=True, stop=True)
                            pe.matmul(banks[4 * u + by][0:fn, :], wgu_sb[:, l, INTER + f0:INTER + f0 + fn],
                                      yT[u][:, :], start=True, stop=True).then_inc(m_gu[l], 1)
                    for u in range(NU):
                        need(pe, m_a[l], it, 2 * NU + u, per=3 * NU)
                        for jj in range(GT):
                            for c, (f0, fn) in enumerate(IC):
                                last = pe.matmul(banks[4 * u + 3][:, jj * D:(jj + 1) * D],
                                                 hT[u][0:fn, c, jj * D:(jj + 1) * D], wd_sb[0:fn, l, c, :],
                                                 start=(c == 0), stop=(c == 2))
                        last.then_inc(m_out[l], 1)

            with pe.Fori(0, IT) as it:
                for u in range(NU):
                    need(pe, e_h, it, u)
                    transposes(banks[4 * u], yn, u, e_tr)
                for u in range(NU):
                    need(pe, e_hT, it, u)
                    for jj in range(GT):
                        last = pe.matmul(banks[4 * u + 1][:, jj * E:(jj + 1) * E], yT[u][:, jj * D:(jj + 1) * D],
                                         gate_sb[:, :], start=True, stop=True)
                    last.then_inc(e_log, 1)

                def gate_up(p, u):
                    n = (p + 1) * NU + u
                    if n >= NU:
                        need(pe, x_a, it, n - NU, per=(NPAIR + 1) * NU)
                    w = p % (NPAIR + 1)
                    pe.matmul(banks[4 * u][:, :], weg_sb[:, w, :], yT[u][:, :], start=True, stop=True)
                    last = pe.matmul(banks[4 * u + 1][:, :], weu_sb[:, w, :], yT[u][:, :], start=True, stop=True)
                    if p >= 0:
                        last = pe.matmul(banks[4 * u + 2][:, :], spread[:, p * P:(p + 1) * P], c3[u][:, :],
                                         start=True, stop=True)
                    last.then_inc(x_gate, 1)

                def down(p, u):
                    n = (p + 1) * NU + u
                    need(pe, x_a, it, n, per=(NPAIR + 1) * NU)
                    pe.matmul(banks[4 * u + 3][:, :], wed_sb[:, p % (NPAIR + 1), :], act_a[u][:, :],
                              start=(p == -1), stop=(p == NPAIR - 1), skip_group_check=True).then_inc(x_down, 1)

                for u in range(NU):
                    need(pe, e_comb, it, u)
                    for jj in range(GT):
                        last = pe.transpose(banks[4 * u + 2][0:E, jj * D:(jj + 1) * D], comb[u][:, jj, :], ident[:, :])
                    last.then_inc(e_ctr, 1)
                order = [(p, u) for p in range(-1, NPAIR) for u in range(NU)]
                for n in range(len(order) + NU):
                    if n < len(order):
                        if n == NU or n == NU + 1:
                            need(pe, e_c3, it, n - NU)
                            need(pe, e_mid, it, n - NU)
                        gate_up(*order[n])
                    if n >= NU:
                        down(*order[n - NU])
                for u in range(NU):
                    need(pe, e_acc, it, u)
                    for jj in range(GT):
                        last = pe.transpose(banks[4 * u][:, jj * D:(jj + 1) * D], r[u][:, jj, :], ident[:, :])
                    last.then_inc(e_otr, 1)

        @block.scalar
        def _(act):
            def copy(out_, in_, scale=1.0):
                return act.activation(out_, in_, ACT.Copy, scale=scale)

            act.wait_ge(const_in, N_CONST)
            copy(gb1s[:, :], colv[:, C_G1:C_G1 + 2], SCALE_ATT).then_inc(gb1s_made, 1)
            act.wait_ge(gb1s_made, 1)
            with act.Fori(0, IT) as it:
                for u in range(NU):
                    need(act, a_tr, it, u, per=3 * NU)
                    copy(yT[u][:, :], banks[6 + u][:, :]).then_inc(a_yT, 1)
                for u in range(NU):
                    need(act, sa_shift, it, u)
                    act.activation(p1[u][:, :, :], s1[u][:, :, :], ACT.Exp, scale=SCALE_ATT).then_inc(sa_exp, 1)
                for u in range(NU):
                    need(act, a_tr, it, NU + u, per=3 * NU)
                    act.activation(yT[u][:, :], banks[6 + u][:, :], ACT.Identity, bias=gb1s[:, 1:2],
                                   scale=gb1s[:, 0:1]).then_inc(a_yT, 1)
                for n in range(NT):
                    need(act, ca_max, it, n, per=NT)
                    act.activation(pc[:, n, :], banks[n % 2][:, 0:KEYS], ACT.Exp, bias=nmax[:, n:n + 1],
                                   accum_out=rsum[:, n:n + 1]).then_inc(ca_exp, 1)
                for u in range(NU):
                    need(act, a_tr, it, 2 * NU + u, per=3 * NU)
                    act.activation(yT[u][:, :], banks[6 + u][:, :], ACT.Identity, bias=colv[:, C_G2 + 1:C_G2 + 2],
                                   scale=colv[:, C_G2:C_G2 + 1]).then_inc(a_yT, 1)
                for u in range(NU):
                    for c in range(FFC):
                        need(act, ff_up, it, u * FFC + c, per=NU * FFC)
                        act.activation(hT[u][:, c, :], banks[2 * u + c % 2][:, :], ACT.Relu,
                                       bias=colv[:, C_B1 + c:C_B1 + c + 1]).then_inc(ff_h, 1)

            def squares(src, it, u, done, sem_in=None, k=0, per=NU):
                if sem_in is not None:
                    need(act, sem_in, it, k, per=per)
                    copy(scrap[u][:, 0:1], colv[:, 0:1])
                for jj in range(GT):
                    last = act.activation(act_g[u][:, jj * D:(jj + 1) * D], tile_of(src, it, u, jj), ACT.Square,
                                          scale=float(D) ** -0.5, accum_out=ss[u][:, jj:jj + 1])
                last.then_inc(done, 1)

            for l in range(L):
                if l > 0:
                    act.wait_ge(r2_ready, l * IT * NU)
                with act.Fori(0, IT) as it:
                    for u in range(NU):
                        if l == 0:
                            squares(R, it, u, q_ss[l], q_r[l], u, NU)
                        else:
                            squares(R, it, u, q_ss[l])
                    for u in range(NU):
                        need(act, q_tr[l], it, u)
                        act.activation(yT[u][:, :], banks[4 * u][:, :], ACT.Copy,
                                       scale=colv[:, C_N1 + l:C_N1 + l + 1]).then_inc(q_hT[l], 1)
                    for u in range(NU):
                        for jj in range(GT):
                            need(act, q_proj[l], it, u * GT + jj, per=NU * GT)
                            act.activation(qkv[u][:, jj, :], banks[4 * u + jj][:, 0:3 * D], ACT.Silu)
                            last = act.activation(th[u][:, jj, :], banks[4 * u + jj][:, 3 * D:QKVB], ACT.Tanh,
                                                  scale=0.5)
                        last.then_inc(q_silu[l], 1)

                act.wait_ge(st_init[l], 1)
                for a in range(NA):
                    act.wait_ge(scan_in[l][a], 16 * HH)
                    with act.Fori(a * T // NA // NST, (a + 1) * T // NA // NST) as it:
                        for k in range(2):
                            need(act, st_ready[l], it, k, per=2)
                            copy(scrap[k][:, 0:1], colv[:, 0:1])
                            ps = PS[:, bass.ds(it * NST + k * HS, HS), :].rearrange(
                                "p t (g s e) -> p (t g) s e", g=H2, s=4)
                            copy(kb_now[k][:, :, 0:DK], ps[:, :, 2, :])
                            copy(k_now[k], ps[:, :, 1, :])
                            first = (k * HS - 1) % NST
                            if k == 0:
                                copy(St[first][:, :, :, DK], ps[:, 0:H2, 3, :], -1.0)
                                copy(ring[:, 0:HS - 1, :, :, DK].rearrange("p i g v -> p (i g) v"),
                                     ps[:, H2:, 3, :], -1.0).then_inc(st_fed[l], 1)
                            else:
                                copy(ring[:, first:first + HS, :, :, DK].rearrange("p i g v -> p (i g) v"),
                                     ps[:, :, 3, :], -1.0).then_inc(st_fed[l], 1)

                with act.Fori(0, IT) as it:
                    for u in range(NU):
                        need(act, o_tr[l], it, u)
                        act.activation(yT[u][:, :], banks[4 * u][:, :], ACT.Copy,
                                       scale=colv[:, C_ON + l:C_ON + l + 1]).then_inc(o_oT[l], 1)
                    for u in range(NU):
                        squares(R, it, u, m_ss[l], r1_ready[l], u, NU)
                    for u in range(NU):
                        need(act, m_tr[l], it, u)
                        act.activation(yT[u][:, :], banks[4 * u][:, :], ACT.Copy,
                                       scale=colv[:, C_N2 + l:C_N2 + l + 1]).then_inc(m_hT[l], 1)
                    for c, (f0, fn) in enumerate(IC):
                        for u in range(NU):
                            need(act, m_gu[l], it, c * NU + u, per=3 * NU)
                            if c > 0:
                                need(act, m_a[l], it, (c - 1) * NU + u, per=3 * NU)
                            bg = (1, 3, 1)[c]
                            act.activation(act_g[u][0:fn, :], banks[4 * u + bg][0:fn, :],
                                           ACT.Silu).then_inc(m_silu[l], 1)
                    if l == L - 1:
                        for u in range(NU):
                            squares(R, it, u, f_ss, r2_ready, u + IT * NU * (L - 1), NU)

            for u in range(NU):
                copy(scrap2[u][:, 0:1], colv[:, 0:1]).then_inc(out_done[u], 16)
            with act.Fori(0, IT) as it:
                for u in range(NU):
                    need(act, e_tr, it, u)
                    copy(yT[u][:, :], banks[4 * u][:, :]).then_inc(e_hT, 1)
                for u in range(NU):
                    need(act, e_log, it, u)
                    act.activation(sg[u][:, :, :].rearrange("p j e -> p (j e)"), banks[4 * u + 1][:, 0:GT * E],
                                   ACT.Sigmoid).then_inc(e_sig, 1)
                for u in range(NU):
                    need(act, e_ctr, it, u)
                    copy(cf[u][:, :], banks[4 * u + 2][0:E, :]).then_inc(e_cf, 1)
                for u in range(NU):
                    need(act, e_c3, it, u)
                    copy(c3[u][E:2 * E, :], cmid[u][:, :]).then_inc(e_mid, 1)
                for p in range(-1, NPAIR):
                    for u in range(NU):
                        n = (p + 1) * NU + u
                        need(act, x_gate, it, n, per=(NPAIR + 1) * NU)
                        if p == 0:
                            need(act, x_a, it, n - NU, per=(NPAIR + 1) * NU)
                        if p > 0:
                            need(act, x_gu, it, n - 2 * NU, per=NPAIR * NU)
                        act.activation(act_g[u][:, :], banks[4 * u][:, :], ACT.Silu).then_inc(x_silu, 1)
                for u in range(NU):
                    need(act, x_down, it, NPAIR * NU + u, per=(NPAIR + 1) * NU)
                    need(act, out_done[u], it * 16, 15, per=1)
                    copy(r[u][:, :, :].rearrange("p j c -> p (j c)"), banks[4 * u + 3][:, :]).then_inc(e_acc, 1)

        @block.gpsimd
        def _(pool):
            pool.memset(neg_half[:, :], -0.5)
            pool.memset(eps_ln[:, :], EPS_LN)
            pool.memset(eps_rms[:, :], EPS_RMS).then_inc(consts_made, 1)
            pool.wait_ge(consts_made, 1)
            pool.wait_ge(const_in, N_CONST)

            def rsqrt(st, u, src, n, eps, done):
                v = ve[u][:, 0:n]
                st.after(pool.tensor_tensor(v, src, eps[:, 0:n], ALU.add))
                pool.tensor_tensor(rstd[u][:, 0:n], v, neg_half[:, 0:n], ALU.pow).then_inc(done, 1)

            def affine(u, g, b, st, done):
                g_ = bc(rowv[:, g:g + 1, :], [P, GT, D])
                b_ = bc(rowv[:, b:b + 1, :], [P, GT, D])
                st.after(pool.tensor_tensor(r[u][:, :, :], yn[u][:, :, :], g_, ALU.mult))
                pool.tensor_tensor(y[u][:, :, :], r[u][:, :, :], b_, ALU.add).then_inc(done, 1)

            with pool.Fori(0, IT) as it:
                st = Steps(pool, pool_steps)
                for k in range(4):
                    for u in range(NU):
                        need(pool, a_var, it, k * NU + u, per=4 * NU)
                        rsqrt(st, u, mv[u][:, :, 1], GT, eps_ln, a_rstd)
                    if k == 0:
                        continue
                    for u in range(NU):
                        need(pool, a_norm, it, (k - 1) * NU + u, per=3 * NU)
                        g, b = ((G1, BE1), (G2, BE2), (G3, BE3))[k - 1]
                        affine(u, g, b, st, a_scaled)
                        if k == 2:
                            need(pool, a_scaled, it, NU * (k - 1) + u, per=3 * NU)
                            pool.tensor_tensor(r[u][:, :, :], y[u][:, :, :],
                                               bc(rowv[:, B2:B2 + 1, :], [P, GT, D]), ALU.add).then_inc(ff_res, 1)
                st.end()

            for l in range(L):
                with pool.Fori(0, IT) as it:
                    st = Steps(pool, pool_steps)
                    if l == 0:
                        for u in range(NU):
                            need(pool, d_var, it, u)
                            rsqrt(st, u, mv[u][:, :, 1], GT, eps_ln, d_rstd)
                    for u in range(NU):
                        need(pool, q_ss[l], it, u)
                        rsqrt(st, u, ss[u][:, 0:GT], GT, eps_rms, q_rr[l])
                    for u in range(NU):
                        need(pool, q_qk[l], it, u)
                        pk = PK[:, bass.ds(it * (NU * GT) + u * GT, GT), :].rearrange(
                            "p j (h t e) -> p (j h) t e", h=H, t=4)
                        b_ = bc(beta[u][:, :, :].rearrange("p j h -> p (j h)").unsqueeze(2), [P, GT * H, DK])
                        st.after(pool.tensor_tensor(pk[:, :, 2, :], pk[:, :, 1, :], b_, ALU.mult))
                        v4 = qkv[u][:, :, 2 * D:3 * D].rearrange("p j (h e) -> p j h e", h=H)
                        b4 = bc(beta[u][:, :, :].unsqueeze(3), [P, GT, H, DK])
                        pk4 = PK[:, bass.ds(it * (NU * GT) + u * GT, GT), :].rearrange(
                            "p j (h t e) -> p j h t e", h=H, t=4)
                        pool.tensor_tensor(pk4[:, :, :, 3, :], v4, b4, ALU.mult).then_inc(q_pk[l], 1)
                    st.end()

                pool.memset(oprod, 0.0).then_inc(st_free[l], 2)
                for a in range(NA):
                    pool.wait_ge(scan_in[l][a], 16 * HH)
                    with pool.Fori(a * T // NA // NST, (a + 1) * T // NA // NST) as it:
                        st = Steps(pool, pool_steps)
                        for k in range(2):
                            need(pool, st_ready[l], it, k + 2, per=2)
                            q_t = PS[:, bass.ds(it * NST + k * HS, HS), :].rearrange(
                                "p t (g s e) -> p (t g) s e", g=H2, s=4)[:, :, 0:1, :]
                            states = mid[:, k * HS * SW:(k + 1) * HS * SW].rearrange(
                                "p (c v k) -> p c v k", v=DK, k=DK + 1)[:, :, :, 0:DK]
                            pool.tensor_tensor(oprod, states, bc(q_t, [P, HS * H2, DK, DK]),
                                               ALU.mult).then_inc(st_free[l], 1)
                            need(pool, st_free[l], it, k + 2, per=2)
                            st.after(pool.tensor_tensor(osum8, oprod[:, :, :, 0:8], oprod[:, :, :, 8:16], ALU.add))
                            st.after(pool.tensor_tensor(osum4, osum8[:, :, :, 0:4], osum8[:, :, :, 4:8], ALU.add))
                            st.after(pool.tensor_tensor(osum2, osum4[:, :, :, 0:2], osum4[:, :, :, 2:4], ALU.add))
                            o_t = Os[:, bass.ds(it * (NST * 32) + k * (HS * 32), HS * 32)].rearrange(
                                "p (g v) -> p g v", v=DK)
                            pool.tensor_tensor(o_t, osum2[:, :, :, 0], osum2[:, :, :, 1], ALU.add).then_inc(o_ready[l], 1)
                        st.end()

                with pool.Fori(0, IT) as it:
                    st = Steps(pool, pool_steps)
                    for u in range(NU):
                        need(pool, m_ss[l], it, u)
                        rsqrt(st, u, ss[u][:, 0:GT], GT, eps_rms, m_rr[l])
                    if l == L - 1:
                        for u in range(NU):
                            need(pool, f_ss, it, u)
                            rsqrt(st, u, ss[u][:, 0:GT], GT, eps_rms, f_rr)
                        for u in range(NU):
                            need(pool, f_n, it, u)
                            pool.tensor_tensor(y[u][:, :, :], yn[u][:, :, :],
                                               bc(rowv[:, FINALW:FINALW + 1, :], [P, GT, D]),
                                               ALU.mult).then_inc(f_w, 1)
                    st.end()

            with pool.Fori(0, IT) as it:
                st = Steps(pool, pool_steps)
                for u in range(NU):
                    need(pool, e_var, it, u)
                    rsqrt(st, u, mv[u][:, :, 1], GT, eps_ln, e_rstd)
                st.end()

        @block.vector
        def _(dve):
            def stats(st, src, u, done):
                for jj in range(GT):
                    last = dve.bn_stats(stat[u][:, jj, :], src(jj))
                st.after(last)
                for jj in range(GT):
                    last = dve.bn_aggr(mv[u][:, jj, :], stat[u][:, jj, :])
                last.then_inc(done, 1)

            def normed(src, dst, u):
                for jj in range(GT):
                    last = dve.tensor_scalar(dst(jj), src(jj), mv[u][:, jj, 0:1], rstd[u][:, jj:jj + 1],
                                             ALU.subtract, ALU.mult)
                return last

            def scaled(src, dst, u):
                for jj in range(GT):
                    last = dve.tensor_scalar(dst(jj), src(jj), rstd[u][:, jj:jj + 1], None, ALU.mult)
                return last

            def head_rsqrt(st, u, n):
                v, g, w = ve[u][:, 0:n], rstdh[u][:, 0:n], ssh[u][:, 0:n]
                st.after(dve.tensor_scalar(v, w, EPS_RMS, None, ALU.add))
                st.after(dve.tensor_scalar(g.bitcast(I32), v.bitcast(I32), -0.5, RSQRT_MAGIC, ALU.mult, ALU.add))
                for _ in range(3):
                    st.after(dve.tensor_tensor(w, g, v, ALU.mult))
                    st.after(dve.scalar_tensor_tensor(out=w, in0=w, scalar=-0.5, in1=g, op0=ALU.mult, op1=ALU.mult))
                    st.after(dve.scalar_tensor_tensor(out=g, in0=w, scalar=1.5, in1=g, op0=ALU.add, op1=ALU.mult))

            dve.wait_ge(x_in, 16)
            dve.wait_ge(const_in, N_CONST)
            with dve.Fori(0, IT) as it:
                st = Steps(dve, dve_steps)
                X_ = [lambda jj, u=u: tile_of(X, it, u, jj) for u in range(NU)]
                y_ = [lambda jj, u=u: y[u][:, jj, :] for u in range(NU)]
                yn_ = [lambda jj, u=u: yn[u][:, jj, :] for u in range(NU)]
                r_ = [lambda jj, u=u: r[u][:, jj, :] for u in range(NU)]
                for u in range(NU):
                    stats(st, X_[u], u, a_var)
                for u in range(NU):
                    need(dve, a_rstd, it, u, per=4 * NU)
                    normed(X_[u], y_[u], u).then_inc(a_y, 1)
                for u in range(NU):
                    need(dve, sa_scores, it, u)
                    s_ps = banks[6 + u][:, 0:GT * S].rearrange("p (j k) -> p j k", j=GT)
                    st.after(dve.tensor_tensor(s1[u][:, :, :], s_ps, bc(causal[:, :].unsqueeze(1), [P, GT, S]), ALU.add))
                    st.after(dve.tensor_reduce(mx[u][:, :], s1[u][:, :, :], AX.X, ALU.max))
                    dve.tensor_tensor(s1[u][:, :, :], s1[u][:, :, :], bc(mx[u][:, :].unsqueeze(2), [P, GT, S]),
                                      ALU.subtract).then_inc(sa_shift, 1)
                for u in range(NU):
                    need(dve, sa_exp, it, u)
                    dve.transpose(p1T[u][:, :, :].rearrange("p j k -> p (j k)"),
                                  p1[u][:, :, :].rearrange("p j k -> p (j k)")).then_inc(sa_pT, 1)
                    st.after(dve.tensor_reduce(rs1[u][:, :], p1[u][:, :, :], AX.X, ALU.add))
                    st.after(dve.reciprocal(ri1[u][:, :], rs1[u][:, :]))
                for u in range(NU):
                    need(dve, sa_out, it, u)
                    for jj in range(GT):
                        last = dve.scalar_tensor_tensor(out=r[u][:, jj, :], in0=banks[6 + u][:, jj * D:(jj + 1) * D],
                                                        scalar=ri1[u][:, jj:jj + 1], in1=y[u][:, jj, :],
                                                        op0=ALU.mult, op1=ALU.add)
                    st.after(last)
                    stats(st, r_[u], u, a_var)
                for u in range(NU):
                    need(dve, a_rstd, it, NU + u, per=4 * NU)
                    normed(r_[u], yn_[u], u).then_inc(a_norm, 1)

                def row_max(n):
                    need(dve, ca_scores, it, n, per=NT)
                    dve.tensor_reduce(nmax[:, n:n + 1], banks[n % 2][:, 0:KEYS], AX.X, ALU.max,
                                      negate=True).then_inc(ca_max, 1)

                def keep_turned(n):
                    need(dve, ca_tr, it, n, per=NT)
                    dve.tensor_copy(pcT[:, n, :], banks[2 + n % 2][:, 0:2 * P]).then_inc(ca_pT, 1)

                def cross_residual(u):
                    st.after(dve.reciprocal(rinv[:, u * GT:(u + 1) * GT], rsum[:, u * GT:(u + 1) * GT]))
                    need(dve, ca_out, it, u * GT + GT - 1, per=NT)
                    need(dve, a_scaled, it, u, per=3 * NU)
                    for jj in range(GT):
                        n = u * GT + jj
                        last = dve.scalar_tensor_tensor(out=yn[u][:, jj, :], in0=tile_of(zlast, it, u, jj),
                                                        scalar=pc[:, n, KEYS - 1:KEYS],
                                                        in1=banks[4 + u][:, jj * D:(jj + 1) * D],
                                                        op0=ALU.mult, op1=ALU.add)
                    st.after(last)
                    for jj in range(GT):
                        n = u * GT + jj
                        last = dve.scalar_tensor_tensor(out=r[u][:, jj, :], in0=yn[u][:, jj, :],
                                                        scalar=rinv[:, n:n + 1], in1=y[u][:, jj, :],
                                                        op0=ALU.mult, op1=ALU.add)
                    st.after(last)
                    stats(st, r_[u], u, a_var)

                dve.wait_ge(zlast_in, 16 * NA)
                for n in range(NT + 1):
                    if n < NT:
                        row_max(n)
                    if n >= 1:
                        keep_turned(n - 1)
                    if n == GT + 1:
                        cross_residual(0)
                cross_residual(1)
                for u in range(NU):
                    need(dve, a_rstd, it, 2 * NU + u, per=4 * NU)
                    normed(r_[u], yn_[u], u).then_inc(a_norm, 1)
                for u in range(NU):
                    need(dve, ff_out, it, u)
                    need(dve, ff_res, it, u)
                    st.after(dve.tensor_tensor(yn[u][:, :, :], banks[4 + u][:, :].rearrange("p (j c) -> p j c", j=GT),
                                               r[u][:, :, :], ALU.add))
                    stats(st, yn_[u], u, a_var)
                for u in range(NU):
                    need(dve, a_rstd, it, 3 * NU + u, per=4 * NU)
                    normed(yn_[u], yn_[u], u).then_inc(a_norm, 1)
                for u in range(NU):
                    need(dve, a_scaled, it, 2 * NU + u, per=3 * NU)
                    st.after(dve.tensor_tensor(group_of(X, it, u), group_of(X, it, u),
                                               y[u][:, :, :].rearrange("p j c -> p (j c)"), ALU.add))
                st.end()

            for l in range(L):
                with dve.Fori(0, IT) as it:
                    R_ = [lambda jj, u=u: tile_of(R, it, u, jj) for u in range(NU)]
                    X_ = [lambda jj, u=u: tile_of(X, it, u, jj) for u in range(NU)]
                    yn_ = [lambda jj, u=u: yn[u][:, jj, :] for u in range(NU)]
                    st = Steps(dve, dve_steps)
                    if l == 0:
                        for u in range(NU):
                            stats(st, X_[u], u, d_var)
                        for u in range(NU):
                            need(dve, d_rstd, it, u)
                            normed(X_[u], R_[u], u).then_inc(q_r[l], 1)
                    for u in range(NU):
                        if l == 0:
                            need(dve, q_r[l], it, u)
                        need(dve, q_rr[l], it, u)
                        scaled(R_[u], yn_[u], u).then_inc(q_h[l], 1)
                    for u in range(NU):
                        need(dve, q_silu[l], it, u)
                        st.after(dve.tensor_scalar(beta[u][:, :, :], th[u][:, :, :], 1.0, None, ALU.add))
                        st.after(dve.tensor_tensor(sq[u][:, :, :], qkv[u][:, :, 0:2 * D], qkv[u][:, :, 0:2 * D], ALU.mult))
                        st.after(dve.tensor_reduce(ssh[u][:, 0:GT * 2 * H],
                                                   sq[u][:, :, :].rearrange("p j (h e) -> p (j h) e", e=DK),
                                                   AX.X, ALU.add))
                        head_rsqrt(st, u, GT * 2 * H)
                        pk4 = PK[:, bass.ds(it * (NU * GT) + u * GT, GT), :].rearrange(
                            "p j (h t e) -> p j h t e", h=H, t=4)
                        rn = rstdh[u][:, 0:GT * 2 * H].rearrange("p (j h) -> p j h", j=GT)
                        for i in range(2):
                            q4 = qkv[u][:, :, i * D:(i + 1) * D].rearrange("p j (h e) -> p j h e", h=H)
                            last = dve.tensor_tensor(pk4[:, :, :, i, :], q4,
                                                     bc(rn[:, :, i * H:(i + 1) * H].unsqueeze(3), [P, GT, H, DK]), ALU.mult)
                            if i == 0:
                                st.after(last)
                        last.then_inc(q_qk[l], 1)
                    st.end()

                dve.wait_ge(st_free[l], 2)
                dve.memset(kb_now[0][:, :, DK:DK + 1], 1.0)
                dve.memset(kb_now[1][:, :, DK:DK + 1], 1.0).then_inc(st_ready[l], 2)
                dve.memset(St[NST - 1][:, :, :, 0:DK], 0.0).then_inc(st_init[l], 1)
                dve.wait_ge(st_init[l], 1)
                with dve.Fori(0, T // NST) as it:
                    st = Steps(dve, dve_steps)
                    for i in range(NST):
                        k, n = divmod(i, HS)
                        old, new = St[(i - 1) % NST], St[i]
                        if n == 0:
                            need(dve, st_ready[l], it, k + 1, per=2)
                            need(dve, st_fed[l], it, k, per=2)
                        st.after(dve.tensor_tensor(prod, old, bc(kb_now[k][:, n * H2:(n + 1) * H2, :].unsqueeze(2),
                                                                 [P, H2, DK, DK + 1]), ALU.mult))
                        st.after(dve.tensor_reduce(negu, prod, AX.X, ALU.add))
                        st.after(dve.tensor_tensor(outer, bc(k_now[k][:, n * H2:(n + 1) * H2, :].unsqueeze(2),
                                                             [P, H2, DK, DK]),
                                                   bc(negu.unsqueeze(3), [P, H2, DK, DK]), ALU.mult))
                        if n == 0:
                            need(dve, st_free[l], it, k, per=2)
                        add = dve.tensor_tensor(new[:, :, :, 0:DK], old[:, :, :, 0:DK], outer, ALU.subtract)
                        if n < HS - 1:
                            st.after(add)
                        else:
                            add.then_inc(st_ready[l], 1)
                    st.end()

                dve.wait_ge(o_home[l], 16 * NA * HH)
                with dve.Fori(0, IT) as it:
                    R_ = [lambda jj, u=u: tile_of(R, it, u, jj) for u in range(NU)]
                    yn_ = [lambda jj, u=u: yn[u][:, jj, :] for u in range(NU)]
                    st = Steps(dve, dve_steps)
                    for u in range(NU):
                        o_g = group_of(O, it, u)
                        st.after(dve.scalar_tensor_tensor(out=sq[u][:, 0:2, :].rearrange("p j c -> p (j c)"), in0=o_g,
                                                          scalar=1.0 / DK, in1=o_g, op0=ALU.mult, op1=ALU.mult))
                        st.after(dve.tensor_reduce(ssh[u][:, 0:GT * H],
                                                   sq[u][:, 0:2, :].rearrange("p j c -> p (j c)").rearrange(
                                                       "p (h e) -> p h e", e=DK), AX.X, ALU.add))
                        head_rsqrt(st, u, GT * H)
                        dve.tensor_tensor(yn[u][:, :, :].rearrange("p j (h e) -> p (j h) e", e=DK),
                                          group_of(O, it, u).rearrange("p (h e) -> p h e", e=DK),
                                          bc(rstdh[u][:, 0:GT * H].unsqueeze(2), [P, GT * H, DK]),
                                          ALU.mult).then_inc(o_n[l], 1)
                    for u in range(NU):
                        need(dve, o_wo[l], it, u)
                        dve.tensor_tensor(group_of(R, it, u), banks[4 * u + 1][:, :], group_of(R, it, u),
                                          ALU.add).then_inc(r1_ready[l], 1)
                    for u in range(NU):
                        need(dve, r1_ready[l], it, u)
                        need(dve, m_rr[l], it, u)
                        scaled(R_[u], yn_[u], u).then_inc(m_h[l], 1)
                    for c, (f0, fn) in enumerate(IC):
                        for u in range(NU):
                            need(dve, m_silu[l], it, c * NU + u, per=3 * NU)
                            by = (2, 0, 2)[c]
                            dve.tensor_tensor(hT[u][0:fn, c, :], banks[4 * u + by][0:fn, :], act_g[u][0:fn, :],
                                              ALU.mult).then_inc(m_a[l], 1)
                    for u in range(NU):
                        need(dve, m_out[l], it, u)
                        dve.tensor_tensor(group_of(R, it, u), banks[4 * u + 3][:, :], group_of(R, it, u),
                                          ALU.add).then_inc(r2_ready, 1)
                    if l == L - 1:
                        for u in range(NU):
                            dve.wait_ge(r2_ready, it * NU + (IT * NU * (L - 1) + u + 1))
                            need(dve, f_rr, it, u)
                            scaled(R_[u], yn_[u], u).then_inc(f_n, 1)
                        for u in range(NU):
                            need(dve, f_w, it, u)
                            st.after(dve.tensor_tensor(group_of(X, it, u), group_of(X, it, u),
                                                       y[u][:, :, :].rearrange("p j c -> p (j c)"), ALU.add))
                    st.end()

            with dve.Fori(0, IT) as it:
                X_ = [lambda jj, u=u: tile_of(X, it, u, jj) for u in range(NU)]
                yn_ = [lambda jj, u=u: yn[u][:, jj, :] for u in range(NU)]
                st = Steps(dve, dve_steps)
                for u in range(NU):
                    stats(st, X_[u], u, e_var)
                for u in range(NU):
                    need(dve, e_rstd, it, u)
                    normed(X_[u], yn_[u], u).then_inc(e_h, 1)
                for u in range(NU):
                    need(dve, e_sig, it, u)
                    tt = dve.tensor_tensor
                    st.after(tt(sc[u][:, :, :], sg[u][:, :, :], bc(gbias[:, :].unsqueeze(1), [P, GT, E]), ALU.add))
                    pair = sc[u][:, :, :].rearrange("p j (g c k) -> p (j g) c k", g=NGRP, c=2)
                    tt(pmx[u][:, :, :], pair[:, :, :, 0], pair[:, :, :, 1], ALU.max)
                    st.after(tt(pmn[u][:, :, :], pair[:, :, :, 0], pair[:, :, :, 1], ALU.min))
                    tt(gs[u][:, 0, :], pmx[u][:, :, 0], pmx[u][:, :, 1], ALU.max)
                    tt(gs[u][:, 1, :], pmx[u][:, :, 0], pmx[u][:, :, 1], ALU.min)
                    st.after(tt(gs[u][:, 2, :], pmn[u][:, :, 0], pmn[u][:, :, 1], ALU.max))
                    st.after(tt(gs[u][:, 3, :], gs[u][:, 1, :], gs[u][:, 2, :], ALU.max))
                    st.after(tt(gs[u][:, 1, :], gs[u][:, 0, :], gs[u][:, 3, :], ALU.add))
                    for jj in range(GT):
                        mine = bc(gs[u][:, 1, jj * NGRP:(jj + 1) * NGRP].unsqueeze(2), [P, NGRP, NGRP])
                        other = bc(gs[u][:, 1, jj * NGRP:(jj + 1) * NGRP].unsqueeze(1), [P, NGRP, NGRP])
                        tt(cmp1[u][:, jj * NGRP:(jj + 1) * NGRP, :], other, mine, ALU.is_gt)
                        last = tt(cmp2[u][:, jj * NGRP:(jj + 1) * NGRP, :], other, mine, ALU.is_equal)
                    st.after(last)
                    c1 = cmp1[u][:, :, :].rearrange("p (j g) o -> p j (g o)", j=GT)
                    c2 = cmp2[u][:, :, :].rearrange("p (j g) o -> p j (g o)", j=GT)
                    st.after(tt(c2, c2, bc(before[:, :].unsqueeze(1), [P, GT, NGRP * NGRP]), ALU.mult))
                    st.after(tt(c1, c1, c2, ALU.add))
                    st.after(dve.tensor_reduce(gs[u][:, 2, :], cmp1[u][:, :, :],
                                               AX.X, ALU.add))
                    st.after(dve.tensor_scalar(gmask[u][:, :], gs[u][:, 2, :], TOPG - 0.5, None, ALU.is_lt))
                    four = msk[u][:, :, :].rearrange("p j (g k) -> p (j g) k", g=NGRP)
                    st.after(tt(four, sc[u][:, :, :].rearrange("p j (g k) -> p (j g) k", g=NGRP),
                                bc(gmask[u][:, :].unsqueeze(2), [P, GT * NGRP, E // NGRP]), ALU.mult))
                    st.after(dve.tensor_scalar(msk[u][:, :, :], msk[u][:, :, :], 0.0, None, ALU.add))
                    for jj in range(GT):
                        last = dve.max(top8[u][:, jj, :], msk[u][:, jj, :])
                    st.after(last)
                    for jj in range(GT):
                        last = dve.match_replace(rep[u][:, jj, :], top8[u][:, jj, :], msk[u][:, jj, :], REPLACED)
                    st.after(last)
                    st.after(tt(rep[u][:, :, :], rep[u][:, :, :], msk[u][:, :, :], ALU.not_equal))
                    st.after(tt(rep[u][:, :, :], rep[u][:, :, :], sg[u][:, :, :], ALU.mult))
                    st.after(dve.tensor_reduce(den[u][:, :], rep[u][:, :, :], AX.X, ALU.add))
                    st.after(dve.tensor_scalar(den[u][:, :], den[u][:, :], 1e-20, None, ALU.add))
                    st.after(dve.reciprocal(mx[u][:, :], den[u][:, :]))
                    st.after(dve.tensor_scalar(mx[u][:, :], mx[u][:, :], ROUTE_SCALE, None, ALU.mult))
                    tt(comb[u][:, :, :], rep[u][:, :, :], bc(mx[u][:, :].unsqueeze(2), [P, GT, E]),
                       ALU.mult).then_inc(e_comb, 1)
                for u in range(NU):
                    need(dve, e_cf, it, u)
                    st.after(dve.tensor_copy(c3[u][0:E, :], cf[u][:, :]))
                    st.after(dve.tensor_tensor(cf[u][:, :], cf[u][:, :], c3[u][0:E, :], ALU.subtract))
                    st.after(dve.tensor_copy(cmid[u][:, :], cf[u][:, :]))
                    dve.tensor_tensor(c3[u][2 * E:3 * E, :], cf[u][:, :], cmid[u][:, :], ALU.subtract).then_inc(e_c3, 1)
                for p in range(-1, NPAIR):
                    for u in range(NU):
                        n = (p + 1) * NU + u
                        need(dve, x_silu, it, n, per=(NPAIR + 1) * NU)
                        if n >= NU:
                            need(dve, x_down, it, n - NU, per=(NPAIR + 1) * NU)
                        dst = act_a[u] if p < 0 else act_gu[u]
                        dve.tensor_tensor(dst[:, :], banks[4 * u + 1][:, :], act_g[u][:, :],
                                          ALU.mult).then_inc(x_a if p < 0 else x_gu, 1)
                        if p >= 0:
                            need(dve, x_gu, it, n - NU, per=NPAIR * NU)
                            dve.tensor_tensor(act_a[u][:, :], banks[4 * u + 2][:, :], act_gu[u][:, :],
                                              ALU.mult).then_inc(x_a, 1)
                for u in range(NU):
                    need(dve, e_otr, it, u)
                    dve.tensor_tensor(r[u][:, :, :].rearrange("p j c -> p (j c)"), banks[4 * u][:, :],
                                      group_of(X, it, u), ALU.add).then_inc(e_xo, 1)
                st.end()


def _layout(inputs):
    import numpy as np

    a = {k: np.asarray(v) for k, v in inputs.items()}

    def tr(w):
        return np.ascontiguousarray(w.T)

    def chunks(w, n):
        return w.reshape(n, P, -1).transpose(1, 0, 2)

    ctx = a["ctx_1024"].reshape(NA, NJ, KEYS, D)
    o = {}
    o["x"] = a["x"].reshape(NA, NJ, S, D).transpose(0, 2, 1, 3).reshape(P, NJ * D)
    o["ctx_t"] = ctx.transpose(1, 3, 0, 2).reshape(NJ, D, NA * KEYS)
    o["ctx_z"] = ctx[:, :, :KEYS - 1].reshape(NA, NJ, 2, P, D).transpose(1, 3, 2, 0, 4).reshape(NJ, P, 2 * NA * D)
    o["ctx_last"] = ctx[:, :, KEYS - 1].reshape(NA, NJ * D)
    o["rows"] = np.stack([a["L0_xattn_g1"], a["L0_xattn_beta1"], a["L0_xattn_g2"], a["L0_xattn_beta2"],
                          a["L0_xattn_g3"], a["L0_xattn_beta3"], a["L0_xattn_b2"], a["L0_attn_final_norm_w"]])
    o["cols"] = np.concatenate([a["L0_attn_norm1_w"].T, a["L0_attn_norm2_w"].T,
                                np.concatenate([a["L0_attn_onorm_w"].T] * H, axis=0),
                                a["L0_xattn_b1"].reshape(FFC, P).T,
                                np.stack([a["L0_xattn_g1"], a["L0_xattn_beta1"],
                                          a["L0_xattn_g2"], a["L0_xattn_beta2"]], axis=1)], axis=1)
    o["w1"] = a["L0_xattn_w1"]
    o["w2"] = chunks(a["L0_xattn_w2"], FFC)
    o["wqkvb"] = np.concatenate([a["L0_attn_Wq"], a["L0_attn_Wk"], a["L0_attn_Wv"], a["L0_attn_Wb"]],
                                axis=2).transpose(1, 0, 2)
    o["wo"] = a["L0_attn_Wo"].transpose(1, 0, 2)
    o["wgu"] = a["L0_attn_Wg"].transpose(1, 0, 2)
    wd = np.zeros((L, 3 * P, D), a["L0_attn_Wd"].dtype)
    wd[:, :INTER] = a["L0_attn_Wd"]
    o["wd"] = wd.reshape(L, 3, P, D).transpose(2, 0, 1, 3)
    o["gate_t"] = tr(a["L0_ffn_gate_w"])
    o["gate_bias"] = a["L0_ffn_gate_bias"].reshape(1, E)
    o["we_gate"] = tr(a["L0_ffn_w_gate"].reshape(E * EI, D)).reshape(D, NPAIR, P)
    o["we_up"] = tr(a["L0_ffn_w_up"].reshape(E * EI, D)).reshape(D, NPAIR, P)
    o["we_down"] = chunks(a["L0_ffn_w_down"].transpose(0, 2, 1).reshape(E * EI, D), NPAIR)
    o["sh_gate"] = tr(a["L0_ffn_sh_gate"])
    o["sh_up"] = tr(a["L0_ffn_sh_up"])
    o["sh_down"] = tr(a["L0_ffn_sh_down"])
    o["ident"] = np.eye(P, dtype=np.float32)
    q, k = np.arange(P)[:, None] % S, np.arange(S)[None, :]
    o["causal"] = np.where(k <= q, 0.0, NEG).astype(np.float32)
    spread = np.zeros((3, E, NPAIR, 2, EI), np.uint16)
    for e in range(E):
        spread[:, e, e // 2, e % 2, :] = 0x3F80
    o["spread"] = spread.reshape(3 * E, NPAIR * P)
    g = np.arange(NGRP)
    before = (g[None, :] < g[:, None]).astype(np.float32).reshape(1, NGRP * NGRP)
    o["before"] = np.repeat(before, P, axis=0)
    return {k_: np.ascontiguousarray(v) for k_, v in o.items()}


_ORDER = ["x", "ctx_t", "ctx_z", "ctx_last", "rows", "cols", "w1", "w2", "wqkvb", "wo", "wgu", "wd", "gate_t",
          "gate_bias", "we_gate", "we_up", "we_down", "sh_gate", "sh_up", "sh_down", "ident", "causal", "spread",
          "before"]


def kernel(**inputs):
    import numpy as _np
    import concourse.bacc as _bacc
    from concourse import mybir as _mybir
    from concourse.bass_utils import run_bass_kernel_spmd as _run

    nc = _bacc.Bacc("TRN2", target_bir_lowering=False, num_devices=1)
    laid = _layout(inputs)
    arrays, args = {}, []
    for name in _ORDER:
        arr = laid[name]
        arrays[f"in_{name}"] = arr
        args.append(nc.dram_tensor(f"in_{name}", arr.shape, _mybir.dt.from_np(arr.dtype), kind="ExternalInput").ap())
    args.append(nc.dram_tensor("out_0", (P, NJ * D), _mybir.dt.float32, kind="ExternalOutput").ap())
    perceiver(nc, *args)
    res = _run(nc, [arrays], core_ids=[0])
    got = _np.asarray(res.results[0]["out_0"])
    return _np.ascontiguousarray(got.reshape(NA, S, NJ, D).transpose(0, 2, 1, 3).reshape(NA * NJ, S, D))
```

```python
from contextlib import ExitStack

import concourse.bass as bass
from concourse import mybir

F32 = mybir.dt.float32
I32 = mybir.dt.int32
BF16 = mybir.dt.bfloat16
ALU = mybir.AluOpType
ACT = mybir.ActivationFunctionType
AX = mybir.AxisListType

P = 128
D = 128
NJ = 16
GT = 4
GW = GT * D
NU = 2
IT = NJ // (GT * NU)
NA, S = 4, 32
KEYS = 257
FFC = 4
L = 2
H, DK = 8, 16
HH, H2 = 4, 2
T = 64
QKVB = 3 * D + H
INTER = 352
IC = [(0, 128), (128, 128), (256, 96)]
E = 32
EI = 64
NPAIR = E // 2
NGRP = 8
TOPG = 4
SCALE_ATT = float(D) ** -0.5
EPS_LN, EPS_RMS = 1e-5, 1e-6
NEG = -1e30
RSQRT_MAGIC = float(0x5F3759DF)
REPLACED = -3e38
ROUTE_SCALE = 2.5

G1, BE1, G2, BE2, G3, BE3, B2, FINALW = range(8)
C_N1, C_N2, C_ON, C_B1 = 0, L, 2 * L, 3 * L
C_G1, C_G2 = 3 * L + FFC, 3 * L + FFC + 2


class Steps:

    def __init__(self, eng, sem):
        self.eng, self.sem, self.n = eng, sem, 0

    def counted(self, ins):
        ins.then_inc(self.sem, 1)
        self.n += 1
        return self.n

    def reached(self, n):
        self.eng.wait_ge(self.sem, n)

    def after(self, ins):
        self.reached(self.counted(ins))

    def end(self):
        self.eng.sem_clear(self.sem)


def need(eng, sem, it, k, per=NU):
    eng.wait_ge(sem, it * per + (k + 1))


def perceiver(nc, x, ctx_t, ctx_z, ctx_last, rows, cols, w1, w2, wqkvb, wo, wgu, wd, gate_t, gate_bias,
              we_gate, we_up, we_down, sh_gate, sh_up, sh_down, ident_in, causal_in, spread_in, before_in, out):
    with ExitStack() as stack:
        def sb(name, shape, dt=F32):
            return stack.enter_context(nc.sbuf_tensor(name, shape, dt))

        def sem(name):
            return stack.enter_context(nc.semaphore(name))

        banks = [stack.enter_context(nc.psum_tensor(f"bank{i}", [P, 512], F32)) for i in range(8)]

        ident = sb("ident", [P, P])
        causal = sb("causal", [P, S])
        spread = sb("spread", [96, NPAIR * P], BF16)
        before = sb("before", [P, NGRP * NGRP])
        rowv = sb("rowv", [P, 8, D])
        colv = sb("colv", [P, 3 * L + FFC + 4])
        gb1s = sb("gb1s", [P, 2])
        gbias = sb("gbias", [P, E])
        w1_sb = sb("w1_sb", [P, FFC * P])
        w2_sb = sb("w2_sb", [P, FFC, D])
        wqkvb_sb = sb("wqkvb_sb", [P, L, QKVB])
        wo_sb = sb("wo_sb", [P, L, D])
        wgu_sb = sb("wgu_sb", [P, L, 2 * INTER])
        wd_sb = sb("wd_sb", [P, L, 3, D])
        gate_sb = sb("gate_sb", [P, E])
        weg_sb = sb("weg_sb", [P, NPAIR + 1, P])
        weu_sb = sb("weu_sb", [P, NPAIR + 1, P])
        wed_sb = sb("wed_sb", [P, NPAIR + 1, D])
        neg_half, eps_ln, eps_rms = sb("neg_half", [P, 64]), sb("eps_ln", [P, 64]), sb("eps_rms", [P, 64])

        X = sb("X", [P, NJ * D])
        R = sb("R", [P, NJ * D])
        zlast = sb("zlast", [P, NJ * D])
        NRING = 8
        arena = sb("arena", [P, NRING * (NA * KEYS + 2 * NA * D)])
        zt_ring = arena[:, 0:NRING * NA * KEYS].rearrange("p (n c) -> p n c", n=NRING)
        z_ring = arena[:, NRING * NA * KEYS:].rearrange("p (n c) -> p n c", n=NRING)
        PKW = H * 4 * DK
        PK = arena[:, 0:NJ * PKW].rearrange("p (n c) -> p n c", n=NJ)
        PS = arena[:, NJ * PKW:NJ * PKW + T * D].rearrange("p (t c) -> p t c", t=T)
        Os = sb("Os", [P, T * 32])
        O = zlast

        yr = [sb(f"yr{u}", [P, 2 * GT, D]) for u in range(NU)]
        y = [yr[u][:, 0:GT, :] for u in range(NU)]
        yn = [sb(f"yn{u}", [P, GT, D]) for u in range(NU)]
        r = [yr[u][:, GT:2 * GT, :] for u in range(NU)]
        yT = [sb(f"yT{u}", [P, GW]) for u in range(NU)]
        NST, HS = 8, 4
        SW = H2 * DK * (DK + 1)
        mid = sb("mid", [P, NST * SW])
        hT = [mid[:, u * FFC * GW:(u + 1) * FFC * GW].rearrange("p (c n) -> p c n", c=FFC) for u in range(NU)]
        stat = [sb(f"stat{u}", [P, GT, 6]) for u in range(NU)]
        mv = [sb(f"mv{u}", [P, GT, 2]) for u in range(NU)]
        ve = [sb(f"ve{u}", [P, 64]) for u in range(NU)]
        rstd = [sb(f"rstd{u}", [P, 64]) for u in range(NU)]
        ss = [sb(f"ss{u}", [P, GT]) for u in range(NU)]
        ssh = [sb(f"ssh{u}", [P, 64]) for u in range(NU)]
        rstdh = [sb(f"rstdh{u}", [P, 64]) for u in range(NU)]
        s1 = [sb(f"s1{u}", [P, GT, S]) for u in range(NU)]
        p1 = [sb(f"p1{u}", [P, GT, S]) for u in range(NU)]
        p1T = [sb(f"p1T{u}", [P, GT, S]) for u in range(NU)]
        mx = [sb(f"mx{u}", [P, GT]) for u in range(NU)]
        rs1 = [sb(f"rs1{u}", [P, GT]) for u in range(NU)]
        ri1 = [sb(f"ri1{u}", [P, GT]) for u in range(NU)]
        NT = NU * GT
        nmax = sb("nmax", [P, NT])
        rsum = sb("rsum", [P, NT])
        rinv = sb("rinv", [P, NT])
        pc = sb("pc", [P, NT, KEYS])
        pcT = sb("pcT", [P, NT, 2 * P])
        qkv = [pc[:, 0:6, :].rearrange("p n c -> p (n c)")[:, 0:GT * 3 * D].rearrange("p (j c) -> p j c", j=GT),
               pcT[:, 0:6, :].rearrange("p n c -> p (n c)").rearrange("p (j c) -> p j c", j=GT)]
        sq = [yr[u][:, :, :].rearrange("p (j i) c -> p j (i c)", j=GT) for u in range(NU)]
        th = [sb(f"th{u}", [P, GT, H]) for u in range(NU)]
        beta = [sb(f"beta{u}", [P, GT, H]) for u in range(NU)]
        act_o = sb("act_o", [P, 2 * GW])
        def carve(flat):
            at = [0]

            def take(shape, parts=P, dt=F32):
                n = 1
                for d in shape:
                    n *= d
                words = n if dt is F32 else n // 2
                piece = flat[0:parts, at[0]:at[0] + words]
                at[0] += words
                if dt is not F32:
                    piece = piece.bitcast(dt)
                if len(shape) == 1:
                    return piece
                names = "abc"[:len(shape)]
                return piece.rearrange(f"p ({' '.join(names)}) -> p {' '.join(names)}",
                                       **{k: v for k, v in zip(names, shape)})
            return take

        ring = mid[:, :].rearrange("p (i g v k) -> p i g v k", i=NST, g=H2, v=DK)
        St = [ring[:, i] for i in range(NST)]
        states = [mid[:, k * HS * SW:(k + 1) * HS * SW].rearrange(
            "p (c v k) -> p c v k", v=DK, k=DK + 1)[:, :, :, 0:DK] for k in range(2)]
        take = carve(pc[:, :, :].rearrange("p n c -> p (n c)"))
        oprod = take((HS * H2, DK, DK))
        take = carve(pcT[:, :, :].rearrange("p n c -> p (n c)"))
        prod, outer = take((H2 * DK, DK + 1)), take((H2 * DK, DK))
        prod = prod.rearrange("p (g v) k -> p g v k", g=H2)
        outer = outer.rearrange("p (g v) k -> p g v k", g=H2)
        negu = take((H2, DK))
        kb_now = [take((HS * H2, DK + 1)) for k in range(2)]
        k_now = [take((HS * H2, DK)) for k in range(2)]
        osum2 = take((HS * H2, DK, 2))
        osum4 = carve(yT[0][:, :])((HS * H2, DK, 4))
        osum8 = carve(act_o[:, :])((HS * H2, DK, 8))
        take = carve(pc[:, :, :].rearrange("p n c -> p (n c)"))
        sg = take((NT, E))
        sc, msk, rep, comb = take((NT, E)), take((NT, E)), take((NT, E)), take((NT, E))
        gs = take((4, NT * NGRP))
        gmask = take((NT * NGRP,))
        pmx, pmn = take((NT * NGRP, 2)), take((NT * NGRP, 2))
        top8 = take((NT, 8))
        den, share = take((NT,)), take((NT,))
        take = carve(pcT[:, :, :].rearrange("p n c -> p (n c)"))
        cmp1, cmp2 = take((NT * NGRP, NGRP)), take((NT * NGRP, NGRP))
        take = carve(arena[:, :])
        cf = [take((GW,), E) for u in range(NU)]
        c3 = [take((GW,), 3 * E, BF16) for u in range(NU)]
        cmid = [take((GW,), E, BF16) for u in range(NU)]
        act_g = [act_o[:, u * GW:(u + 1) * GW] for u in range(NU)]
        scrap = [sb(f"scrap{u}", [P, 1]) for u in range(NU)]
        scrap2 = [sb(f"scrap2{u}", [P, 1]) for u in range(NU)]
        act_gu = [hT[u][:, 0, :] for u in range(NU)]
        act_a = [hT[u][:, 1, :] for u in range(NU)]

        x_in, const_in, zlast_in, w_in = sem("x_in"), sem("const_in"), sem("zlast_in"), sem("w_in")
        ring_in = [sem(f"ring_in{i}") for i in range(NRING)]
        consts_made, gb1s_made = sem("consts_made"), sem("gb1s_made")
        dve_steps, pool_steps = sem("dve_steps"), sem("pool_steps")
        a_var, a_rstd, a_norm, a_scaled = sem("a_var"), sem("a_rstd"), sem("a_norm"), sem("a_scaled")
        a_y, a_tr, a_yT = sem("a_y"), sem("a_tr"), sem("a_yT")
        sa_scores, sa_shift, sa_exp, sa_pT, sa_out = (sem("sa_scores"), sem("sa_shift"), sem("sa_exp"),
                                                      sem("sa_pT"), sem("sa_out"))
        ca_scores, ca_max, ca_exp, ca_tr, ca_pT, ca_out = (sem("ca_scores"), sem("ca_max"), sem("ca_exp"),
                                                           sem("ca_tr"), sem("ca_pT"), sem("ca_out"))
        ff_up, ff_h, ff_out, ff_res = sem("ff_up"), sem("ff_h"), sem("ff_out"), sem("ff_res")
        def lsem(name):
            return [sem(f"{name}_{l}") for l in range(L)]
        d_var, d_rstd = sem("d_var"), sem("d_rstd")
        q_r, q_ss, q_rr, q_h, q_tr, q_hT, q_proj, q_silu, q_sq, q_beta, q_k, q_qk, q_pk = map(lsem, (
            "q_r", "q_ss", "q_rr", "q_h", "q_tr", "q_hT", "q_proj", "q_silu", "q_sq", "q_beta", "q_k", "q_qk",
            "q_pk"))
        scan_in = [[sem(f"scan_in_{l}_{a}") for a in range(NA)] for l in range(L)]
        st_init, st_fed = map(lsem, ("st_init", "st_fed"))
        st_ready, st_free, o_ready, o_home = map(lsem, ("st_ready", "st_free", "o_ready", "o_home"))
        o_n, o_tr, o_oT, o_wo, r1_ready, m_ss, m_rr, m_h, m_tr, m_hT, m_gu, m_silu, m_a, m_out = map(
            lsem, ("o_n", "o_tr", "o_oT", "o_wo", "r1_ready", "m_ss", "m_rr", "m_h", "m_tr",
                   "m_hT", "m_gu", "m_silu", "m_a", "m_out"))
        r2_ready, f_ss, f_rr, f_n, f_w = sem("r2_ready"), sem("f_ss"), sem("f_rr"), sem("f_n"), sem("f_w")
        e_var, e_rstd, e_h, e_tr, e_hT, e_log, e_sig, e_comb, e_ctr, e_c3, e_mid, e_cf = (
            sem("e_var"), sem("e_rstd"), sem("e_h"), sem("e_tr"), sem("e_hT"), sem("e_log"), sem("e_sig"),
            sem("e_comb"), sem("e_ctr"), sem("e_c3"), sem("e_mid"), sem("e_cf"))
        x_gate, x_silu, x_gu, x_a, x_down = sem("x_gate"), sem("x_silu"), sem("x_gu"), sem("x_a"), sem("x_down")
        e_acc, e_otr, e_xo = sem("e_acc"), sem("e_otr"), sem("e_xo")
        out_done = [sem(f"out_done{u}") for u in range(NU)]

        consts = [(ident, ident_in), (causal, causal_in), (before, before_in),
                  (colv, cols)]
        N_CONST = 16 * (len(consts) + 1 + 1)
        weights = [(w1_sb, w1), (w2_sb, w2), (spread[:, :].bitcast(mybir.dt.uint16), spread_in), (wqkvb_sb, wqkvb), (wo_sb, wo), (wgu_sb, wgu), (wd_sb, wd),
                   (gate_sb, gate_t), (weg_sb, we_gate), (weu_sb, we_up), (wed_sb, we_down)]
        shared = [(weg_sb, sh_gate), (weu_sb, sh_up), (wed_sb, sh_down)]
        N_WEIGHT = 16 * (len(weights) + len(shared))

        def whole(t):
            if isinstance(t, bass.AP):
                return t
            return t[:, :] if len(t.shape) == 2 else t[:, :, :] if len(t.shape) == 3 else t[:, :, :, :]

        def tile_of(t, it, u, jj):
            return t[:, bass.ds(it * (NU * GW) + (u * GW + jj * D), D)]

        def group_of(t, it, u):
            return t[:, bass.ds(it * (NU * GW) + u * GW, GW)]

        def bc(ap, shape):
            return ap.to_broadcast(shape)

        block = stack.enter_context(nc.Block())

        @block.sync
        def _(sp):
            sp.dma_start(X[:, :], x).then_inc(x_in, 16)
            for dst, src in consts:
                sp.dma_start(whole(dst), src).then_inc(const_in, 16)
            sp.dma_start(rowv[:, :, :].rearrange("p i c -> p (i c)"), rows.partition_broadcast(P)).then_inc(const_in, 16)
            sp.dma_start(gbias[:, :], gate_bias.partition_broadcast(P)).then_inc(const_in, 16)

            def load_ctx(half):
                for n in range(NRING):
                    if half > 0:
                        sp.wait_ge(ca_out, (half - 1) * NT + n + 1)
                    sp.dma_start(zt_ring[:, n, :], ctx_t[half * NRING + n]).then_inc(ring_in[n], 16)
                    sp.dma_start(z_ring[:, n, :], ctx_z[half * NRING + n]).then_inc(ring_in[n], 16)

            load_ctx(0)
            for a in range(NA):
                sp.dma_start(zlast[S * a:S * a + S, :],
                             ctx_last[a:a + 1, :].partition_broadcast(S)).then_inc(zlast_in, 16)
            for dst, src in weights:
                d = dst[:, 0:NPAIR, :] if dst is weg_sb or dst is weu_sb or dst is wed_sb else whole(dst)
                sp.dma_start(d, src).then_inc(w_in, 16)
            for dst, src in shared:
                sp.dma_start(dst[:, NPAIR, :], src).then_inc(w_in, 16)
            load_ctx(1)

            for l in range(L):
                sp.wait_ge(q_pk[l], IT * NU)
                sp.wait_ge(q_qk[l], IT * NU)
                for a in range(NA):
                    for hh in range(HH):
                        sp.dma_start(PS[S * hh:S * hh + S, NJ * a:NJ * a + NJ, :],
                                     PK[S * a:S * a + S, :, D * hh:D * hh + D]).then_inc(scan_in[l][a], 16)
                for a in range(NA):
                    sp.wait_ge(o_ready[l], NJ // HS * (a + 1))
                    for hh in range(HH):
                        sp.dma_start(O[S * a:S * a + S, :].rearrange("p (j c) -> p j c", j=NJ)[:, :, 32 * hh:32 * hh + 32],
                                     Os[S * hh:S * hh + S, 32 * NJ * a:32 * NJ * (a + 1)]
                                     .rearrange("p (j c) -> p j c", j=NJ)).then_inc(o_home[l], 16)

            with sp.Fori(0, IT) as it:
                for u in range(NU):
                    need(sp, e_xo, it, u)
                    sp.dma_start(out[:, bass.ds(it * (NU * GW) + u * GW, GW)],
                                 r[u][:, :, :].rearrange("p j c -> p (j c)")).then_inc(out_done[u], 16)
            for u in range(NU):
                sp.wait_ge(out_done[u], 16 * (IT + 1))

        @block.tensor
        def _(pe):
            def transposes(bank, src, u, ready):
                for jj in range(GT):
                    last = pe.transpose(bank[:, jj * D:(jj + 1) * D], src[u][:, jj, :], ident[:, :])
                last.then_inc(ready, 1)

            pe.wait_ge(const_in, N_CONST)

            with pe.Fori(0, IT) as it:
                for u in range(NU):
                    need(pe, a_y, it, u)
                    transposes(banks[6 + u], y, u, a_tr)
                for u in range(NU):
                    need(pe, a_yT, it, u, per=3 * NU)
                    for jj in range(GT):
                        for a in range(NA):
                            q = yT[u][:, jj * D + a * S:jj * D + a * S + S]
                            last = pe.matmul(banks[6 + u][a * S:a * S + S, jj * S:jj * S + S], q, q,
                                             start=True, stop=True)
                    last.then_inc(sa_scores, 1)
                for u in range(NU):
                    pe.wait_ge(sa_pT, u + 1)
                    for jj in range(GT):
                        for a in range(NA):
                            rows_ = slice(a * S, a * S + S)
                            last = pe.matmul(banks[6 + u][rows_, jj * D:(jj + 1) * D], p1T[u][rows_, jj, :],
                                             y[u][rows_, jj, :], start=True, stop=True)
                    last.then_inc(sa_out, 1)
                pe.sem_clear(sa_pT)
                for u in range(NU):
                    need(pe, a_norm, it, u, per=2 * NU)
                    transposes(banks[6 + u], yn, u, a_tr)

                def scores(n):
                    u, jj = divmod(n, GT)
                    need(pe, a_yT, it, NU + u, per=3 * NU)
                    pe.wait_ge(ring_in[n], 32 * it + 32)
                    for a in range(NA):
                        last = pe.matmul(banks[n % 2][a * S:a * S + S, 0:KEYS],
                                         yT[u][:, jj * D + a * S:jj * D + a * S + S],
                                         zt_ring[:, n, a * KEYS:(a + 1) * KEYS], start=True, stop=True)
                    last.then_inc(ca_scores, 1)

                def turn(n):
                    need(pe, ca_exp, it, n, per=NT)
                    for c in range(2):
                        last = pe.transpose(banks[2 + n % 2][:, c * P:(c + 1) * P], pc[:, n, c * P:(c + 1) * P],
                                            ident[:, :])
                    last.then_inc(ca_tr, 1)

                def attend(n):
                    u, jj = divmod(n, GT)
                    need(pe, ca_pT, it, n, per=NT)
                    for a in range(NA):
                        for c in range(2):
                            last = pe.matmul(banks[4 + u][a * S:a * S + S, jj * D:(jj + 1) * D],
                                             pcT[:, n, c * P + a * S:c * P + a * S + S],
                                             z_ring[:, n, (c * NA + a) * D:(c * NA + a + 1) * D],
                                             start=(c == 0), stop=(c == 1))
                    last.then_inc(ca_out, 1)

                for n in range(NT + 2):
                    if n < NT:
                        scores(n)
                    if 1 <= n <= NT:
                        turn(n - 1)
                    if n >= 2:
                        attend(n - 2)
                for u in range(NU):
                    need(pe, a_norm, it, NU + u, per=2 * NU)
                    transposes(banks[6 + u], yn, u, a_tr)
                pe.wait_ge(w_in, N_WEIGHT)
                for u in range(NU):
                    need(pe, a_yT, it, 2 * NU + u, per=3 * NU)
                    for c in range(FFC):
                        if c >= 2:
                            need(pe, ff_h, it, u * FFC + c - 2, per=NU * FFC)
                        pe.matmul(banks[2 * u + c % 2][:, :], w1_sb[:, c * P:(c + 1) * P], yT[u][:, :],
                                  start=True, stop=True).then_inc(ff_up, 1)
                for u in range(NU):
                    need(pe, ff_h, it, u * FFC + FFC - 1, per=NU * FFC)
                    for jj in range(GT):
                        for c in range(FFC):
                            last = pe.matmul(banks[4 + u][:, jj * D:(jj + 1) * D], hT[u][:, c, jj * D:(jj + 1) * D],
                                             w2_sb[:, c, :], start=(c == 0), stop=(c == FFC - 1))
                    last.then_inc(ff_out, 1)

            for l in range(L):
                with pe.Fori(0, IT) as it:
                    for u in range(NU):
                        need(pe, q_h[l], it, u)
                        transposes(banks[4 * u], yn, u, q_tr[l])
                    for u in range(NU):
                        need(pe, q_hT[l], it, u)
                        for jj in range(GT):
                            pe.matmul(banks[4 * u + jj][:, 0:QKVB], yT[u][:, jj * D:(jj + 1) * D],
                                      wqkvb_sb[:, l, :], start=True, stop=True).then_inc(q_proj[l], 1)

                with pe.Fori(0, IT) as it:
                    for u in range(NU):
                        need(pe, o_n[l], it, u)
                        transposes(banks[4 * u], yn, u, o_tr[l])
                    for u in range(NU):
                        need(pe, o_oT[l], it, u)
                        for jj in range(GT):
                            last = pe.matmul(banks[4 * u + 1][:, jj * D:(jj + 1) * D], yT[u][:, jj * D:(jj + 1) * D],
                                             wo_sb[:, l, :], start=True, stop=True)
                        last.then_inc(o_wo[l], 1)
                    for u in range(NU):
                        need(pe, m_h[l], it, u)
                        transposes(banks[4 * u], yn, u, m_tr[l])
                    for c, (f0, fn) in enumerate(IC):
                        for u in range(NU):
                            need(pe, m_hT[l], it, u)
                            if c == 2:
                                need(pe, m_a[l], it, u, per=3 * NU)
                            bg, by = ((1, 2), (3, 0), (1, 2))[c]
                            pe.matmul(banks[4 * u + bg][0:fn, :], wgu_sb[:, l, f0:f0 + fn], yT[u][:, :],
                                      start=True, stop=True)
                            pe.matmul(banks[4 * u + by][0:fn, :], wgu_sb[:, l, INTER + f0:INTER + f0 + fn],
                                      yT[u][:, :], start=True, stop=True).then_inc(m_gu[l], 1)
                    for u in range(NU):
                        need(pe, m_a[l], it, 2 * NU + u, per=3 * NU)
                        for jj in range(GT):
                            for c, (f0, fn) in enumerate(IC):
                                last = pe.matmul(banks[4 * u + 3][:, jj * D:(jj + 1) * D],
                                                 hT[u][0:fn, c, jj * D:(jj + 1) * D], wd_sb[0:fn, l, c, :],
                                                 start=(c == 0), stop=(c == 2))
                        last.then_inc(m_out[l], 1)

            with pe.Fori(0, IT) as it:
                for u in range(NU):
                    need(pe, e_h, it, u)
                    transposes(banks[4 * u], yn, u, e_tr)
                for u in range(NU):
                    need(pe, e_hT, it, u)
                    for jj in range(GT):
                        last = pe.matmul(banks[4 * u + 1][:, jj * E:(jj + 1) * E], yT[u][:, jj * D:(jj + 1) * D],
                                         gate_sb[:, :], start=True, stop=True)
                    last.then_inc(e_log, 1)

                def gate_up(p, u):
                    n = (p + 1) * NU + u
                    if n >= NU:
                        need(pe, x_a, it, n - NU, per=(NPAIR + 1) * NU)
                    w = p % (NPAIR + 1)
                    pe.matmul(banks[4 * u][:, :], weg_sb[:, w, :], yT[u][:, :], start=True, stop=True)
                    last = pe.matmul(banks[4 * u + 1][:, :], weu_sb[:, w, :], yT[u][:, :], start=True, stop=True)
                    if p >= 0:
                        last = pe.matmul(banks[4 * u + 2][:, :], spread[:, p * P:(p + 1) * P], c3[u][:, :],
                                         start=True, stop=True)
                    last.then_inc(x_gate, 1)

                def down(p, u):
                    n = (p + 1) * NU + u
                    need(pe, x_a, it, n, per=(NPAIR + 1) * NU)
                    pe.matmul(banks[4 * u + 3][:, :], wed_sb[:, p % (NPAIR + 1), :], act_a[u][:, :],
                              start=(p == -1), stop=(p == NPAIR - 1), skip_group_check=True).then_inc(x_down, 1)

                for u in range(NU):
                    need(pe, e_sig, it, u)
                    gate_up(-1, u)
                for u in range(NU):
                    down(-1, u)
                for u in range(NU):
                    need(pe, e_comb, it, u)
                    for jj in range(GT):
                        last = pe.transpose(banks[4 * u + 2][0:E, jj * D:(jj + 1) * D], comb[:, u * GT + jj, :], ident[:, :])
                    last.then_inc(e_ctr, 1)
                order = [(p, u) for p in range(NPAIR) for u in range(NU)]
                for n in range(len(order) + NU):
                    if n < len(order):
                        if n < NU:
                            need(pe, e_c3, it, n)
                            need(pe, e_mid, it, n)
                        gate_up(*order[n])
                    if n >= NU:
                        down(*order[n - NU])
                for u in range(NU):
                    need(pe, e_acc, it, u)
                    for jj in range(GT):
                        last = pe.transpose(banks[4 * u][:, jj * D:(jj + 1) * D], r[u][:, jj, :], ident[:, :])
                    last.then_inc(e_otr, 1)

        @block.scalar
        def _(act):
            def copy(out_, in_, scale=1.0):
                return act.activation(out_, in_, ACT.Copy, scale=scale)

            act.wait_ge(const_in, N_CONST)
            copy(gb1s[:, :], colv[:, C_G1:C_G1 + 2], SCALE_ATT).then_inc(gb1s_made, 1)
            act.wait_ge(gb1s_made, 1)
            with act.Fori(0, IT) as it:
                for u in range(NU):
                    need(act, a_tr, it, u, per=3 * NU)
                    copy(yT[u][:, :], banks[6 + u][:, :]).then_inc(a_yT, 1)
                for u in range(NU):
                    need(act, sa_shift, it, u)
                    act.activation(p1[u][:, :, :], s1[u][:, :, :], ACT.Exp, scale=SCALE_ATT).then_inc(sa_exp, 1)
                for u in range(NU):
                    need(act, a_tr, it, NU + u, per=3 * NU)
                    act.activation(yT[u][:, :], banks[6 + u][:, :], ACT.Identity, bias=gb1s[:, 1:2],
                                   scale=gb1s[:, 0:1]).then_inc(a_yT, 1)
                for n in range(NT):
                    need(act, ca_max, it, n, per=NT)
                    act.activation(pc[:, n, :], banks[n % 2][:, 0:KEYS], ACT.Exp, bias=nmax[:, n:n + 1],
                                   accum_out=rsum[:, n:n + 1]).then_inc(ca_exp, 1)
                for u in range(NU):
                    need(act, a_tr, it, 2 * NU + u, per=3 * NU)
                    act.activation(yT[u][:, :], banks[6 + u][:, :], ACT.Identity, bias=colv[:, C_G2 + 1:C_G2 + 2],
                                   scale=colv[:, C_G2:C_G2 + 1]).then_inc(a_yT, 1)
                for u in range(NU):
                    for c in range(FFC):
                        need(act, ff_up, it, u * FFC + c, per=NU * FFC)
                        act.activation(hT[u][:, c, :], banks[2 * u + c % 2][:, :], ACT.Relu,
                                       bias=colv[:, C_B1 + c:C_B1 + c + 1]).then_inc(ff_h, 1)

            def squares(src, it, u, done, sem_in=None, k=0, per=NU):
                if sem_in is not None:
                    need(act, sem_in, it, k, per=per)
                    copy(scrap[u][:, 0:1], colv[:, 0:1])
                for jj in range(GT):
                    last = act.activation(act_g[u][:, jj * D:(jj + 1) * D], tile_of(src, it, u, jj), ACT.Square,
                                          scale=float(D) ** -0.5, accum_out=ss[u][:, jj:jj + 1])
                last.then_inc(done, 1)

            for l in range(L):
                if l > 0:
                    act.wait_ge(r2_ready, l * IT * NU)
                with act.Fori(0, IT) as it:
                    for u in range(NU):
                        if l == 0:
                            squares(R, it, u, q_ss[l], q_r[l], u, NU)
                        else:
                            squares(R, it, u, q_ss[l])
                    for u in range(NU):
                        need(act, q_tr[l], it, u)
                        act.activation(yT[u][:, :], banks[4 * u][:, :], ACT.Copy,
                                       scale=colv[:, C_N1 + l:C_N1 + l + 1]).then_inc(q_hT[l], 1)
                    for u in range(NU):
                        for jj in range(GT):
                            need(act, q_proj[l], it, u * GT + jj, per=NU * GT)
                            act.activation(qkv[u][:, jj, :], banks[4 * u + jj][:, 0:3 * D], ACT.Silu)
                            last = act.activation(th[u][:, jj, :], banks[4 * u + jj][:, 3 * D:QKVB], ACT.Tanh,
                                                  scale=0.5)
                        last.then_inc(q_silu[l], 1)
                    need(act, q_silu[l], it, NU - 1)
                    act.activation(sq[NU - 1][:, :, :], qkv[NU - 1][:, :, 0:2 * D], ACT.Square).then_inc(q_sq[l], 1)

                act.wait_ge(st_init[l], 1)
                for a in range(NA):
                    act.wait_ge(scan_in[l][a], 16 * HH)
                    with act.Fori(a * T // NA // NST, (a + 1) * T // NA // NST) as it:
                        for k in range(2):
                            need(act, st_ready[l], it, k, per=2)
                            copy(scrap[k][:, 0:1], colv[:, 0:1])
                            ps = PS[:, bass.ds(it * NST + k * HS, HS), :].rearrange(
                                "p t (g s e) -> p (t g) s e", g=H2, s=4)
                            copy(kb_now[k][:, :, 0:DK], ps[:, :, 2, :])
                            copy(k_now[k], ps[:, :, 1, :])
                            first = (k * HS - 1) % NST
                            if k == 0:
                                copy(St[first][:, :, :, DK], ps[:, 0:H2, 3, :], -1.0)
                                copy(ring[:, 0:HS - 1, :, :, DK].rearrange("p i g v -> p (i g) v"),
                                     ps[:, H2:, 3, :], -1.0).then_inc(st_fed[l], 1)
                            else:
                                copy(ring[:, first:first + HS, :, :, DK].rearrange("p i g v -> p (i g) v"),
                                     ps[:, :, 3, :], -1.0).then_inc(st_fed[l], 1)

                with act.Fori(0, IT) as it:
                    for u in range(NU):
                        need(act, o_tr[l], it, u)
                        act.activation(yT[u][:, :], banks[4 * u][:, :], ACT.Copy,
                                       scale=colv[:, C_ON + l:C_ON + l + 1]).then_inc(o_oT[l], 1)
                    for u in range(NU):
                        squares(R, it, u, m_ss[l], r1_ready[l], u, NU)
                    for u in range(NU):
                        need(act, m_tr[l], it, u)
                        act.activation(yT[u][:, :], banks[4 * u][:, :], ACT.Copy,
                                       scale=colv[:, C_N2 + l:C_N2 + l + 1]).then_inc(m_hT[l], 1)
                    for c, (f0, fn) in enumerate(IC):
                        for u in range(NU):
                            need(act, m_gu[l], it, c * NU + u, per=3 * NU)
                            if c > 0:
                                need(act, m_a[l], it, (c - 1) * NU + u, per=3 * NU)
                            bg = (1, 3, 1)[c]
                            act.activation(act_g[u][0:fn, :], banks[4 * u + bg][0:fn, :],
                                           ACT.Silu).then_inc(m_silu[l], 1)
                    if l == L - 1:
                        for u in range(NU):
                            squares(R, it, u, f_ss, r2_ready, u + IT * NU * (L - 1), NU)

            for u in range(NU):
                copy(scrap2[u][:, 0:1], colv[:, 0:1]).then_inc(out_done[u], 16)
            with act.Fori(0, IT) as it:
                for u in range(NU):
                    need(act, e_tr, it, u)
                    copy(yT[u][:, :], banks[4 * u][:, :]).then_inc(e_hT, 1)
                for u in range(NU):
                    need(act, e_log, it, u)
                    act.activation(sg[:, u * GT:(u + 1) * GT, :].rearrange("p j e -> p (j e)"), banks[4 * u + 1][:, 0:GT * E],
                                   ACT.Sigmoid).then_inc(e_sig, 1)
                for u in range(NU):
                    need(act, x_gate, it, u, per=(NPAIR + 1) * NU)
                    act.activation(act_g[u][:, :], banks[4 * u][:, :], ACT.Silu).then_inc(x_silu, 1)
                for u in range(NU):
                    need(act, e_ctr, it, u)
                    copy(cf[u][:, :], banks[4 * u + 2][0:E, :]).then_inc(e_cf, 1)
                for u in range(NU):
                    need(act, e_c3, it, u)
                    copy(c3[u][E:2 * E, :], cmid[u][:, :]).then_inc(e_mid, 1)
                for p in range(NPAIR):
                    for u in range(NU):
                        n = (p + 1) * NU + u
                        need(act, x_gate, it, n, per=(NPAIR + 1) * NU)
                        if p == 0:
                            need(act, x_a, it, n - NU, per=(NPAIR + 1) * NU)
                        if p > 0:
                            need(act, x_gu, it, n - 2 * NU, per=NPAIR * NU)
                        act.activation(act_g[u][:, :], banks[4 * u][:, :], ACT.Silu).then_inc(x_silu, 1)
                for u in range(NU):
                    need(act, x_down, it, NPAIR * NU + u, per=(NPAIR + 1) * NU)
                    need(act, out_done[u], it * 16, 15, per=1)
                    copy(r[u][:, :, :].rearrange("p j c -> p (j c)"), banks[4 * u + 3][:, :]).then_inc(e_acc, 1)

        @block.gpsimd
        def _(pool):
            pool.memset(neg_half[:, :], -0.5)
            pool.memset(eps_ln[:, :], EPS_LN)
            pool.memset(eps_rms[:, :], EPS_RMS).then_inc(consts_made, 1)
            pool.wait_ge(consts_made, 1)
            pool.wait_ge(const_in, N_CONST)

            def rsqrt(st, u, src, n, eps, done):
                v = ve[u][:, 0:n]
                st.after(pool.tensor_tensor(v, src, eps[:, 0:n], ALU.add))
                pool.tensor_tensor(rstd[u][:, 0:n], v, neg_half[:, 0:n], ALU.pow).then_inc(done, 1)

            def affine(u, g, b, st, done):
                g_ = bc(rowv[:, g:g + 1, :], [P, GT, D])
                b_ = bc(rowv[:, b:b + 1, :], [P, GT, D])
                st.after(pool.tensor_tensor(r[u][:, :, :], yn[u][:, :, :], g_, ALU.mult))
                pool.tensor_tensor(y[u][:, :, :], r[u][:, :, :], b_, ALU.add).then_inc(done, 1)

            with pool.Fori(0, IT) as it:
                st = Steps(pool, pool_steps)
                for k in range(4):
                    for u in range(NU):
                        need(pool, a_var, it, k * NU + u, per=4 * NU)
                        rsqrt(st, u, mv[u][:, :, 1], GT, eps_ln, a_rstd)
                    if k == 0 or k == 3:
                        continue
                    for u in range(NU):
                        need(pool, a_norm, it, (k - 1) * NU + u, per=2 * NU)
                        g, b = ((G1, BE1), (G2, BE2))[k - 1]
                        affine(u, g, b, st, a_scaled)
                        if k == 2:
                            need(pool, a_scaled, it, NU * (k - 1) + u, per=3 * NU)
                            pool.tensor_tensor(r[u][:, :, :], y[u][:, :, :],
                                               bc(rowv[:, B2:B2 + 1, :], [P, GT, D]), ALU.add).then_inc(ff_res, 1)
                    if k == 2:
                        for u in range(NU):
                            x_g = group_of(X, it, u).rearrange("p (j c) -> p j c", j=GT)
                            pool.tensor_tensor(x_g, x_g, bc(rowv[:, BE3:BE3 + 1, :], [P, GT, D]),
                                               ALU.add).then_inc(a_scaled, 1)
                st.end()

            for l in range(L):
                with pool.Fori(0, IT) as it:
                    st = Steps(pool, pool_steps)
                    if l == 0:
                        for u in range(NU):
                            need(pool, d_var, it, u)
                            rsqrt(st, u, mv[u][:, :, 1], GT, eps_ln, d_rstd)
                    for u in range(NU):
                        need(pool, q_ss[l], it, u)
                        rsqrt(st, u, ss[u][:, 0:GT], GT, eps_rms, q_rr[l])
                    for u in range(NU):
                        need(pool, q_beta[l], it, u)
                        v4 = qkv[u][:, :, 2 * D:3 * D].rearrange("p j (h e) -> p j h e", h=H)
                        b4 = bc(beta[u][:, :, :].unsqueeze(3), [P, GT, H, DK])
                        pk4 = PK[:, bass.ds(it * (NU * GT) + u * GT, GT), :].rearrange(
                            "p j (h t e) -> p j h t e", h=H, t=4)
                        st.after(pool.tensor_tensor(pk4[:, :, :, 3, :], v4, b4, ALU.mult))
                    for u in range(NU):
                        need(pool, q_k[l], it, u)
                        pk = PK[:, bass.ds(it * (NU * GT) + u * GT, GT), :].rearrange(
                            "p j (h t e) -> p (j h) t e", h=H, t=4)
                        b_ = bc(beta[u][:, :, :].rearrange("p j h -> p (j h)").unsqueeze(2), [P, GT * H, DK])
                        pool.tensor_tensor(pk[:, :, 2, :], pk[:, :, 1, :], b_, ALU.mult).then_inc(q_pk[l], 1)
                    st.end()

                pool.wait_ge(q_qk[l], IT * NU)
                pool.memset(oprod[:, 0, 0, 0:1], 0.0).then_inc(st_free[l], 2)
                def outputs(st, it, k):
                    need(pool, st_ready[l], it, k + 2, per=2)
                    q_t = PS[:, bass.ds(it * NST + k * HS, HS), :].rearrange(
                        "p t (g s e) -> p (t g) s e", g=H2, s=4)[:, :, 0:1, :]
                    pool.tensor_tensor(oprod, states[k], bc(q_t, [P, HS * H2, DK, DK]),
                                       ALU.mult).then_inc(st_free[l], 1)
                    need(pool, st_free[l], it, k + 2, per=2)
                    st.after(pool.tensor_tensor(osum8, oprod[:, :, :, 0:8], oprod[:, :, :, 8:16], ALU.add))
                    st.after(pool.tensor_tensor(osum4, osum8[:, :, :, 0:4], osum8[:, :, :, 4:8], ALU.add))
                    st.after(pool.tensor_tensor(osum2, osum4[:, :, :, 0:2], osum4[:, :, :, 2:4], ALU.add))
                    o_t = Os[:, bass.ds(it * (NST * 32) + k * (HS * 32), HS * 32)].rearrange(
                        "p (g v) -> p g v", v=DK)
                    pool.tensor_tensor(o_t, osum2[:, :, :, 0], osum2[:, :, :, 1], ALU.add).then_inc(o_ready[l], 1)

                NTURN = T // NST
                for a in range(NA):
                    pool.wait_ge(scan_in[l][a], 16 * HH)
                    with pool.Fori(a * NTURN // NA, min((a + 1) * NTURN // NA, NTURN - 1)) as it:
                        st = Steps(pool, pool_steps)
                        for k in range(2):
                            outputs(st, it, k)
                        st.end()
                st = Steps(pool, pool_steps)
                outputs(st, NTURN - 1, 0)
                st.end()

                with pool.Fori(0, IT) as it:
                    st = Steps(pool, pool_steps)
                    for u in range(NU):
                        need(pool, m_ss[l], it, u)
                        rsqrt(st, u, ss[u][:, 0:GT], GT, eps_rms, m_rr[l])
                    if l == L - 1:
                        for u in range(NU):
                            need(pool, f_ss, it, u)
                            rsqrt(st, u, ss[u][:, 0:GT], GT, eps_rms, f_rr)
                        for u in range(NU):
                            need(pool, f_n, it, u)
                            pool.tensor_tensor(y[u][:, :, :], yn[u][:, :, :],
                                               bc(rowv[:, FINALW:FINALW + 1, :], [P, GT, D]),
                                               ALU.mult).then_inc(f_w, 1)
                    st.end()

            with pool.Fori(0, IT) as it:
                st = Steps(pool, pool_steps)
                for u in range(NU):
                    need(pool, e_var, it, u)
                    rsqrt(st, u, mv[u][:, :, 1], GT, eps_ln, e_rstd)
                st.end()

        @block.vector
        def _(dve):
            def stats(st, src, u, done):
                for jj in range(GT):
                    last = dve.bn_stats(stat[u][:, jj, :], src(jj))
                st.after(last)
                for jj in range(GT):
                    last = dve.bn_aggr(mv[u][:, jj, :], stat[u][:, jj, :])
                last.then_inc(done, 1)

            def normed(src, dst, u):
                for jj in range(GT):
                    last = dve.tensor_scalar(dst(jj), src(jj), mv[u][:, jj, 0:1], rstd[u][:, jj:jj + 1],
                                             ALU.subtract, ALU.mult)
                return last

            def scaled(src, dst, u):
                for jj in range(GT):
                    last = dve.tensor_scalar(dst(jj), src(jj), rstd[u][:, jj:jj + 1], None, ALU.mult)
                return last

            def head_rsqrt(st, n, done):
                v, g, w = ([t[:, 0:n] for t in buf] for buf in (ve, rstdh, ssh))

                def each(op):
                    for u in range(NU):
                        st.reached(done[u])
                        done[u] = st.counted(op(u))

                each(lambda u: dve.tensor_scalar(v[u], w[u], EPS_RMS, None, ALU.add))
                each(lambda u: dve.tensor_scalar(g[u].bitcast(I32), v[u].bitcast(I32), -0.5, RSQRT_MAGIC,
                                                 ALU.mult, ALU.add))
                for _ in range(3):
                    each(lambda u: dve.tensor_tensor(w[u], g[u], v[u], ALU.mult))
                    each(lambda u: dve.scalar_tensor_tensor(out=w[u], in0=w[u], scalar=-0.5, in1=g[u],
                                                            op0=ALU.mult, op1=ALU.mult))
                    each(lambda u: dve.scalar_tensor_tensor(out=g[u], in0=w[u], scalar=1.5, in1=g[u],
                                                            op0=ALU.add, op1=ALU.mult))

            dve.wait_ge(x_in, 16)
            dve.wait_ge(const_in, N_CONST)
            with dve.Fori(0, IT) as it:
                st = Steps(dve, dve_steps)
                X_ = [lambda jj, u=u: tile_of(X, it, u, jj) for u in range(NU)]
                y_ = [lambda jj, u=u: y[u][:, jj, :] for u in range(NU)]
                yn_ = [lambda jj, u=u: yn[u][:, jj, :] for u in range(NU)]
                r_ = [lambda jj, u=u: r[u][:, jj, :] for u in range(NU)]
                for u in range(NU):
                    stats(st, X_[u], u, a_var)
                for u in range(NU):
                    need(dve, a_rstd, it, u, per=4 * NU)
                    normed(X_[u], y_[u], u).then_inc(a_y, 1)
                for u in range(NU):
                    need(dve, sa_scores, it, u)
                    s_ps = banks[6 + u][:, 0:GT * S].rearrange("p (j k) -> p j k", j=GT)
                    st.after(dve.tensor_tensor(s1[u][:, :, :], s_ps, bc(causal[:, :].unsqueeze(1), [P, GT, S]), ALU.add))
                    st.after(dve.tensor_reduce(mx[u][:, :], s1[u][:, :, :], AX.X, ALU.max))
                    dve.tensor_tensor(s1[u][:, :, :], s1[u][:, :, :], bc(mx[u][:, :].unsqueeze(2), [P, GT, S]),
                                      ALU.subtract).then_inc(sa_shift, 1)
                for u in range(NU):
                    need(dve, sa_exp, it, u)
                    dve.transpose(p1T[u][:, :, :].rearrange("p j k -> p (j k)"),
                                  p1[u][:, :, :].rearrange("p j k -> p (j k)")).then_inc(sa_pT, 1)
                    st.after(dve.tensor_reduce(rs1[u][:, :], p1[u][:, :, :], AX.X, ALU.add))
                    st.after(dve.reciprocal(ri1[u][:, :], rs1[u][:, :]))
                for u in range(NU):
                    need(dve, sa_out, it, u)
                    for jj in range(GT):
                        last = dve.scalar_tensor_tensor(out=r[u][:, jj, :], in0=banks[6 + u][:, jj * D:(jj + 1) * D],
                                                        scalar=ri1[u][:, jj:jj + 1], in1=y[u][:, jj, :],
                                                        op0=ALU.mult, op1=ALU.add)
                    st.after(last)
                    stats(st, r_[u], u, a_var)
                for u in range(NU):
                    need(dve, a_rstd, it, NU + u, per=4 * NU)
                    normed(r_[u], yn_[u], u).then_inc(a_norm, 1)

                def row_max(n):
                    need(dve, ca_scores, it, n, per=NT)
                    dve.tensor_reduce(nmax[:, n:n + 1], banks[n % 2][:, 0:KEYS], AX.X, ALU.max,
                                      negate=True).then_inc(ca_max, 1)

                def keep_turned(n):
                    need(dve, ca_tr, it, n, per=NT)
                    dve.tensor_copy(pcT[:, n, :], banks[2 + n % 2][:, 0:2 * P]).then_inc(ca_pT, 1)

                def cross_residual(u):
                    st.after(dve.reciprocal(rinv[:, u * GT:(u + 1) * GT], rsum[:, u * GT:(u + 1) * GT]))
                    need(dve, ca_out, it, u * GT + GT - 1, per=NT)
                    need(dve, a_scaled, it, u, per=3 * NU)
                    for jj in range(GT):
                        n = u * GT + jj
                        last = dve.scalar_tensor_tensor(out=yn[u][:, jj, :], in0=tile_of(zlast, it, u, jj),
                                                        scalar=pc[:, n, KEYS - 1:KEYS],
                                                        in1=banks[4 + u][:, jj * D:(jj + 1) * D],
                                                        op0=ALU.mult, op1=ALU.add)
                    st.after(last)
                    for jj in range(GT):
                        n = u * GT + jj
                        last = dve.scalar_tensor_tensor(out=r[u][:, jj, :], in0=yn[u][:, jj, :],
                                                        scalar=rinv[:, n:n + 1], in1=y[u][:, jj, :],
                                                        op0=ALU.mult, op1=ALU.add)
                    st.after(last)
                    stats(st, r_[u], u, a_var)

                dve.wait_ge(zlast_in, 16 * NA)
                for n in range(NT + 1):
                    if n < NT:
                        row_max(n)
                    if n >= 1:
                        keep_turned(n - 1)
                    if n == GT + 1:
                        cross_residual(0)
                cross_residual(1)
                for u in range(NU):
                    need(dve, a_rstd, it, 2 * NU + u, per=4 * NU)
                    normed(r_[u], yn_[u], u).then_inc(a_norm, 1)
                for u in range(NU):
                    need(dve, ff_out, it, u)
                    need(dve, ff_res, it, u)
                    st.after(dve.tensor_tensor(yn[u][:, :, :], banks[4 + u][:, :].rearrange("p (j c) -> p j c", j=GT),
                                               r[u][:, :, :], ALU.add))
                    stats(st, yn_[u], u, a_var)
                done = [None] * NU
                for u in range(NU):
                    need(dve, a_rstd, it, 3 * NU + u, per=4 * NU)
                    done[u] = st.counted(normed(yn_[u], yn_[u], u))
                for u in range(NU):
                    st.reached(done[u])
                    done[u] = st.counted(dve.tensor_tensor(yn[u][:, :, :], yn[u][:, :, :],
                                                           bc(rowv[:, G3:G3 + 1, :], [P, GT, D]), ALU.mult))
                for u in range(NU):
                    need(dve, a_scaled, it, 2 * NU + u, per=3 * NU)
                    st.reached(done[u])
                    done[u] = st.counted(dve.tensor_tensor(group_of(X, it, u), group_of(X, it, u),
                                                           yn[u][:, :, :].rearrange("p j c -> p (j c)"), ALU.add))
                st.reached(done[NU - 1])
                st.end()

            for l in range(L):
                with dve.Fori(0, IT) as it:
                    R_ = [lambda jj, u=u: tile_of(R, it, u, jj) for u in range(NU)]
                    X_ = [lambda jj, u=u: tile_of(X, it, u, jj) for u in range(NU)]
                    yn_ = [lambda jj, u=u: yn[u][:, jj, :] for u in range(NU)]
                    st = Steps(dve, dve_steps)
                    if l == 0:
                        for u in range(NU):
                            stats(st, X_[u], u, d_var)
                        for u in range(NU):
                            need(dve, d_rstd, it, u)
                            normed(X_[u], R_[u], u).then_inc(q_r[l], 1)
                    for u in range(NU):
                        if l == 0:
                            need(dve, q_r[l], it, u)
                        need(dve, q_rr[l], it, u)
                        scaled(R_[u], yn_[u], u).then_inc(q_h[l], 1)
                    done = [None] * NU
                    for u in range(NU):
                        need(dve, q_silu[l], it, u)
                        dve.tensor_scalar(beta[u][:, :, :], th[u][:, :, :], 1.0, None, ALU.add).then_inc(q_beta[l], 1)
                        if u < NU - 1:
                            st.after(dve.tensor_tensor(sq[u][:, :, :], qkv[u][:, :, 0:2 * D], qkv[u][:, :, 0:2 * D],
                                                       ALU.mult))
                        else:
                            need(dve, q_sq[l], it, 0, per=1)
                        done[u] = st.counted(dve.tensor_reduce(ssh[u][:, 0:GT * 2 * H],
                                                               sq[u][:, :, :].rearrange("p j (h e) -> p (j h) e", e=DK),
                                                               AX.X, ALU.add))
                    head_rsqrt(st, GT * 2 * H, done)
                    for i, packed in ((1, q_k), (0, q_qk)):
                        for u in range(NU):
                            st.reached(done[u])
                            pk4 = PK[:, bass.ds(it * (NU * GT) + u * GT, GT), :].rearrange(
                                "p j (h t e) -> p j h t e", h=H, t=4)
                            rn = rstdh[u][:, 0:GT * 2 * H].rearrange("p (j h) -> p j h", j=GT)
                            q4 = qkv[u][:, :, i * D:(i + 1) * D].rearrange("p j (h e) -> p j h e", h=H)
                            dve.tensor_tensor(pk4[:, :, :, i, :], q4,
                                              bc(rn[:, :, i * H:(i + 1) * H].unsqueeze(3), [P, GT, H, DK]),
                                              ALU.mult).then_inc(packed[l], 1)
                    st.end()

                dve.wait_ge(st_free[l], 2)
                dve.memset(kb_now[0][:, :, DK:DK + 1], 1.0)
                dve.memset(kb_now[1][:, :, DK:DK + 1], 1.0).then_inc(st_ready[l], 2)
                dve.memset(St[NST - 1][:, :, :, 0:DK], 0.0).then_inc(st_init[l], 1)
                dve.wait_ge(st_init[l], 1)
                with dve.Fori(0, T // NST) as it:
                    st = Steps(dve, dve_steps)
                    added = [None, None]
                    for i in range(NST):
                        k, n = divmod(i, HS)
                        old, new = St[(i - 1) % NST], St[i]
                        mine = [slice(n * H2 + g, n * H2 + g + 1) for g in range(H2)]
                        halves = range(H2)
                        done = [None, None]
                        for g in halves:
                            if n == 0 and g == 0:
                                need(dve, st_fed[l], it, k, per=2)
                            if n == 0 and g == 1:
                                need(dve, st_ready[l], it, k + 1, per=2)
                            elif added[g] is not None:
                                st.reached(added[g])
                            done[g] = st.counted(dve.tensor_tensor(
                                prod[:, g], old[:, g], bc(kb_now[k][:, mine[g], :], [P, DK, DK + 1]), ALU.mult))
                        for g in halves:
                            st.reached(done[g])
                            done[g] = st.counted(dve.tensor_reduce(negu[:, g], prod[:, g], AX.X, ALU.add))
                        for g in halves:
                            st.reached(done[g])
                            done[g] = st.counted(dve.tensor_tensor(
                                outer[:, g], bc(k_now[k][:, mine[g], :], [P, DK, DK]),
                                bc(negu[:, g].unsqueeze(2), [P, DK, DK]), ALU.mult))
                        for g in halves:
                            if n == 0 and g == 0:
                                need(dve, st_free[l], it, k, per=2)
                            st.reached(done[g])
                            add = dve.tensor_tensor(new[:, g, :, 0:DK], old[:, g, :, 0:DK], outer[:, g], ALU.subtract)
                            if n == HS - 1 and g == H2 - 1:
                                add.then_inc(st_ready[l], 1)
                            else:
                                added[g] = st.counted(add)
                    st.reached(added[0])
                    st.end()

                st = Steps(dve, dve_steps)
                dve.wait_ge(st_ready[l], T // HS + 2)
                dve.wait_ge(o_ready[l], T // HS - 1)
                q_t = PS[:, T - HS:T, :].rearrange("p t (g s e) -> p (t g) s e", g=H2, s=4)[:, :, 0:1, :]
                st.after(dve.tensor_tensor(oprod, states[1], bc(q_t, [P, HS * H2, DK, DK]), ALU.mult))
                dve.tensor_reduce(Os[:, (T - HS) * 32:T * 32].rearrange("p (g v) -> p g v", v=DK), oprod,
                                  AX.X, ALU.add).then_inc(o_ready[l], 1)
                st.end()

                dve.wait_ge(o_home[l], 16 * NA * HH)
                with dve.Fori(0, IT) as it:
                    R_ = [lambda jj, u=u: tile_of(R, it, u, jj) for u in range(NU)]
                    yn_ = [lambda jj, u=u: yn[u][:, jj, :] for u in range(NU)]
                    st = Steps(dve, dve_steps)
                    done = [None] * NU
                    for u in range(NU):
                        o_g = group_of(O, it, u)
                        done[u] = st.counted(dve.scalar_tensor_tensor(
                            out=sq[u][:, 0:2, :].rearrange("p j c -> p (j c)"), in0=o_g, scalar=1.0 / DK, in1=o_g,
                            op0=ALU.mult, op1=ALU.mult))
                    for u in range(NU):
                        st.reached(done[u])
                        done[u] = st.counted(dve.tensor_reduce(
                            ssh[u][:, 0:GT * H], sq[u][:, 0:2, :].rearrange("p j c -> p (j c)").rearrange(
                                "p (h e) -> p h e", e=DK), AX.X, ALU.add))
                    head_rsqrt(st, GT * H, done)
                    for u in range(NU):
                        st.reached(done[u])
                        dve.tensor_tensor(yn[u][:, :, :].rearrange("p j (h e) -> p (j h) e", e=DK),
                                          group_of(O, it, u).rearrange("p (h e) -> p h e", e=DK),
                                          bc(rstdh[u][:, 0:GT * H].unsqueeze(2), [P, GT * H, DK]),
                                          ALU.mult).then_inc(o_n[l], 1)
                    for u in range(NU):
                        need(dve, o_wo[l], it, u)
                        dve.tensor_tensor(group_of(R, it, u), banks[4 * u + 1][:, :], group_of(R, it, u),
                                          ALU.add).then_inc(r1_ready[l], 1)
                    for u in range(NU):
                        need(dve, r1_ready[l], it, u)
                        need(dve, m_rr[l], it, u)
                        scaled(R_[u], yn_[u], u).then_inc(m_h[l], 1)
                    for c, (f0, fn) in enumerate(IC):
                        for u in range(NU):
                            need(dve, m_silu[l], it, c * NU + u, per=3 * NU)
                            by = (2, 0, 2)[c]
                            dve.tensor_tensor(hT[u][0:fn, c, :], banks[4 * u + by][0:fn, :], act_g[u][0:fn, :],
                                              ALU.mult).then_inc(m_a[l], 1)
                    for u in range(NU):
                        need(dve, m_out[l], it, u)
                        dve.tensor_tensor(group_of(R, it, u), banks[4 * u + 3][:, :], group_of(R, it, u),
                                          ALU.add).then_inc(r2_ready, 1)
                    if l == L - 1:
                        for u in range(NU):
                            dve.wait_ge(r2_ready, it * NU + (IT * NU * (L - 1) + u + 1))
                            need(dve, f_rr, it, u)
                            scaled(R_[u], yn_[u], u).then_inc(f_n, 1)
                        for u in range(NU):
                            need(dve, f_w, it, u)
                            st.after(dve.tensor_tensor(group_of(X, it, u), group_of(X, it, u),
                                                       y[u][:, :, :].rearrange("p j c -> p (j c)"), ALU.add))
                    st.end()

            with dve.Fori(0, IT) as it:
                X_ = [lambda jj, u=u: tile_of(X, it, u, jj) for u in range(NU)]
                yn_ = [lambda jj, u=u: yn[u][:, jj, :] for u in range(NU)]
                st = Steps(dve, dve_steps)
                for u in range(NU):
                    stats(st, X_[u], u, e_var)
                for u in range(NU):
                    need(dve, e_rstd, it, u)
                    normed(X_[u], yn_[u], u).then_inc(e_h, 1)
                need(dve, e_sig, it, NU - 1)
                tt = dve.tensor_tensor
                st.after(tt(sc[:, :, :], sg[:, :, :], bc(gbias[:, :].unsqueeze(1), [P, NT, E]), ALU.add))
                pair = sc[:, :, :].rearrange("p j (g c k) -> p (j g) c k", g=NGRP, c=2)
                tt(pmx[:, :, :], pair[:, :, :, 0], pair[:, :, :, 1], ALU.max)
                st.after(tt(pmn[:, :, :], pair[:, :, :, 0], pair[:, :, :, 1], ALU.min))
                tt(gs[:, 0, :], pmx[:, :, 0], pmx[:, :, 1], ALU.max)
                tt(gs[:, 1, :], pmx[:, :, 0], pmx[:, :, 1], ALU.min)
                st.after(tt(gs[:, 2, :], pmn[:, :, 0], pmn[:, :, 1], ALU.max))
                st.after(tt(gs[:, 3, :], gs[:, 1, :], gs[:, 2, :], ALU.max))
                st.after(tt(gs[:, 1, :], gs[:, 0, :], gs[:, 3, :], ALU.add))
                sums = gs[:, 1, :].rearrange("p (j g) -> p j g", j=NT)
                mine = bc(sums.unsqueeze(3), [P, NT, NGRP, NGRP])
                other = bc(sums.unsqueeze(2), [P, NT, NGRP, NGRP])
                tt(cmp1[:, :, :].rearrange("p (j g) o -> p j g o", j=NT), other, mine, ALU.is_gt)
                st.after(tt(cmp2[:, :, :].rearrange("p (j g) o -> p j g o", j=NT), other, mine, ALU.is_equal))
                c1 = cmp1[:, :, :].rearrange("p (j g) o -> p j (g o)", j=NT)
                c2 = cmp2[:, :, :].rearrange("p (j g) o -> p j (g o)", j=NT)
                st.after(tt(c2, c2, bc(before[:, :].unsqueeze(1), [P, NT, NGRP * NGRP]), ALU.mult))
                st.after(tt(c1, c1, c2, ALU.add))
                st.after(dve.tensor_reduce(gs[:, 2, :], cmp1[:, :, :],
                                           AX.X, ALU.add))
                st.after(dve.tensor_scalar(gmask[:, :], gs[:, 2, :], TOPG - 0.5, None, ALU.is_lt))
                four = msk[:, :, :].rearrange("p j (g k) -> p (j g) k", g=NGRP)
                st.after(tt(four, sc[:, :, :].rearrange("p j (g k) -> p (j g) k", g=NGRP),
                            bc(gmask[:, :].unsqueeze(2), [P, NT * NGRP, E // NGRP]), ALU.mult))
                for u in range(NU):
                    need(dve, x_silu, it, u, per=(NPAIR + 1) * NU)
                    dve.tensor_tensor(act_a[u][:, :], banks[4 * u + 1][:, :], act_g[u][:, :],
                                      ALU.mult).then_inc(x_a, 1)
                st.after(dve.tensor_scalar(msk[:, :, :], msk[:, :, :], 0.0, None, ALU.add))
                for jj in range(NT):
                    last = dve.max(top8[:, jj, :], msk[:, jj, :])
                st.after(last)
                for jj in range(NT):
                    last = dve.match_replace(rep[:, jj, :], top8[:, jj, :], msk[:, jj, :], REPLACED)
                st.after(last)
                st.after(tt(rep[:, :, :], rep[:, :, :], msk[:, :, :], ALU.not_equal))
                st.after(tt(rep[:, :, :], rep[:, :, :], sg[:, :, :], ALU.mult))
                st.after(dve.tensor_reduce(den[:, :], rep[:, :, :], AX.X, ALU.add))
                st.after(dve.tensor_scalar(den[:, :], den[:, :], 1e-20, None, ALU.add))
                st.after(dve.reciprocal(share[:, :], den[:, :]))
                st.after(dve.tensor_scalar(share[:, :], share[:, :], ROUTE_SCALE, None, ALU.mult))
                tt(comb[:, :, :], rep[:, :, :], bc(share[:, :].unsqueeze(2), [P, NT, E]),
                   ALU.mult).then_inc(e_comb, NU)
                for u in range(NU):
                    need(dve, e_cf, it, u)
                    st.after(dve.tensor_copy(c3[u][0:E, :], cf[u][:, :]))
                    st.after(dve.tensor_tensor(cf[u][:, :], cf[u][:, :], c3[u][0:E, :], ALU.subtract))
                    st.after(dve.tensor_copy(cmid[u][:, :], cf[u][:, :]))
                    dve.tensor_tensor(c3[u][2 * E:3 * E, :], cf[u][:, :], cmid[u][:, :], ALU.subtract).then_inc(e_c3, 1)
                for p in range(NPAIR):
                    for u in range(NU):
                        n = (p + 1) * NU + u
                        need(dve, x_silu, it, n, per=(NPAIR + 1) * NU)
                        need(dve, x_down, it, n - NU, per=(NPAIR + 1) * NU)
                        dve.tensor_tensor(act_gu[u][:, :], banks[4 * u + 1][:, :], act_g[u][:, :],
                                          ALU.mult).then_inc(x_gu, 1)
                        need(dve, x_gu, it, n - NU, per=NPAIR * NU)
                        dve.tensor_tensor(act_a[u][:, :], banks[4 * u + 2][:, :], act_gu[u][:, :],
                                          ALU.mult).then_inc(x_a, 1)
                for u in range(NU):
                    need(dve, e_otr, it, u)
                    dve.tensor_tensor(r[u][:, :, :].rearrange("p j c -> p (j c)"), banks[4 * u][:, :],
                                      group_of(X, it, u), ALU.add).then_inc(e_xo, 1)
                st.end()


def _layout(inputs):
    import numpy as np

    a = {k: np.asarray(v) for k, v in inputs.items()}

    def tr(w):
        return np.ascontiguousarray(w.T)

    def chunks(w, n):
        return w.reshape(n, P, -1).transpose(1, 0, 2)

    ctx = a["ctx_1024"].reshape(NA, NJ, KEYS, D)
    o = {}
    o["x"] = a["x"].reshape(NA, NJ, S, D).transpose(0, 2, 1, 3).reshape(P, NJ * D)
    o["ctx_t"] = ctx.transpose(1, 3, 0, 2).reshape(NJ, D, NA * KEYS)
    o["ctx_z"] = ctx[:, :, :KEYS - 1].reshape(NA, NJ, 2, P, D).transpose(1, 3, 2, 0, 4).reshape(NJ, P, 2 * NA * D)
    o["ctx_last"] = ctx[:, :, KEYS - 1].reshape(NA, NJ * D)
    o["rows"] = np.stack([a["L0_xattn_g1"], a["L0_xattn_beta1"], a["L0_xattn_g2"], a["L0_xattn_beta2"],
                          a["L0_xattn_g3"], a["L0_xattn_beta3"], a["L0_xattn_b2"], a["L0_attn_final_norm_w"]]).reshape(1, -1)
    o["cols"] = np.concatenate([a["L0_attn_norm1_w"].T, a["L0_attn_norm2_w"].T,
                                np.concatenate([a["L0_attn_onorm_w"].T] * H, axis=0),
                                a["L0_xattn_b1"].reshape(FFC, P).T,
                                np.stack([a["L0_xattn_g1"], a["L0_xattn_beta1"],
                                          a["L0_xattn_g2"], a["L0_xattn_beta2"]], axis=1)], axis=1)
    o["w1"] = a["L0_xattn_w1"]
    o["w2"] = chunks(a["L0_xattn_w2"], FFC)
    o["wqkvb"] = np.concatenate([a["L0_attn_Wq"], a["L0_attn_Wk"], a["L0_attn_Wv"], a["L0_attn_Wb"]],
                                axis=2).transpose(1, 0, 2)
    o["wo"] = a["L0_attn_Wo"].transpose(1, 0, 2)
    o["wgu"] = a["L0_attn_Wg"].transpose(1, 0, 2)
    wd = np.zeros((L, 3 * P, D), a["L0_attn_Wd"].dtype)
    wd[:, :INTER] = a["L0_attn_Wd"]
    o["wd"] = wd.reshape(L, 3, P, D).transpose(2, 0, 1, 3)
    o["gate_t"] = tr(a["L0_ffn_gate_w"])
    o["gate_bias"] = a["L0_ffn_gate_bias"].reshape(1, E)
    o["we_gate"] = tr(a["L0_ffn_w_gate"].reshape(E * EI, D)).reshape(D, NPAIR, P)
    o["we_up"] = tr(a["L0_ffn_w_up"].reshape(E * EI, D)).reshape(D, NPAIR, P)
    o["we_down"] = chunks(a["L0_ffn_w_down"].transpose(0, 2, 1).reshape(E * EI, D), NPAIR)
    o["sh_gate"] = tr(a["L0_ffn_sh_gate"])
    o["sh_up"] = tr(a["L0_ffn_sh_up"])
    o["sh_down"] = tr(a["L0_ffn_sh_down"])
    o["ident"] = np.eye(P, dtype=np.float32)
    q, k = np.arange(P)[:, None] % S, np.arange(S)[None, :]
    o["causal"] = np.where(k <= q, 0.0, NEG).astype(np.float32)
    spread = np.zeros((3, E, NPAIR, 2, EI), np.uint16)
    for e in range(E):
        spread[:, e, e // 2, e % 2, :] = 0x3F80
    o["spread"] = spread.reshape(3 * E, NPAIR * P)
    g = np.arange(NGRP)
    before = (g[None, :] < g[:, None]).astype(np.float32).reshape(1, NGRP * NGRP)
    o["before"] = np.repeat(before, P, axis=0)
    return {k_: np.ascontiguousarray(v) for k_, v in o.items()}


_ORDER = ["x", "ctx_t", "ctx_z", "ctx_last", "rows", "cols", "w1", "w2", "wqkvb", "wo", "wgu", "wd", "gate_t",
          "gate_bias", "we_gate", "we_up", "we_down", "sh_gate", "sh_up", "sh_down", "ident", "causal", "spread",
          "before"]


def kernel(**inputs):
    import numpy as _np
    import concourse.bacc as _bacc
    from concourse import mybir as _mybir
    from concourse.bass_utils import run_bass_kernel_spmd as _run

    nc = _bacc.Bacc("TRN2", target_bir_lowering=False, num_devices=1)
    laid = _layout(inputs)
    arrays, args = {}, []
    for name in _ORDER:
        arr = laid[name]
        arrays[f"in_{name}"] = arr
        args.append(nc.dram_tensor(f"in_{name}", arr.shape, _mybir.dt.from_np(arr.dtype), kind="ExternalInput").ap())
    args.append(nc.dram_tensor("out_0", (P, NJ * D), _mybir.dt.float32, kind="ExternalOutput").ap())
    perceiver(nc, *args)
    res = _run(nc, [arrays], core_ids=[0])
    got = _np.asarray(res.results[0]["out_0"])
    return _np.ascontiguousarray(got.reshape(NA, S, NJ, D).transpose(0, 2, 1, 3).reshape(NA * NJ, S, D))
```
